# Optimizing a Trainium2 kernel written in Bass

```python
import numpy as np
import jax
import jax.numpy as jnp

def _softmax(x, axis=-1):
    return jax.nn.softmax(x, axis=axis)

def _gelu(x):
    return jax.nn.gelu(x, approximate=True)

def _silu(x):
    return jax.nn.silu(x)

def _sigmoid(x):
    return jax.nn.sigmoid(x)

def _layernorm(x, axis=-1, eps=1e-05):
    m = jnp.mean(x, axis=axis, keepdims=True)
    v = jnp.var(x, axis=axis, keepdims=True)
    return (x - m) / jnp.sqrt(v + eps)

def _scatter_add(tgt, idx, src, axis=0):
    return tgt.at[idx].add(src)

def _segment_sum(src, seg, n):
    return jax.ops.segment_sum(src, seg, n)
kernel_name = 'mk_gnn_preln_d2_gnn_r8_25824b'

def setup_inputs(seed: int=0):
    np.random.seed(seed)
    _w = jnp.asarray

    def _rec_inputs():
        import jax
        import jax.numpy as jnp
        _gk = jax.random.key(seed)
        x = -0.0003713 + 1 * jax.random.normal(jax.random.fold_in(_gk, 1), (6250, 256), jnp.float32)
        _s = jax.random.randint(jax.random.fold_in(_gk, 2), (50000,), 0, 6250, jnp.int32)
        _d = jax.random.randint(jax.random.fold_in(_gk, 3), (50000,), 0, 6250, jnp.int32)
        _loop = jnp.arange(6250, dtype=jnp.int32)
        src = jnp.concatenate([_s, _d, _loop])
        dst = jnp.concatenate([_d, _s, _loop])
        _o = jnp.argsort(dst, stable=True)
        src = src[_o]
        dst = dst[_o]
        edge_weight = jax.random.uniform(jax.random.fold_in(_gk, 13), (106250,), jnp.float32, 0.0, 1)
        return (x, src, dst, edge_weight)
    x, src, dst, edge_weight = _rec_inputs()

    def _L0_gnn_setup():
        import jax, jax.numpy as jnp
        import numpy as np
        N_NODES = 6250
        N_EDGES = 200000
        D = 256

        def spmm(edge_row, edge_col, edge_val, dense):
            msgs = edge_val[:, None] * dense[edge_col]
            return jax.ops.segment_sum(msgs, edge_row, num_segments=N_NODES)
        key = jax.random.key(seed)
        k1, k2, k3, k4, k5, k6 = jax.random.split(key, 6)
        x = jax.random.normal(k1, (N_NODES, D), dtype=jnp.float32)
        weight = jax.random.normal(k2, (D, D), dtype=jnp.float32) * (1.0 / np.sqrt(D))
        hop_logits = jnp.array([1.2, 0.0], dtype=jnp.float32)
        edge_row = jax.random.randint(k4, (N_EDGES,), 0, N_NODES, dtype=jnp.int32)
        edge_col = jax.random.randint(k5, (N_EDGES,), 0, N_NODES, dtype=jnp.int32)
        edge_val = jax.random.uniform(k6, (N_EDGES,), dtype=jnp.float32)
        return {'x': x, 'weight': weight, 'hop_logits': hop_logits, 'edge_row': edge_row, 'edge_col': edge_col, 'edge_val': edge_val}
    _L0_gnn_all = _L0_gnn_setup()
    _L0_gnn_in = {k: v for k, v in _L0_gnn_all.items() if k in ('weight', 'hop_logits')}
    del _L0_gnn_all

    def _L1_gnn_setup():
        import jax, jax.numpy as jnp
        import numpy as np
        BN_EPS = 1e-05
        CHANNELS = [256, 512, 1024, 512, 256]

        def _bn(h, gamma, beta):
            m = h.mean(axis=0)
            v = h.var(axis=0)
            return gamma * (h - m) * jax.lax.rsqrt(v + BN_EPS) + beta
        key = jax.random.key(seed)
        N, E = (6250, 100000)
        ks = jax.random.split(key, 16)
        inp = {'x': jax.random.normal(ks[0], (N, CHANNELS[0]), dtype=jnp.float32), 'edge_index': jax.random.randint(ks[1], (2, E), 0, N, dtype=jnp.int32), 'eps': jnp.float32(0.1)}
        for i in range(4):
            cin, cout = (CHANNELS[i], CHANNELS[i + 1])
            inp[f'W{i + 1}'] = jax.random.normal(ks[2 + 3 * i], (cin, cout), dtype=jnp.float32) * (1.0 / np.sqrt(cin))
            inp[f'b{i + 1}'] = jnp.zeros((cout,), dtype=jnp.float32)
            if i < 3:
                inp[f'g{i + 1}'] = jnp.ones((cout,), dtype=jnp.float32)
                inp[f'beta{i + 1}'] = jnp.zeros((cout,), dtype=jnp.float32)
        return inp
    _L1_gnn_all = _L1_gnn_setup()
    _L1_gnn_in = {k: v for k, v in _L1_gnn_all.items() if k in ('eps', 'W1', 'b1', 'g1', 'beta1', 'W2', 'b2', 'g2', 'beta2', 'W3', 'b3', 'g3', 'beta3', 'W4', 'b4')}
    del _L1_gnn_all
    return {'x': x, 'src': src, 'dst': dst, 'edge_weight': edge_weight, 'L0_gnn_weight': _L0_gnn_in['weight'], 'L0_gnn_hop_logits': _L0_gnn_in['hop_logits'], 'L1_gnn_eps': _L1_gnn_in['eps'], 'L1_gnn_W1': _L1_gnn_in['W1'], 'L1_gnn_b1': _L1_gnn_in['b1'], 'L1_gnn_g1': _L1_gnn_in['g1'], 'L1_gnn_beta1': _L1_gnn_in['beta1'], 'L1_gnn_W2': _L1_gnn_in['W2'], 'L1_gnn_b2': _L1_gnn_in['b2'], 'L1_gnn_g2': _L1_gnn_in['g2'], 'L1_gnn_beta2': _L1_gnn_in['beta2'], 'L1_gnn_W3': _L1_gnn_in['W3'], 'L1_gnn_b3': _L1_gnn_in['b3'], 'L1_gnn_g3': _L1_gnn_in['g3'], 'L1_gnn_beta3': _L1_gnn_in['beta3'], 'L1_gnn_W4': _L1_gnn_in['W4'], 'L1_gnn_b4': _L1_gnn_in['b4']}

def reference(x, src, dst, edge_weight, L0_gnn_weight, L0_gnn_hop_logits, L1_gnn_eps, L1_gnn_W1, L1_gnn_b1, L1_gnn_g1, L1_gnn_beta1, L1_gnn_W2, L1_gnn_b2, L1_gnn_g2, L1_gnn_beta2, L1_gnn_W3, L1_gnn_b3, L1_gnn_g3, L1_gnn_beta3, L1_gnn_W4, L1_gnn_b4):
    import jax
    import jax.numpy as jnp

    def _L0_gnn_ref(x, weight, hop_logits, edge_row, edge_col, edge_val):
        import jax, jax.numpy as jnp
        import numpy as np
        N_NODES = 6250
        N_EDGES = 200000
        D = 256

        def spmm(edge_row, edge_col, edge_val, dense):
            msgs = edge_val[:, None] * dense[edge_col]
            return jax.ops.segment_sum(msgs, edge_row, num_segments=N_NODES)
        residual = x
        support = x @ weight
        hop_w = jax.nn.softmax(hop_logits)
        h1 = spmm(edge_row, edge_col, edge_val, support)
        h2 = spmm(edge_row, edge_col, edge_val, h1)
        out = hop_w[0] * h1 + hop_w[1] * h2 + residual
        return jax.nn.relu(out)

    def _L1_gnn_ref(x, edge_index, eps, W1, b1, g1, beta1, W2, b2, g2, beta2, W3, b3, g3, beta3, W4, b4):
        import jax, jax.numpy as jnp
        import numpy as np
        BN_EPS = 1e-05
        CHANNELS = [256, 512, 1024, 512, 256]

        def _bn(h, gamma, beta):
            m = h.mean(axis=0)
            v = h.var(axis=0)
            return gamma * (h - m) * jax.lax.rsqrt(v + BN_EPS) + beta
        src, dst = (edge_index[0], edge_index[1])
        agg = jax.ops.segment_sum(x[src], dst, num_segments=x.shape[0])
        h = (1.0 + eps) * x + agg
        h = jax.nn.elu(_bn(h @ W1 + b1, g1, beta1))
        h = jax.nn.elu(_bn(h @ W2 + b2, g2, beta2))
        h = jax.nn.elu(_bn(h @ W3 + b3, g3, beta3))
        return h @ W4 + b4
    edge_index = jnp.stack([src, dst])
    h = jnp.maximum(_layernorm(x, axis=-1), 0.0)
    x = x + _L0_gnn_ref(h, L0_gnn_weight, L0_gnn_hop_logits, src, dst, edge_weight)
    h = jnp.maximum(_layernorm(x, axis=-1), 0.0)
    x = x + _L1_gnn_ref(h, edge_index, L1_gnn_eps, L1_gnn_W1, L1_gnn_b1, L1_gnn_g1, L1_gnn_beta1, L1_gnn_W2, L1_gnn_b2, L1_gnn_g2, L1_gnn_beta2, L1_gnn_W3, L1_gnn_b3, L1_gnn_g3, L1_gnn_beta3, L1_gnn_W4, L1_gnn_b4)
    return x

_drawn_inputs = setup_inputs


def setup_inputs(seed=0):
    import zlib

    import numpy as np

    out = dict(_drawn_inputs(seed))
    spreads = {'L1_gnn_b1': (0.0, 0.8),
     'L1_gnn_g1': (1.0, 0.58),
     'L1_gnn_beta1': (0.0, 0.8),
     'L1_gnn_b2': (0.0, 0.8),
     'L1_gnn_g2': (1.0, 0.6),
     'L1_gnn_beta2': (0.0, 0.8),
     'L1_gnn_b3': (0.0, 0.8),
     'L1_gnn_g3': (1.0, 0.6),
     'L1_gnn_beta3': (0.0, 0.617),
     'L1_gnn_b4': (0.0, 0.523)}
    factors = {}
    for name, (base, spread) in spreads.items():
        noise = np.random.default_rng([zlib.crc32(name.encode()), seed]).standard_normal(out[name].shape)
        drawn = base * np.exp(spread * noise) if base else spread * noise
        out[name] = jnp.asarray(drawn.astype(out[name].dtype))
    for name, factor in factors.items():
        out[name] = (out[name] * factor).astype(out[name].dtype)
    return out
```

```python
from contextlib import ExitStack

import concourse.bass as bass
from concourse import mybir

F32 = mybir.dt.float32
I32 = mybir.dt.int32
ALU = mybir.AluOpType
ACT = mybir.ActivationFunctionType
AX_X = mybir.AxisListType.X

P = 128
N = 6250
D = 256
E = 106250
DH = D // P
LN_EPS = 1e-5
BN_EPS = 1e-5

GT = 8
GROUPS = -(-E // (GT * P))
TILES = GROUPS * GT
RING = 4
WIN = P

CT = 4
CN = CT * P
FULL = N // CN
CHUNKS = FULL + 1
TAIL = N - FULL * CN
NT = FULL * CT + 1
ROWS = NT * P
QT = 4
QUADS = TILES // QT
COPIES = QT
SPARE = ROWS + P
FAR = 65536.0

H1, H2, H3 = 512, 1024, 512
K1, K2, K3, K4 = D // P, H1 // P, H2 // P, H3 // P

assert TAIL <= P and FULL % 2 == 0 and GROUPS % RING == 0 and GT == 2 * QT and N + P <= SPARE


def over_chunks(eng, step):
    for q in range(2):
        step(0, q, CT, True)
    with eng.Fori(1, FULL // 2) as i:
        for q in range(2):
            step(i, q, CT, False)
    step(FULL // 2, 0, 1, False)


def over_groups(eng, step):
    for q in range(RING):
        step(0, q, True, False)
    with eng.Fori(1, GROUPS // RING - 1) as i:
        for q in range(RING):
            step(i, q, False, False)
    for q in range(RING):
        step(GROUPS // RING - 1, q, False, True)


def over_quads(eng, step):
    for q in range(4):
        step(0, q, True, False)
    with eng.Fori(1, QUADS // 4 - 1) as i:
        for q in range(4):
            step(i, q, False, False)
    for q in range(4):
        step(QUADS // 4 - 1, q, False, True)


def gnn(nc, x, src_t, dst_t, dst_g, w_t, wg, logits, eps, W1, b1, g1, be1, W2, b2, g2, be2,
        W3, b3, g3, be3, W4, b4, out):
    with ExitStack() as ctx:
        def sb(name, shape, dt=F32):
            return ctx.enter_context(nc.sbuf_tensor(name, shape, dt))

        def sem(name):
            return ctx.enter_context(nc.semaphore(name))

        def dram(name, shape):
            return nc.dram_tensor(name, shape, F32, kind="Internal").ap()

        table = [dram("table_hop1", (ROWS, D)), dram("table_hop2", (ROWS, D)), dram("table_gin", (ROWS, D))]
        copies = [[dram(f"hop{h + 1}_copy{k}", (SPARE, D)) for k in range(COPIES)] for h in range(2)]
        x1_dram = dram("x1_dram", (ROWS, D))
        z2_dram = dram("z2_dram", (CHUNKS * P, K3 * CN))

        big = sb("big", [P, K2 * N])
        sum_b = sb("sum_b", [P, DH * ROWS])
        edge_buf = sb("edge_buf", [P, 5 * TILES])
        work = sb("work", [P, 8 * CT * D])
        w1_sb = sb("w1_sb", [P, K1, H1])
        w4_sb = sb("w4_sb", [P, K4, D])
        iota = sb("iota", [P, WIN])
        ident = sb("ident", [P, P])
        ones = sb("ones", [P, P])

        acc_b = sum_b[:, :].rearrange("p (h n) -> p h n", h=DH)
        z = big[:, :].rearrange("p (m n) -> p m n", m=K2)

        src_all = edge_buf[:, 0:TILES]
        dst_all = edge_buf[:, TILES:2 * TILES]
        dst_loc = edge_buf[:, 2 * TILES:3 * TILES]
        w_all = edge_buf[:, 3 * TILES:4 * TILES]
        to_all = edge_buf[:, 4 * TILES:5 * TILES].bitcast(I32)

        rows = work[:, 0:2 * GT * D].rearrange("p (s t d) -> p s t d", s=2, t=GT)
        onehot = work[:, 2 * GT * D:2 * GT * (D + WIN)].rearrange("p (s t w) -> p s t w", s=2, t=GT)
        dst_i = work[:, 0:TILES].bitcast(I32)
        dst_gi = work[:, TILES:TILES + GT * P].bitcast(I32)
        src_i = work[:, TILES + GT * P:2 * TILES + GT * P].bitcast(I32)
        diag = work[:, 3 * TILES:3 * TILES + 2 * P].rearrange("p (a b) -> p a b", a=2)

        at = [0]

        def place(n, **dims):
            at[0] += 2 * n
            return big[:, at[0] - 2 * n:at[0]]
        window = place(D).rearrange("p (s d) -> p s d", s=2)
        same = place(QT * P).rearrange("p (s t e) -> p s t e", s=2, t=QT)
        hot = place(QT * P).rearrange("p (s t e) -> p s t e", s=2, t=QT)
        mix = place(QT * P).rearrange("p (s t e) -> p s t e", s=2, t=QT)
        msgs = place(QT * D).rearrange("p (s t d) -> p s t d", s=2, t=QT)
        parts = place(COPIES * CT * D).rearrange("p (s k t d) -> p s k t d", s=2, k=COPIES, t=CT)
        xr, hr, nr = [place(CT * D).rearrange("p (s t d) -> p s t d", s=2, t=CT) for _ in range(3)]
        stage = place(DH * CN).rearrange("p (s h n) -> p s h n", s=2, h=DH)
        wg_sb = place(DH * D // 2).rearrange("p (k m) -> p k m", k=DH)
        before = big[:, at[0]:at[0] + P]
        same_src = big[:, at[0] + P:at[0] + (1 + QT) * P].rearrange("p (t e) -> p t e", e=P)
        assert at[0] + (1 + QT) * P <= K2 * N
        w2_sb = work[:, 0:K2 * H2].rearrange("p (k m) -> p k m", k=K2)
        w3_sb = work[:, K2 * H2:K2 * H2 + K3 * H3].rearrange("p (k m) -> p k m", k=K3)

        base_bc = sb("base_bc", [P, GROUPS])
        reach = sb("reach", [P, 2])
        base_i = sb("base_i", [1, GROUPS], I32)
        reach_i = sb("reach_i", [1, 1], I32)
        ends = sb("ends", [P, 2])
        idx = sb("idx", [P, RING, GT], I32)
        to_ring = sb("to_ring", [P, 4, QT], I32)
        src_ring = sb("src_ring", [P, 4, QT])
        dup = sb("dup", [P, 4, QT])
        dup_to = sb("dup_to", [P, 4, QT])
        from_any = sb("from_any", [P, 1], I32)
        spare_row = sb("spare_row", [P, 1])
        lg = sb("lg", [P, 2])
        hw = sb("hw", [P, 8])
        eps_sb = sb("eps_sb", [P, 2])
        done = sb("done", [P, 1])
        lst = sb("lst", [P, 2, CT, 6])
        lmv = sb("lmv", [P, 2, CT, 2])
        lve = sb("lve", [P, 2, CT])
        lsd = sb("lsd", [P, 2, CT])
        lrs = sb("lrs", [P, 2, CT])
        lnm = sb("lnm", [P, 2, CT])

        M = [K2, K3, K4]
        bvec = [sb(f"bvec{n}", [P, M[n]]) for n in range(3)]
        gvec = [sb(f"gvec{n}", [P, M[n]]) for n in range(3)]
        tvec = [sb(f"tvec{n}", [P, M[n]]) for n in range(3)]
        bcor = [bvec[0], sb("bcor1", [P, K3]), sb("bcor2", [P, K4])]
        b4_bc = sb("b4_bc", [P, D])
        bn = edge_buf[:, 2700:2700 + 8 * K3].rearrange("p (a m) -> p a m", a=8)
        mv = edge_buf[:, 2700 + 8 * K3:2700 + 10 * K3].rearrange("p (m a) -> p m a", a=2)
        stats = edge_buf[:, 2048:2048 + K3 * CHUNKS * 6].rearrange("p (m c s) -> p m c s", m=K3, c=CHUNKS)
        ev = edge_buf[:, 0:2 * CN].rearrange("p (s n) -> p s n", s=2)
        yv = edge_buf[:, 2 * CN:4 * CN - 0].rearrange("p (s n) -> p s n", s=2)
        a1 = sum_b[:, 0:2 * K2 * CN].rearrange("p (s k n) -> p s k n", s=2, k=K2)
        z2_out = sum_b[:, 2 * K2 * CN:2 * K2 * CN + 2 * K3 * CN].rearrange("p (s k n) -> p s k n", s=2, k=K3)
        z2_in = sum_b[:, 0:K3 * CN].rearrange("p (k n) -> p k n", k=K3)
        a2 = sum_b[:, K3 * CN:3 * K3 * CN].rearrange("p (s k n) -> p s k n", s=2, k=K3)
        x1_in = sum_b[:, 2 * K4 * CN:2 * K4 * CN + 2 * CT * D].rearrange("p (s t d) -> p s t d", s=2, t=CT)
        o_out = sum_b[:, 2 * K4 * CN + 2 * CT * D:2 * K4 * CN + 4 * CT * D].rearrange("p (s t d) -> p s t d", s=2, t=CT)

        ps = ctx.enter_context(nc.psum_tensor("ps", [P, 8, 512], F32))
        ps_rows = [ps[:, 2 * s:2 * s + 2, :].rearrange("p b (t d) -> p (b t) d", d=D) for s in range(2)]
        ps_cols = [ps[:, 4 + 2 * s:6 + 2 * s, :] for s in range(2)]

        ps_src = [ps[:, s, :].rearrange("p (t e) -> p t e", e=P) for s in range(2)]
        ps_mix = [ps[:, 2 + s, :].rearrange("p (t e) -> p t e", e=P) for s in range(2)]
        ps_msg = [ps[:, 4 + 2 * s:6 + 2 * s, :].rearrange("p b (t d) -> p (b t) d", d=D) for s in range(2)]

        edges_in = sem("edges_in")
        vectors_in = sem("vectors_in")
        weights_in = sem("weights_in")
        consts_made = sem("consts_made")
        dst_cast = sem("dst_cast")
        dst_masked = sem("dst_masked")
        prep = sem("prep")
        prep_mm = sem("prep_mm")
        edges_ready = sem("edges_ready")
        act_small = sem("act_small")
        dve_small = sem("dve_small")
        zeroed = sem("zeroed")
        zeros_stored = sem("zeros_stored")
        zeros2_stored = sem("zeros2_stored")
        hop_done = sem("hop_done")
        window_in = [sem("window_in0"), sem("window_in1")]
        src_staged = sem("src_staged")
        src_turned = sem("src_turned")
        dup_found = sem("dup_found")
        to_step = sem("to_step")
        to_found = sem("to_found")
        same_done = sem("same_done")
        mix_mm = sem("mix_mm")
        mix_done = sem("mix_done")
        msg_mm = sem("msg_mm")
        msg_done = sem("msg_done")
        to_staged = sem("to_staged")
        scattered = [sem(f"scattered{k}") for k in range(COPIES)]
        scatter_opened = sem("scatter_opened")
        far_src = sem("far_src")
        far_turned = sem("far_turned")
        far_rows = sem("far_rows")
        far_step = sem("far_step")
        far_same = sem("far_same")
        far_mm = sem("far_mm")
        far_msg = sem("far_msg")
        far_done = sem("far_done")
        idx_ready = sem("idx_ready")
        gathered = [sem("gathered0"), sem("gathered1")]
        gather_opened = sem("gather_opened")
        ln_aggr_opened = sem("ln_aggr_opened")
        eq_done = sem("eq_done")
        onehot_ready = sem("onehot_ready")
        mm_done = sem("mm_done")
        evac_done = sem("evac_done")
        far_zeros = sem("far_zeros")
        far_zeroed = sem("far_zeroed")
        far_back = sem("far_back")
        far_cols = sem("far_cols")
        far_added = sem("far_added")
        ln_in = [[sem(f"ln{n}_in{q}") for q in range(2)] for n in range(2)]
        ln_pad = sem("ln_pad")
        ln_bn = [sem(f"ln{n}_bn") for n in range(2)]
        ln_ag = [sem(f"ln{n}_ag") for n in range(2)]
        ln_var = [sem(f"ln{n}_var") for n in range(2)]
        ln_std = [sem(f"ln{n}_std") for n in range(2)]
        ln_rstd = [sem(f"ln{n}_rstd") for n in range(2)]
        ln_coef = [sem(f"ln{n}_coef") for n in range(2)]
        ln_h = [sem(f"ln{n}_h") for n in range(2)]
        ln_stored = [[sem(f"ln{n}_stored{q}") for q in range(2)] for n in range(2)]
        h_turned = sem("h_turned")
        h_cols = sem("h_cols")
        sup_mm = sem("sup_mm")
        sup_rows = sem("sup_rows")
        sup_stored = [sem(f"sup_stored{q}") for q in range(2)]
        t2_in = [sem(f"t2_in{q}") for q in range(2)]
        t2_half = sem("t2_half")
        t2_other = sem("t2_other")
        t2_rows = sem("t2_rows")
        t2_scaled = sem("t2_scaled")
        t2_stored = [sem(f"t2_stored{q}") for q in range(2)]
        w_scaled = sem("w_scaled")
        c_half = sem("c_half")
        c_other = sem("c_other")
        c_sum = sem("c_sum")
        c_x1 = sem("c_x1")
        c_turned = sem("c_turned")
        c_cols = sem("c_cols")
        z_mm = [sem(f"z{n}_mm") for n in range(3)]
        z_evac = [sem(f"z{n}_evac") for n in range(3)]
        z_stat = [sem(f"z{n}_stat") for n in range(3)]
        bn_step = [sem(f"bn{n}_step") for n in range(3)]
        bn_std = [sem(f"bn{n}_std") for n in range(3)]
        bn_ready = [sem(f"bn{n}_ready") for n in range(3)]
        e_done = [sem(f"e{n}_done") for n in range(3)]
        a_done = [sem(f"a{n}_done") for n in range(3)]
        z2_stored = [sem(f"z2_stored{q}") for q in range(2)]
        z2_loaded = sem("z2_loaded")
        w23_in = sem("w23_in")
        colsum_mm = sem("colsum_mm")
        colsum_done = sem("colsum_done")
        x1_loaded = [sem(f"x1_loaded{q}") for q in range(2)]
        o_mm = sem("o_mm")
        o_b4 = sem("o_b4")
        o_ready = sem("o_ready")
        o_stored = [sem(f"o_stored{q}") for q in range(2)]

        block = ctx.enter_context(nc.Block())

        def rows_of(t, c, tiles):
            return t[bass.ds(c * CN, tiles * P), :].rearrange("(t p) d -> p t d", p=P)

        def is_near(eng):
            eng.wait_ge(edges_ready, 1)
            return eng.value_load(reach_i[0:1, 0:1], min_val=0, max_val=N) < WIN

        @block.sync
        def _(sp):
            sp.dma_start(dst_i, dst_t).then_inc(edges_in, 16)
            sp.dma_start(dst_gi[0:GROUPS, :], dst_g).then_inc(edges_in, 16)
            sp.dma_start(src_i, src_t).then_inc(edges_in, 16)
            sp.dma_start(w_all, w_t).then_inc(edges_in, 16)
            for to, of in ((lg[:, :], logits), (eps_sb[:, 0:1], eps), (b4_bc[:, :], b4),
                           (bvec[0][:, :], b1), (gvec[0][:, :], g1), (tvec[0][:, :], be1),
                           (bvec[1][:, :], b2), (gvec[1][:, :], g2), (tvec[1][:, :], be2),
                           (bvec[2][:, :], b3), (gvec[2][:, :], g3), (tvec[2][:, :], be3)):
                sp.dma_start(to, of).then_inc(vectors_in, 16)
            sp.dma_start(wg_sb, wg.rearrange("(k p) m -> p k m", p=P)).then_inc(weights_in, 16)
            sp.dma_start(w1_sb[:, :, :], W1.rearrange("(k p) m -> p k m", p=P)).then_inc(weights_in, 16)
            sp.dma_start(w4_sb[:, :, :], W4.rearrange("(k p) m -> p k m", p=P)).then_inc(weights_in, 16)

            def zero(h, k, whole, s):
                if whole:
                    sp.dma_start(copies[h][k][0:ROWS, :].rearrange("(p a) d -> p (a d)", p=P),
                                 sum_b[:, :]).then_inc(s, 16)
                sp.dma_start(copies[h][k][ROWS:SPARE, :], sum_b[:, 0:D]).then_inc(s, 16)

            sp.wait_ge(ln_pad, 1)

            def load_x(n, i, q, tiles):
                if tiles == CT:
                    sp.dma_start(xr[:, q], rows_of(x, 2 * i + q, tiles)).then_inc(ln_in[n][q], 16)
                else:
                    sp.dma_start(xr[0:TAIL, q, 0, :], x[FULL * CN:N, :]).then_inc(ln_in[n][q], 16)

            def ln0(i, q, tiles, first):
                if not first:
                    sp.wait_ge(ln_h[0], 2 * i + q - 1)
                load_x(0, i, q, tiles)
                if first:
                    if q == 0:
                        sp.wait_ge(zeroed, 1)
                    for k in range(q * COPIES // 2, (q + 1) * COPIES // 2):
                        zero(0, k, True, zeros_stored)
            over_chunks(sp, ln0)
            for k in range(COPIES):
                zero(1, k, k >= 2, zeros2_stored)
            near = is_near(sp)

            def hop(h, table_ready):
                off = h * QUADS
                for s, n in table_ready:
                    sp.wait_ge(s, n)

                def load(i, q, first, last):
                    if q % 2 == 0:
                        g = 2 * i + q // 2
                        par = q // 2
                        base = sp.value_load(base_i[0:1, bass.ds(g, 1)], min_val=0, max_val=ROWS - WIN)
                        if not first:
                            sp.wait_ge(msg_mm, off + 4 * i + q - 2)
                        sp.dma_start(window[:, par, :], table[h][bass.ds(base, WIN), :]).then_inc(window_in[par], 16)

                with sp.If(near):
                    over_quads(sp, load)
                with sp.Else():
                    sp.wait_ge(edges_ready, 1)
                sp.wait_ge(hop_done, h + 1)

            def load_parts(h, i, q, tiles, s):
                for k in range(COPIES):
                    sp.dma_start(parts[:, q, k, 0:tiles, :], rows_of(copies[h][k], 2 * i + q, tiles)).then_inc(s[q], 16)
            hop(0, [(sup_stored[0], 16 * (FULL // 2 + 1)), (sup_stored[1], 16 * (FULL // 2))])

            def t2(i, q, tiles, first):
                if not first:
                    sp.wait_ge(t2_rows, 2 * i + q - 1)
                load_parts(0, i, q, tiles, t2_in)
            over_chunks(sp, t2)
            hop(1, [(t2_stored[0], 32 * (FULL // 2 + 1)), (t2_stored[1], 32 * (FULL // 2))])

            def mid_in(i, q, tiles, first):
                if not first:
                    sp.wait_ge(ln_stored[1][q], 32 * i)
                load_x(1, i, q, tiles)
                load_parts(1, i, q, tiles, ln_in[1])
            over_chunks(sp, mid_in)

            sp.wait_ge(hop_done, 3)
            sp.dma_start(w2_sb, W2.rearrange("(k p) m -> p k m", p=P)).then_inc(w23_in, 16)
            sp.dma_start(w3_sb, W3.rearrange("(k p) m -> p k m", p=P)).then_inc(w23_in, 16)

            def z2_save(i, q, tiles, first):
                n = CN if tiles == CT else TAIL
                sp.wait_ge(z_evac[1], K3 * (2 * i + q + 1))
                to = z2_dram[bass.ds((2 * i + q) * P, P), :].rearrange("p (k n) -> p k n", k=K3)
                sp.dma_start(to[:, :, 0:n], z2_out[:, q, :, 0:n]).then_inc(z2_stored[q], 16)
            over_chunks(sp, z2_save)

            sp.wait_ge(z2_stored[0], 16 * (FULL // 2 + 1))
            sp.wait_ge(z2_stored[1], 16 * (FULL // 2))
            sp.wait_ge(z_mm[1], K3 * CHUNKS)

            def z2_load(i, q, tiles, first):
                n = CN if tiles == CT else TAIL
                if not (first and q == 0):
                    sp.wait_ge(e_done[1], K3 * (2 * i + q))
                of = z2_dram[bass.ds((2 * i + q) * P, P), :].rearrange("p (k n) -> p k n", k=K3)
                sp.dma_start(z2_in[:, :, 0:n], of[:, :, 0:n]).then_inc(z2_loaded, 16)
            over_chunks(sp, z2_load)

            sp.wait_ge(z_mm[2], K4 * CHUNKS)

            def last(i, q, tiles, first):
                if not first:
                    sp.wait_ge(o_ready, 2 * i + q - 1)
                sp.dma_start(x1_in[:, q, 0:tiles, :], rows_of(x1_dram, 2 * i + q, tiles)).then_inc(x1_loaded[q], 16)
            over_chunks(sp, last)
            sp.wait_ge(o_stored[0], 16 * (FULL // 2 + 1))
            sp.wait_ge(o_stored[1], 16 * (FULL // 2))

        @block.gpsimd
        def _(pool):
            pool.memset(ident[:, :], 0.0).then_inc(consts_made, 1)
            pool.wait_ge(consts_made, 1)
            pool.affine_select(out=ident[:, :], in_=ident[:, :], compare_op=ALU.not_equal, fill=1.0, base=0,
                               pattern=[[-1, P]], channel_multiplier=1).then_inc(consts_made, 1)
            pool.memset(ones[:, :], 1.0).then_inc(consts_made, 1)
            pool.iota(iota[:, :], pattern=[[1, WIN]], base=0, channel_multiplier=0,
                      allow_small_or_imprecise_dtypes=True).then_inc(consts_made, 1)
            pool.wait_ge(consts_made, 3)
            pool.affine_select(out=before, in_=ones[:, :], compare_op=ALU.is_gt, fill=0.0, base=0,
                               pattern=[[-1, P]], channel_multiplier=1).then_inc(consts_made, 1)
            pool.iota(spare_row[:, :], pattern=[[0, 1]], base=N, channel_multiplier=1,
                      allow_small_or_imprecise_dtypes=True).then_inc(consts_made, 1)
            pool.wait_ge(dst_cast, 1)
            t0 = TILES - GT
            pool.affine_select(out=dst_all[:, t0:TILES], in_=dst_all[:, t0:TILES], compare_op=ALU.is_ge, fill=FAR,
                               base=E - 1 - t0 * P, pattern=[[-P, GT]], channel_multiplier=-1).then_inc(dst_masked, 1)

            def support(i, q, tiles, first):
                c = 2 * i + q
                pool.wait_ge(sup_rows, c + 1)
                pool.sem_inc(scatter_opened, 1)
                pool.dma_start(rows_of(table[0], c, tiles), nr[:, q, 0:tiles, :]).then_inc(sup_stored[q], 16)
            over_chunks(pool, support)
            near = is_near(pool)

            def far_hop(h, sums):
                with pool.Fori(0, TILES) as t:
                    n = h * TILES + t
                    pool.wait_ge(far_src, n + 1)
                    pool.sem_inc(scatter_opened, 1)
                    pool.indirect_dma_start(rows[:, 0, 0, :], None, table[h],
                                            bass.IndirectOffsetOnAxis(from_any[:, 0:1], 0)).then_inc(far_rows, 16)
                    pool.wait_ge(far_msg, n + 1)
                    pool.sem_inc(scatter_opened, 1)
                    pool.indirect_dma_start(sums, bass.IndirectOffsetOnAxis(to_ring[:, 0, 0:1], 0),
                                            msgs[:, 0, 0, :], None, compute_op=ALU.add).then_inc(far_done, 16)

            def scatter_hop(h, sums_ready):
                off = h * QUADS
                for s, n in sums_ready:
                    pool.wait_ge(s, n)

                def scatter(i, q, first, last):
                    u = 4 * i + q
                    pool.wait_ge(msg_done, off + u + 1)
                    pool.wait_ge(to_staged, off + u + 1)
                    pool.sem_inc(scatter_opened, 1)
                    for t in range(QT):
                        if not (first and q == 0):
                            pool.wait_ge(scattered[t], 16 * (off + u))
                            pool.sem_inc(scatter_opened, 1)
                        pool.indirect_dma_start(copies[h][t], bass.IndirectOffsetOnAxis(to_ring[:, q, t:t + 1], 0),
                                                msgs[:, q % 2, t, :], None, compute_op=ALU.add).then_inc(scattered[t], 16)

                with pool.If(near):
                    over_quads(pool, scatter)
                with pool.Else():
                    far_hop(h, copies[h][0])
                pool.wait_ge(hop_done, h + 1)

            def add_parts(i, q, tiles, loaded, per, done_):
                pool.wait_ge(loaded[q], per * (i + 1))
                pool.tensor_tensor(parts[:, q, 2, 0:tiles, :], parts[:, q, 2, 0:tiles, :], parts[:, q, 3, 0:tiles, :],
                                   ALU.add).then_inc(done_, 1)

            scatter_hop(0, [(zeros_stored, 32 * COPIES), (sup_stored[0], 16 * (FULL // 2 + 1)),
                            (sup_stored[1], 16 * (FULL // 2))])
            over_chunks(pool, lambda i, q, tiles, first: add_parts(i, q, tiles, t2_in, 16 * COPIES, t2_other))
            scatter_hop(1, [(zeros2_stored, 16 * (COPIES + 2)), (t2_stored[0], 32 * (FULL // 2 + 1)),
                            (t2_stored[1], 32 * (FULL // 2)), (ln_stored[0][0], 16 * (FULL // 2 + 1)),
                            (ln_stored[0][1], 16 * (FULL // 2))])
            over_chunks(pool, lambda i, q, tiles, first: add_parts(i, q, tiles, ln_in[1], 16 * (COPIES + 1), c_other))

            def gather_hop(table_ready):
                off = 0
                for s, n in table_ready:
                    pool.wait_ge(s, n)

                def gather(i, q, first, last):
                    par = q % 2
                    pool.wait_ge(idx_ready, off + RING * i + q + 1)
                    if not (first and q < 2):
                        pool.wait_ge(mm_done, off + RING * i + q - 1)
                    pool.sem_inc(gather_opened, 1)
                    for t in range(GT):
                        pool.indirect_dma_start(rows[:, par, t, :], None, table[2],
                                                bass.IndirectOffsetOnAxis(idx[:, q, t:t + 1], 0)).then_inc(gathered[par], 16)

                with pool.If(near):
                    over_groups(pool, gather)
                with pool.Else():
                    pool.memset(msgs[:, 1, 0, :], 0.0).then_inc(far_zeros, 1)
                    pool.wait_ge(far_zeros, 1)
                    with pool.Fori(0, SPARE // P) as b:
                        pool.dma_start(copies[0][0][bass.ds(b * P, P), :], msgs[:, 1, 0, :]).then_inc(far_zeroed, 16)
                    pool.wait_ge(far_zeroed, 16 * (SPARE // P))
                    far_hop(2, copies[0][0])
                    pool.wait_ge(far_done, 16 * 3 * TILES)
                    with pool.Fori(0, NT) as b:
                        pool.dma_start(rows[:, 0, 1, :], copies[0][0][bass.ds(b * P, P), :]).then_inc(far_back, 16)
                        pool.wait_ge(far_added, b + 1)
                pool.wait_ge(hop_done, 3)
            gather_hop([(ln_stored[1][0], 32 * (FULL // 2 + 1)), (ln_stored[1][1], 32 * (FULL // 2))])

        @block.scalar
        def _(act):
            act.wait_ge(prep, 2)
            act.activation(hw[:, 0:2], lg[:, :], ACT.Exp, bias=hw[:, 3:4]).then_inc(act_small, 1)

            def ln_std_and_norm(n, i, q, tiles, to):
                c = 2 * i + q
                act.wait_ge(ln_var[n], c + 1)
                act.activation(lsd[:, q, 0:tiles], lve[:, q, 0:tiles], ACT.Sqrt).then_inc(ln_std[n], 1)
                act.wait_ge(ln_coef[n], c + 1)
                for t in range(tiles):
                    last = act.activation(to[:, q, t, :], xr[:, q, t, :], ACT.Relu,
                                          scale=lrs[:, q, t:t + 1], bias=lnm[:, q, t:t + 1])
                last.then_inc(ln_h[n], 1)

            def ln0(i, q, tiles, first):
                c = 2 * i + q
                if not first:
                    act.wait_ge(ln_stored[0][q], 16 * i)
                    act.wait_ge(h_turned, c - 1)
                ln_std_and_norm(0, i, q, tiles, hr)
                act.wait_ge(ln_h[0], c + 1)
                act.dma_start(rows_of(copies[1][1], c, tiles), hr[:, q, 0:tiles, :]).then_inc(ln_stored[0][q], 16)
                if not first:
                    act.wait_ge(sup_mm, c - 1)
                act.wait_ge(h_turned, c + 1)
                act.copy(stage[:, q, :, 0:tiles * P], ps_cols[q][:, :, 0:tiles * P]).then_inc(h_cols, 1)
            over_chunks(act, ln0)
            near = is_near(act)

            def first_hop(h):
                off = h * QUADS

                def stage_src(i, q, first):
                    u = 4 * i + q
                    if not first:
                        act.wait_ge(src_turned, off + u - 3)
                    act.wait_ge(edges_ready, 1)
                    act.copy(src_ring[:, q, :], src_all[:, bass.ds(u * QT, QT)]).then_inc(src_staged, 1)

                def take_mix(i, q, first):
                    u = 4 * i + q
                    par = q % 2
                    act.wait_ge(mix_mm, off + u + 1)
                    if not (first and q < 2):
                        act.wait_ge(msg_mm, off + u - 1)
                    act.copy(mix[:, par], ps_mix[par]).then_inc(mix_done, 1)

                def take_msgs(i, q, first):
                    u = 4 * i + q
                    par = q % 2
                    act.wait_ge(msg_mm, off + u + 1)
                    if not (first and q < 2):
                        for t in range(QT):
                            act.wait_ge(scattered[t], 16 * (off + u - 1))
                    act.copy(msgs[:, par], ps_msg[par]).then_inc(msg_done, 1)

                def stage_to(i, q, first):
                    u = 4 * i + q
                    if h == 0:
                        act.wait_ge(to_found, u + 1)
                    if not first:
                        for t in range(QT):
                            act.wait_ge(scattered[t], 16 * (off + u - 3))
                    act.wait_ge(edges_ready, 1)
                    act.copy(to_ring[:, q, :], to_all[:, bass.ds(u * QT, QT)]).then_inc(to_staged, 1)

                def step(i, q, first, last):
                    take_mix(i, q, first)
                    if not (first and q == 0):
                        take_msgs(i if q > 0 else i - 1, (q - 1) % 4, first)
                    if not (last and q > 0):
                        stage_src(i if q == 0 else i + 1, (q + 3) % 4, first and q == 0)
                    stage_to(i, q, first)

                with act.If(near):
                    for q in range(3):
                        stage_src(0, q, True)
                    over_quads(act, step)
                    take_msgs(QUADS // 4 - 1, 3, False)
                with act.Else():
                    act.wait_ge(edges_ready, 1)
                act.wait_ge(hop_done, h + 1)

            first_hop(0)

            def t2(i, q, tiles, first):
                c = 2 * i + q
                act.wait_ge(t2_rows, c + 1)
                act.dma_start(rows_of(table[1], c, tiles), hr[:, q, 0:tiles, :]).then_inc(t2_stored[q], 16)
                if not first:
                    act.wait_ge(t2_stored[q], 32 * i)
                act.activation(nr[:, q, 0:tiles, :], hr[:, q, 0:tiles, :], ACT.Copy, scale=hw[:, 6:7]).then_inc(t2_scaled, 1)
                act.wait_ge(t2_scaled, c + 1)
                act.dma_start(rows_of(copies[1][0], c, tiles), nr[:, q, 0:tiles, :]).then_inc(t2_stored[q], 16)
            over_chunks(act, t2)
            first_hop(1)

            act.wait_ge(zeros_stored, 32 * COPIES)
            act.wait_ge(zeros2_stored, 16 * (COPIES + 2))

            def mid(i, q, tiles, first):
                c = 2 * i + q
                if not first:
                    act.wait_ge(ln_stored[1][q], 32 * i)
                    act.wait_ge(c_turned, c - 1)
                ln_std_and_norm(1, i, q, tiles, nr)
                act.wait_ge(ln_h[1], c + 1)
                act.dma_start(rows_of(table[2], c, tiles), nr[:, q, 0:tiles, :]).then_inc(ln_stored[1][q], 16)
                act.dma_start(rows_of(x1_dram, c, tiles), xr[:, q, 0:tiles, :]).then_inc(ln_stored[1][q], 16)
                act.wait_ge(c_turned, c + 1)
                act.activation(acc_b[:, :, bass.ds(c * CN, tiles * P)], ps_cols[q][:, :, 0:tiles * P], ACT.Copy,
                               scale=eps_sb[:, 1:2]).then_inc(c_cols, 1)
            over_chunks(act, mid)

            def fill(i, q, first, last):
                g = RING * i + q
                if not first:
                    act.wait_ge(mm_done, g - RING + 1)
                act.wait_ge(edges_ready, 1)
                act.copy(idx[:, q, :], src_all[:, bass.ds(g * GT, GT)]).then_inc(idx_ready, 1)

            with act.If(near):
                over_groups(act, fill)
            with act.Else():
                act.wait_ge(edges_ready, 1)
            act.wait_ge(hop_done, 3)

            def z1(i, q, tiles, first):
                n = CN if tiles == CT else TAIL
                c = 2 * i + q
                for m in range(K2):
                    act.wait_ge(z_mm[0], K2 * c + m + 1)
                    act.wait_ge(vectors_in, 16 * 12)
                    act.activation(z[:, m, bass.ds(c * CN, n)], ps[:, K2 * q + m, 0:n], ACT.Identity,
                                   bias=bvec[0][:, m:m + 1]).then_inc(z_evac[0], 1)
            over_chunks(act, z1)

            def bn_sqrt(n):
                act.wait_ge(bn_step[n], 2)
                act.activation(bn[:, 2, 0:M[n]], bn[:, 1, 0:M[n]], ACT.Sqrt).then_inc(bn_std[n], 1)
                act.wait_ge(bn_ready[n], 1)

            def elu_terms(n, zk, k, c, width, K):
                j = K * c + k
                if not (isinstance(j, int) and j < 2):
                    act.wait_ge(a_done[n], j - 1)
                act.wait_ge(bn_ready[n], 1)
                act.activation(ev[:, k % 2, 0:width], zk, ACT.Exp,
                               scale=bn[:, 4, k:k + 1], bias=bn[:, 5, k:k + 1])
                act.activation(yv[:, k % 2, 0:width], zk, ACT.Identity,
                               scale=bn[:, 4, k:k + 1], bias=bn[:, 6, k:k + 1]).then_inc(e_done[n], 1)

            bn_sqrt(0)
            act.wait_ge(colsum_done, 2)

            def save_z2(i, q, tiles, first):
                n = CN if tiles == CT else TAIL
                c = 2 * i + q
                if not first:
                    act.wait_ge(z2_stored[q], 16 * i)
                    act.wait_ge(z_stat[1], K3 * (c - 1))
                for m in range(K3):
                    act.wait_ge(z_mm[1], K3 * c + m + 1)
                    act.activation(z2_out[:, q, m, 0:n], ps[:, m, 0:n], ACT.Identity,
                                   bias=bcor[1][:, m:m + 1]).then_inc(z_evac[1], 1)

            def elu1(i, q, tiles, first):
                n = CN if tiles == CT else TAIL
                c = 2 * i + q
                for k in range(K2):
                    elu_terms(0, z[:, k, bass.ds(c * CN, n)], k, c, n, K2)

            elu1(0, 0, CT, True)

            def z2(i, q, tiles, first):
                if tiles == CT:
                    if q == 0:
                        elu1(i, 1, CT, False)
                    else:
                        elu1(i + 1, 0, CT, False)
                save_z2(i, q, tiles, first)
            z2(0, 0, CT, True)
            z2(0, 1, CT, True)
            with act.Fori(1, FULL // 2 - 1) as i:
                for q in range(2):
                    z2(i, q, CT, False)
            z2(FULL // 2 - 1, 0, CT, False)
            elu1(FULL // 2, 0, 1, False)
            save_z2(FULL // 2 - 1, 1, CT, False)
            save_z2(FULL // 2, 0, 1, False)
            bn_sqrt(1)
            act.wait_ge(colsum_done, 3)

            def elu2(i, q, tiles):
                n = CN if tiles == CT else TAIL
                c = 2 * i + q
                act.wait_ge(z2_loaded, 16 * (c + 1))
                for k in range(K3):
                    elu_terms(1, z2_in[:, k, 0:n], k, c, n, K3)

            def save_z3(i, q, tiles):
                n = CN if tiles == CT else TAIL
                c = 2 * i + q
                for m in range(K4):
                    act.wait_ge(z_mm[2], K4 * c + m + 1)
                    act.wait_ge(colsum_done, 3)
                    act.activation(z[:, m, bass.ds(c * CN, n)], ps[:, K4 * q + m, 0:n], ACT.Identity,
                                   bias=bcor[2][:, m:m + 1]).then_inc(z_evac[2], 1)
            elu2(0, 0, CT)
            elu2(0, 1, CT)
            save_z3(0, 0, CT)
            with act.Fori(1, FULL // 2) as i:
                elu2(i, 0, CT)
                save_z3(i - 1, 1, CT)
                elu2(i, 1, CT)
                save_z3(i, 0, CT)
            elu2(FULL // 2, 0, 1)
            save_z3(FULL // 2 - 1, 1, CT)
            save_z3(FULL // 2, 0, 1)
            bn_sqrt(2)

            def elu3(i, q, tiles, first):
                n = CN if tiles == CT else TAIL
                c = 2 * i + q
                for k in range(K4):
                    elu_terms(2, z[:, k, bass.ds(c * CN, n)], k, c, n, K4)
            def store(i, q, tiles):
                c = 2 * i + q
                act.wait_ge(o_ready, c + 1)
                if tiles == CT:
                    act.dma_start(rows_of(out, c, tiles), o_out[:, q, :, :]).then_inc(o_stored[q], 16)
                else:
                    act.dma_start(out[FULL * CN:N, :], o_out[0:TAIL, q, 0, :]).then_inc(o_stored[q], 16)
            elu3(0, 0, CT, True)
            elu3(0, 1, CT, True)
            store(0, 0, CT)
            with act.Fori(1, FULL // 2) as i:
                elu3(i, 0, CT, False)
                store(i - 1, 1, CT)
                elu3(i, 1, CT, False)
                store(i, 0, CT)
            elu3(FULL // 2, 0, 1, False)
            store(FULL // 2 - 1, 1, CT)
            store(FULL // 2, 0, 1)

        @block.vector
        def _(dve):
            small = [0]

            def chain(ins):
                small[0] += 1
                ins.then_inc(dve_small, 1)
                dve.wait_ge(dve_small, small[0])

            dve.memset(xr[96:P, 0, 0, :], 0.0).then_inc(ln_pad, 1)
            dve.memset(sum_b[:, :], 0.0).then_inc(zeroed, 1)
            dve.wait_ge(edges_in, 64)
            dve.tensor_copy(dst_all, dst_i).then_inc(dst_cast, 1)
            chain(dve.tensor_copy(src_all, src_i))
            dve.wait_ge(vectors_in, 16 * 12)
            dve.tensor_tensor(hw[:, 2:3], lg[:, 0:1], lg[:, 1:2], ALU.max).then_inc(prep, 1)
            dve.wait_ge(prep, 1)
            dve.tensor_scalar(hw[:, 3:4], hw[:, 2:3], -1.0, None, ALU.mult).then_inc(prep, 1)
            chain(dve.tensor_scalar(eps_sb[:, 1:2], eps_sb[:, 0:1], 1.0, None, ALU.add))
            chain(dve.tensor_reduce(ends[0:GROUPS, 0:1], dst_gi[0:GROUPS, :], AX_X, ALU.min))
            chain(dve.tensor_reduce(ends[0:GROUPS, 1:2], dst_gi[0:GROUPS, :], AX_X, ALU.max))
            dve.wait_ge(consts_made, 6)
            for a in range(2):
                chain(dve.tensor_scalar(diag[0:GROUPS, a, 0:GROUPS], ident[0:GROUPS, 0:GROUPS], ends[0:GROUPS, a:a + 1],
                                        None, ALU.mult))
            dve.wait_ge(prep_mm, 1)
            chain(dve.tensor_scalar(base_bc[:, :], ps[:, 0, 0:GROUPS], float(ROWS - WIN), None, ALU.min))
            chain(dve.tensor_copy(base_i[:, :], base_bc[0:1, :]))
            chain(dve.tensor_tensor(diag[:, 0, 0:GROUPS], ps[:, 1, 0:GROUPS], base_bc[:, :], ALU.subtract))
            chain(dve.tensor_reduce(reach[:, 0:1], diag[:, 0, 0:GROUPS], AX_X, ALU.max))
            chain(dve.tensor_copy(reach_i[:, :], reach[0:1, 0:1]))
            dve.wait_ge(dst_masked, 1)
            by_group = [a.rearrange("p (g t) -> p g t", t=GT) for a in (dst_loc, dst_all)]
            chain(dve.tensor_tensor(by_group[0], by_group[1], base_bc[:, :].unsqueeze(2).to_broadcast([P, GROUPS, GT]),
                                    ALU.subtract))
            dve.wait_ge(act_small, 1)
            chain(dve.tensor_tensor(hw[:, 4:5], hw[:, 0:1], hw[:, 1:2], ALU.add))
            chain(dve.reciprocal(hw[:, 5:6], hw[:, 4:5]))
            chain(dve.tensor_scalar(hw[:, 6:8], hw[:, 0:2], hw[:, 5:6], None, ALU.mult))
            dve.memset(done[:, :], 0.0).then_inc(edges_ready, 1)
            near = is_near(dve)

            def ln_coefficients(n, i, q, tiles):
                c = 2 * i + q
                for t in range(tiles):
                    last = dve.bn_stats(lst[:, q, t, :], xr[:, q, t, :])
                last.then_inc(ln_bn[n], 1)
                dve.wait_ge(ln_bn[n], c + 1)
                dve.sem_inc(ln_aggr_opened, 1)
                for t in range(tiles):
                    last = dve.bn_aggr(lmv[:, q, t, :], lst[:, q, t, :])
                last.then_inc(ln_ag[n], 1)
                dve.wait_ge(ln_ag[n], c + 1)
                dve.tensor_scalar(lve[:, q, 0:tiles], lmv[:, q, 0:tiles, 1], LN_EPS, None, ALU.add).then_inc(ln_var[n], 1)
                dve.wait_ge(ln_std[n], c + 1)
                dve.reciprocal(lrs[:, q, 0:tiles], lsd[:, q, 0:tiles]).then_inc(ln_rstd[n], 1)
                dve.wait_ge(ln_rstd[n], c + 1)
                dve.scalar_tensor_tensor(out=lnm[:, q, 0:tiles], in0=lmv[:, q, 0:tiles, 0], scalar=-1.0,
                                         in1=lrs[:, q, 0:tiles], op0=ALU.mult, op1=ALU.mult).then_inc(ln_coef[n], 1)

            def ln0(i, q, tiles, first):
                c = 2 * i + q
                if not first:
                    dve.wait_ge(ln_h[0], c - 1)
                dve.wait_ge(ln_in[0][q], 16 * (i + 1))
                ln_coefficients(0, i, q, tiles)

            def support(i, q, tiles):
                c = 2 * i + q
                if not (isinstance(i, int) and i == 0):
                    dve.wait_ge(sup_stored[q], 16 * i)
                dve.wait_ge(sup_mm, c + 1)
                dve.tensor_copy(nr[:, q, 0:tiles, :], ps_rows[q][:, 0:tiles, :]).then_inc(sup_rows, 1)

            def ln0_step(i, q, tiles, first):
                ln0(i, q, tiles, first)
                if not (first and q == 0):
                    support(i if q else i - 1, 1 - q, CT)
            over_chunks(dve, ln0_step)
            support(FULL // 2, 0, 1)

            def far_hop(h):
                with dve.Fori(0, TILES) as t:
                    n = h * TILES + t
                    col = bass.ds(t, 1)
                    if h > 0:
                        dve.wait_ge(far_done, 16 * n)
                    if h < 2:
                        added, read, weight = src_all, dst_all, w_all[:, col]
                        dve.tensor_copy(src_ring[:, 0, 0:1], added[:, col]).then_inc(far_step, 1)
                    else:
                        added, read, weight = dst_all, src_all, ones[:, 0:1]
                        dve.tensor_scalar(src_ring[:, 0, 0:1], added[:, col], float(N), None, ALU.min).then_inc(far_step, 1)
                    dve.tensor_scalar(from_any[:, :], read[:, col], float(N - 1), None, ALU.min).then_inc(far_src, 1)
                    dve.wait_ge(far_turned, n + 1)
                    dve.wait_ge(far_step, 4 * n + 1)
                    dve.tensor_scalar(same[:, 0, 0, :], ps_src[0][:, 0, :], src_ring[:, 0, 0:1], weight,
                                      ALU.is_equal, ALU.mult).then_inc(far_same, 1)
                    dve.scalar_tensor_tensor(out=same_src[:, 0, :], in0=ps_src[0][:, 0, :], scalar=src_ring[:, 0, 0:1],
                                             in1=before, op0=ALU.is_equal, op1=ALU.mult,
                                             accum_out=dup[:, 0, 0:1]).then_inc(far_step, 1)
                    dve.wait_ge(far_step, 4 * n + 2)
                    to = dup_to[:, 0, 0:1]
                    dve.tensor_scalar(to, src_ring[:, 0, 0:1], -1.0, spare_row[:, 0:1], ALU.mult, ALU.add).then_inc(far_step, 1)
                    dve.wait_ge(far_step, 4 * n + 3)
                    dve.scalar_tensor_tensor(out=to, in0=dup[:, 0, 0:1], scalar=1.0, in1=to,
                                             op0=ALU.min, op1=ALU.mult).then_inc(far_step, 1)
                    dve.wait_ge(far_step, 4 * n + 4)
                    dve.tensor_tensor(to_ring[:, 0, 0:1], src_ring[:, 0, 0:1], to, ALU.add)
                    dve.wait_ge(far_mm, n + 1)
                    dve.tensor_copy(msgs[:, 0, 0, :], ps_msg[0][:, 0, :]).then_inc(far_msg, 1)
                    dve.wait_ge(far_done, 16 * n + 16)

            def first_hop(h):
                off = h * QUADS

                def step(i, q, first, last):
                    u = 4 * i + q
                    par = q % 2
                    cols = bass.ds(u * QT, QT)
                    dve.wait_ge(src_turned, off + u + 1)
                    if not (first and q < 2):
                        dve.wait_ge(mix_mm, off + u - 1)
                    for t in range(QT):
                        dve.tensor_scalar(same[:, par, t, :], ps_src[par][:, t, :], src_all[:, bass.ds(u * QT + t, 1)],
                                          w_all[:, bass.ds(u * QT + t, 1)], ALU.is_equal, ALU.mult)
                    loc = dst_loc[:, cols].unsqueeze(2).to_broadcast([P, QT, WIN])
                    nodes = iota[:, :].unsqueeze(1).to_broadcast([P, QT, WIN])
                    dve.tensor_tensor(hot[:, par], nodes, loc, ALU.is_equal).then_inc(same_done, 1)
                    if h == 0:
                        for t in range(QT):
                            last_ = dve.scalar_tensor_tensor(out=same_src[:, t, :], in0=ps_src[par][:, t, :],
                                                             scalar=src_all[:, bass.ds(u * QT + t, 1)], in1=before,
                                                             op0=ALU.is_equal, op1=ALU.mult, accum_out=dup[:, q, t:t + 1])
                        last_.then_inc(dup_found, 1)
                        to = dup_to[:, q, :]
                        dve.tensor_scalar(to, src_all[:, cols], -1.0, spare_row[:, 0:1], ALU.mult, ALU.add).then_inc(to_step, 1)
                        dve.wait_ge(dup_found, u + 1)
                        dve.wait_ge(to_step, 2 * u + 1)
                        dve.scalar_tensor_tensor(out=to, in0=dup[:, q, :], scalar=1.0, in1=to,
                                                 op0=ALU.min, op1=ALU.mult).then_inc(to_step, 1)
                        dve.wait_ge(to_step, 2 * u + 2)
                        dve.tensor_tensor(to_all[:, cols], src_all[:, cols], to, ALU.add).then_inc(to_found, 1)

                with dve.If(near):
                    over_quads(dve, step)
                    for t in range(COPIES):
                        dve.wait_ge(scattered[t], 16 * (off + QUADS))
                with dve.Else():
                    far_hop(h)
                dve.memset(done[:, :], 0.0).then_inc(hop_done, 1)

            def sum_parts(i, q, tiles, loaded, per, half, other, to, done_):
                c = 2 * i + q
                dve.wait_ge(loaded[q], per * (i + 1))
                dve.tensor_tensor(parts[:, q, 0, 0:tiles, :], parts[:, q, 0, 0:tiles, :], parts[:, q, 1, 0:tiles, :],
                                  ALU.add).then_inc(half, 1)
                dve.wait_ge(half, c + 1)
                dve.wait_ge(other, c + 1)
                dve.tensor_tensor(to, parts[:, q, 0, 0:tiles, :], parts[:, q, 2, 0:tiles, :], ALU.add).then_inc(done_, 1)

            first_hop(0)

            def t2(i, q, tiles, first):
                if not first:
                    dve.wait_ge(t2_stored[q], 32 * i)
                    dve.wait_ge(t2_scaled, 2 * i + q - 1)
                sum_parts(i, q, tiles, t2_in, 16 * COPIES, t2_half, t2_other, hr[:, q, 0:tiles, :], t2_rows)
            for q in range(2):
                dve.wait_ge(ln_stored[0][q], 16 * (FULL // 2 + 1 - q))
            over_chunks(dve, t2)
            dve.tensor_scalar(w_all, w_all, hw[:, 7:8], None, ALU.mult).then_inc(w_scaled, 1)
            dve.wait_ge(w_scaled, 1)
            first_hop(1)

            def mid(i, q, tiles, first):
                c = 2 * i + q
                to = parts[:, q, 0, 0:tiles, :]
                sum_parts(i, q, tiles, ln_in[1], 16 * (COPIES + 1), c_half, c_other, to, c_sum)
                dve.wait_ge(c_sum, c + 1)
                x1 = xr[:, q, 0:tiles, :].rearrange("p t d -> p (t d)")
                dve.scalar_tensor_tensor(out=x1, in0=to.rearrange("p t d -> p (t d)"), scalar=0.0, in1=x1,
                                         op0=ALU.max, op1=ALU.add).then_inc(c_x1, 1)
                dve.wait_ge(c_x1, c + 1)
                if not first:
                    dve.wait_ge(ln_h[1], c - 1)
                ln_coefficients(1, i, q, tiles)
            over_chunks(dve, mid)
            dve.wait_ge(c_cols, CHUNKS)

            def build(i, q, first):
                g = RING * i + q
                if not (first and q < 2):
                    dve.wait_ge(mm_done, g - 1)
                loc = dst_loc[:, bass.ds(g * GT, GT)].unsqueeze(2).to_broadcast([P, GT, WIN])
                nodes = iota[:, :].unsqueeze(1).to_broadcast([P, GT, WIN])
                dve.tensor_tensor(onehot[:, q % 2], nodes, loc, ALU.is_equal).then_inc(onehot_ready, 1)

            def add(i, q, first):
                g = RING * i + q
                par = q % 2
                base = dve.value_load(base_i[0:1, bass.ds(g, 1)], min_val=0, max_val=ROWS - WIN)
                dve.wait_ge(mm_done, g + 1)
                if not (first and q == 0):
                    dve.wait_ge(evac_done, g)
                to = acc_b[:, :, bass.ds(base, WIN)]
                dve.tensor_tensor(to, to, ps[:, 2 * par:2 * par + 2, 0:WIN], ALU.add).then_inc(evac_done, 1)

            def gin(i, q, first, last):
                if not (last and q == RING - 1):
                    build(i if q < RING - 1 else i + 1, (q + 1) % RING, first and q < RING - 1)
                add(i, q, first)

            with dve.If(near):
                build(0, 0, True)
                over_groups(dve, gin)
                dve.wait_ge(evac_done, GROUPS)
            with dve.Else():
                far_hop(2)
                with dve.Fori(0, NT) as b:
                    dve.wait_ge(far_cols, b + 1)
                    to = acc_b[:, :, bass.ds(b * P, P)]
                    dve.tensor_tensor(to, to, ps[:, 0:2, 0:P], ALU.add).then_inc(far_added, 1)
                dve.wait_ge(far_added, NT)
            dve.memset(done[:, :], 0.0).then_inc(hop_done, 1)

            def column_stats(n, i, q, tiles, slices, of):
                width = CN if tiles == CT else TAIL
                c = 2 * i + q
                for m in range(slices):
                    dve.wait_ge(z_evac[n], slices * c + m + 1)
                    dve.bn_stats(stats[:, m, bass.ds(c, 1), :].rearrange("p c s -> p (c s)"), of(m, c, width)).then_inc(z_stat[n], 1)

            def bn_vectors(n):
                m = M[n]
                dve.wait_ge(z_stat[n], m * CHUNKS)
                for k in range(m):
                    last = dve.bn_aggr(mv[:, k, :], stats[:, k, :, :].rearrange("p c s -> p (c s)"))
                last.then_inc(bn_step[n], 1)
                dve.wait_ge(bn_step[n], 1)
                dve.tensor_scalar(bn[:, 1, 0:m], mv[:, 0:m, 1], BN_EPS, None, ALU.add).then_inc(bn_step[n], 1)
                dve.wait_ge(bn_std[n], 1)
                chain(dve.reciprocal(bn[:, 3, 0:m], bn[:, 2, 0:m]))
                chain(dve.tensor_tensor(bn[:, 4, 0:m], bn[:, 3, 0:m], gvec[n][:, :], ALU.mult))
                chain(dve.tensor_tensor(bn[:, 7, 0:m], mv[:, 0:m, 0], bn[:, 4, 0:m], ALU.mult))
                chain(dve.tensor_tensor(bn[:, 5, 0:m], tvec[n][:, :], bn[:, 7, 0:m], ALU.subtract))
                chain(dve.tensor_scalar(bn[:, 6, 0:m], bn[:, 5, 0:m], 1.0, None, ALU.add))
                dve.memset(done[:, :], 0.0).then_inc(bn_ready[n], 1)

            def z1(i, q, tiles, first):
                column_stats(0, i, q, tiles, K2, lambda m, c, w: z[:, m, bass.ds(c * CN, w)])
            over_chunks(dve, z1)
            dve.wait_ge(colsum_mm, 1)
            chain(dve.tensor_tensor(bcor[1][:, :], bvec[1][:, :], ps[:, 0, 0:K3], ALU.subtract))
            chain(dve.tensor_tensor(bcor[2][:, :], bvec[2][:, :], ps[:, 1, 0:K4], ALU.subtract))
            chain(dve.tensor_tensor(b4_bc[:, :], b4_bc[:, :], ps[:, 2, 0:D], ALU.subtract))
            dve.memset(done[:, :], 0.0).then_inc(colsum_done, 3)
            bn_vectors(0)

            def elu(n, k, c, width, to, K):
                dve.wait_ge(e_done[n], K * c + k + 1)
                dve.scalar_tensor_tensor(out=to, in0=ev[:, k % 2, 0:width], scalar=1.0, in1=yv[:, k % 2, 0:width],
                                         op0=ALU.min, op1=ALU.max).then_inc(a_done[n], 1)

            def elu1(i, q, tiles, first):
                w = CN if tiles == CT else TAIL
                if not first:
                    dve.wait_ge(z_mm[1], K3 * (2 * i + q - 1))
                for k in range(K2):
                    elu(0, k, 2 * i + q, w, a1[:, q, k, 0:w], K2)

            def stats2(i, q, tiles):
                column_stats(1, i, q, tiles, K3, lambda m, c, w: z2_out[:, q, m, 0:w])
            elu1(0, 0, CT, True)
            elu1(0, 1, CT, True)
            stats2(0, 0, CT)
            with dve.Fori(1, FULL // 2) as i:
                elu1(i, 0, CT, False)
                stats2(i - 1, 1, CT)
                elu1(i, 1, CT, False)
                stats2(i, 0, CT)
            elu1(FULL // 2, 0, 1, False)
            stats2(FULL // 2 - 1, 1, CT)
            stats2(FULL // 2, 0, 1)
            bn_vectors(1)

            def elu2(i, q, tiles, first):
                w = CN if tiles == CT else TAIL
                if not first:
                    dve.wait_ge(z_mm[2], K4 * (2 * i + q - 1))
                for k in range(K3):
                    elu(1, k, 2 * i + q, w, a2[:, q, k, 0:w], K3)

            def stats3(i, q, tiles):
                column_stats(2, i, q, tiles, K4, lambda m, c, w: z[:, m, bass.ds(c * CN, w)])
            dve.wait_ge(z_mm[1], K3 * CHUNKS)
            for q in range(2):
                dve.wait_ge(z2_stored[q], 16 * (FULL // 2 + 1 - q))
            elu2(0, 0, CT, True)
            elu2(0, 1, CT, True)
            stats3(0, 0, CT)
            with dve.Fori(1, FULL // 2) as i:
                elu2(i, 0, CT, False)
                stats3(i - 1, 1, CT)
                elu2(i, 1, CT, False)
                stats3(i, 0, CT)
            elu2(FULL // 2, 0, 1, False)
            stats3(FULL // 2 - 1, 1, CT)
            stats3(FULL // 2, 0, 1)
            bn_vectors(2)
            dve.wait_ge(z_mm[2], K4 * CHUNKS)

            def elu3(i, q, tiles, first):
                w = CN if tiles == CT else TAIL
                if not first:
                    dve.wait_ge(o_mm, 2 * i + q - 1)
                for k in range(K4):
                    elu(2, k, 2 * i + q, w, a1[:, q, k, 0:w], K4)

            def result(i, q, tiles, first):
                c = 2 * i + q
                dve.wait_ge(o_mm, c + 1)
                dve.wait_ge(x1_loaded[q], 16 * (i + 1))
                to = x1_in[:, q, 0:tiles, :]
                bias = b4_bc[:, :].unsqueeze(1).to_broadcast([P, tiles, D])
                dve.tensor_tensor(to, to, bias, ALU.add).then_inc(o_b4, 1)
                dve.wait_ge(o_b4, c + 1)
                if not first:
                    dve.wait_ge(o_stored[q], 16 * i)
                dve.tensor_tensor(o_out[:, q, 0:tiles, :], ps_rows[q][:, 0:tiles, :], to, ALU.add).then_inc(o_ready, 1)
            elu3(0, 0, CT, True)
            elu3(0, 1, CT, True)
            result(0, 0, CT, True)
            elu3(1, 0, CT, False)
            result(0, 1, CT, True)
            elu3(1, 1, CT, False)
            result(1, 0, CT, False)
            with dve.Fori(2, FULL // 2) as i:
                elu3(i, 0, CT, False)
                result(i - 1, 1, CT, False)
                elu3(i, 1, CT, False)
                result(i, 0, CT, False)
            elu3(FULL // 2, 0, 1, False)
            result(FULL // 2 - 1, 1, CT, False)
            result(FULL // 2, 0, 1, False)

        @block.tensor
        def _(pe):
            pe.wait_ge(dve_small, 6)
            for a in range(2):
                mm = pe.matmul(ps[:, a, 0:GROUPS], ones[0:GROUPS, :], diag[0:GROUPS, a, 0:GROUPS], start=True, stop=True)
            mm.then_inc(prep_mm, 1)
            near = is_near(pe)
            pe.wait_ge(weights_in, 48)

            def turn(i, q, tiles, of, ready, free, done_, first):
                c = 2 * i + q
                pe.wait_ge(ready, c + 1)
                if not first:
                    pe.wait_ge(free, c - 1)
                for t in range(tiles):
                    for a in range(DH):
                        mm = pe.transpose(ps_cols[q][:, a, t * P:(t + 1) * P], of[:, q, t, a * P:(a + 1) * P], ident[:, :])
                mm.then_inc(done_, 1)

            def support(i, q, tiles, first):
                c = 2 * i + q
                turn(i, q, tiles, hr, ln_h[0], h_cols, h_turned, first)
                pe.wait_ge(h_cols, c + 1)
                if not first:
                    pe.wait_ge(sup_rows, c - 1)
                for t in range(tiles):
                    for a in range(DH):
                        mm = pe.matmul(ps_rows[q][:, t, :], stage[:, q, a, t * P:(t + 1) * P], wg_sb[:, a, :],
                                       start=(a == 0), stop=(a == DH - 1))
                mm.then_inc(sup_mm, 1)
            over_chunks(pe, support)
            pe.wait_ge(sup_rows, CHUNKS)

            def far_hop(h):
                with pe.Fori(0, TILES) as t:
                    n = h * TILES + t
                    pe.wait_ge(far_step, 4 * n + 1)
                    pe.transpose(ps_src[0][:, 0, :], src_ring[:, 0, 0:1].to_broadcast([P, P]), ident[:, :]).then_inc(far_turned, 1)
                    pe.wait_ge(far_same, n + 1)
                    pe.wait_ge(far_rows, 16 * n + 16)
                    pe.matmul(ps_msg[0][:, 0, :], same[:, 0, 0, :], rows[:, 0, 0, :], start=True, stop=True).then_inc(far_mm, 1)

            def first_hop(h):
                off = h * QUADS

                def turn_src(i, q, first):
                    u = 4 * i + q
                    par = q % 2
                    pe.wait_ge(src_staged, off + u + 1)
                    if not (first and q < 2):
                        pe.wait_ge(same_done, off + u - 1)
                        if h == 0:
                            pe.wait_ge(to_found, u - 1)
                    for t in range(QT):
                        mm = pe.transpose(ps_src[par][:, t, :], src_ring[:, q, t:t + 1].to_broadcast([P, P]), ident[:, :])
                    mm.then_inc(src_turned, 1)

                def mix_edges(i, q, first):
                    u = 4 * i + q
                    par = q % 2
                    pe.wait_ge(same_done, off + u + 1)
                    if not (first and q < 2):
                        pe.wait_ge(mix_done, off + u - 1)
                    for t in range(QT):
                        mm = pe.matmul(ps_mix[par][:, t, :], hot[:, par, t, :], same[:, par, t, :], start=True, stop=True)
                    mm.then_inc(mix_mm, 1)

                def messages(i, q, first):
                    u = 4 * i + q
                    par = q % 2
                    pe.wait_ge(mix_done, off + u + 1)
                    pe.wait_ge(window_in[q // 2], 16 * (off // 4 + i + 1))
                    if not (first and q < 2):
                        pe.wait_ge(msg_done, off + u - 1)
                    for t in range(QT):
                        mm = pe.matmul(ps_msg[par][:, t, :], mix[:, par, t, :], window[:, q // 2, :], start=True, stop=True)
                    mm.then_inc(msg_mm, 1)

                def step(i, q, first, last):
                    mix_edges(i, q, first)
                    if not (first and q == 0):
                        messages(i if q > 0 else i - 1, (q - 1) % 4, first)
                    if not (last and q > 1):
                        turn_src(i if q < 2 else i + 1, (q + 2) % 4, False)

                with pe.If(near):
                    for q in range(2):
                        turn_src(0, q, True)
                    over_quads(pe, step)
                    messages(QUADS // 4 - 1, 3, False)
                with pe.Else():
                    far_hop(h)
                pe.wait_ge(hop_done, h + 1)
            first_hop(0)
            first_hop(1)

            over_chunks(pe, lambda i, q, tiles, first: turn(i, q, tiles, nr, ln_h[1], c_cols, c_turned, first))

            def group(i, q, first, last):
                g = RING * i + q
                par = q % 2
                pe.wait_ge(onehot_ready, g + 1)
                pe.wait_ge(gathered[par], 16 * GT * (2 * i + q // 2 + 1))
                if not (first and q < 2):
                    pe.wait_ge(evac_done, g - 1)
                for t in range(GT):
                    for a in range(DH):
                        mm = pe.matmul(ps[:, 2 * par + a, 0:WIN], rows[:, par, t, a * P:(a + 1) * P],
                                       onehot[:, par, t, :], start=(t == 0), stop=(t == GT - 1))
                mm.then_inc(mm_done, 1)

            with pe.If(near):
                over_groups(pe, group)
            with pe.Else():
                far_hop(2)
                with pe.Fori(0, NT) as b:
                    pe.wait_ge(far_back, 16 * b + 16)
                    for a in range(DH):
                        mm = pe.transpose(ps[:, a, 0:P], rows[:, 0, 1, a * P:(a + 1) * P], ident[:, :])
                    mm.then_inc(far_cols, 1)
            pe.wait_ge(hop_done, 3)

            def z1(i, q, tiles, first):
                n = CN if tiles == CT else TAIL
                c = 2 * i + q
                for m in range(K2):
                    if not first:
                        pe.wait_ge(z_evac[0], K2 * (c - 2) + m + 1)
                    for k in range(K1):
                        mm = pe.matmul(ps[:, K2 * q + m, 0:n], w1_sb[:, k, m * P:(m + 1) * P],
                                       acc_b[:, k, bass.ds(c * CN, n)], start=(k == 0), stop=(k == K1 - 1))
                    mm.then_inc(z_mm[0], 1)
            over_chunks(pe, z1)

            pe.wait_ge(w23_in, 32)
            pe.wait_ge(z_evac[0], K2 * CHUNKS)
            for bank, w, kk, mm_ in ((0, w2_sb, K2, K3), (1, w3_sb, K3, K4)):
                for m in range(mm_):
                    for k in range(kk):
                        pe.matmul(ps[:, bank, m:m + 1], w[:, k, m * P:(m + 1) * P], ones[:, 0:1],
                                  start=(k == 0), stop=(k == kk - 1))
            for k in range(K4):
                mm = pe.matmul(ps[:, 2, 0:D], ones[:, :], w4_sb[:, k, :], start=(k == 0), stop=(k == K4 - 1))
            mm.then_inc(colsum_mm, 1)
            pe.wait_ge(colsum_done, 3)

            def z2(i, q, tiles, first):
                n = CN if tiles == CT else TAIL
                c = 2 * i + q
                pe.wait_ge(a_done[0], K2 * (c + 1))
                for m in range(K3):
                    if not (first and q == 0):
                        pe.wait_ge(z_evac[1], K3 * (c - 1) + m + 1)
                    for k in range(K2):
                        mm = pe.matmul(ps[:, m, 0:n], w2_sb[:, k, m * P:(m + 1) * P], a1[:, q, k, 0:n],
                                       start=(k == 0), stop=(k == K2 - 1))
                    mm.then_inc(z_mm[1], 1)
            over_chunks(pe, z2)
            pe.wait_ge(z_evac[1], K3 * CHUNKS)

            def z3(i, q, tiles, first):
                n = CN if tiles == CT else TAIL
                c = 2 * i + q
                pe.wait_ge(a_done[1], K3 * (c + 1))
                for m in range(K4):
                    if not first:
                        pe.wait_ge(z_evac[2], K4 * (c - 2) + m + 1)
                    for k in range(K3):
                        mm = pe.matmul(ps[:, K4 * q + m, 0:n], w3_sb[:, k, m * P:(m + 1) * P], a2[:, q, k, 0:n],
                                       start=(k == 0), stop=(k == K3 - 1))
                    mm.then_inc(z_mm[2], 1)
            over_chunks(pe, z3)
            pe.wait_ge(z_evac[2], K4 * CHUNKS)

            def last(i, q, tiles, first):
                rest = P if tiles == CT else TAIL
                c = 2 * i + q
                pe.wait_ge(a_done[2], K4 * (c + 1))
                if not first:
                    pe.wait_ge(o_ready, c - 1)
                for t in range(tiles):
                    for k in range(K4):
                        mm = pe.matmul(ps_rows[q][0:rest, t, :], a1[:, q, k, t * P:t * P + rest], w4_sb[:, k, :],
                                       start=(k == 0), stop=(k == K4 - 1))
                mm.then_inc(o_mm, 1)
            over_chunks(pe, last)


def kernel(**inputs):
    import numpy as np
    import concourse.bacc as bacc
    from concourse.bass_utils import run_bass_kernel_spmd

    nc = bacc.Bacc("TRN2", target_bir_lowering=False, num_devices=1)
    arrays, args = {}, []

    def give(name, a):
        a = np.ascontiguousarray(a)
        arrays[name] = a
        args.append(nc.dram_tensor(name, a.shape, mybir.dt.from_np(a.dtype), kind="ExternalInput").ap())

    def by_tile(a, mode):
        return np.pad(np.asarray(a), (0, TILES * P - E), mode=mode).reshape(TILES, P).T

    def by_feature(name):
        return np.asarray(inputs[name]).reshape(-1, P).T

    give("x", inputs["x"])
    give("src_t", by_tile(inputs["src"], "edge"))
    give("dst_t", by_tile(inputs["dst"], "edge"))
    give("dst_g", np.pad(np.asarray(inputs["dst"]), (0, TILES * P - E), mode="edge").reshape(GROUPS, GT * P))
    give("w_t", by_tile(inputs["edge_weight"], "constant"))
    give("wg", inputs["L0_gnn_weight"])
    give("logits", np.broadcast_to(np.asarray(inputs["L0_gnn_hop_logits"]), (P, 2)))
    give("eps", np.broadcast_to(np.asarray(inputs["L1_gnn_eps"]), (P, 1)))
    for n in (1, 2, 3):
        give(f"W{n}", inputs[f"L1_gnn_W{n}"])
        give(f"b{n}", by_feature(f"L1_gnn_b{n}"))
        give(f"g{n}", by_feature(f"L1_gnn_g{n}"))
        give(f"be{n}", by_feature(f"L1_gnn_beta{n}"))
    give("W4", inputs["L1_gnn_W4"])
    give("b4", np.broadcast_to(np.asarray(inputs["L1_gnn_b4"]), (P, D)))
    args.append(nc.dram_tensor("out_0_dram", (N, D), F32, kind="ExternalOutput").ap())
    gnn(nc, *args)
    r = run_bass_kernel_spmd(nc, [arrays], core_ids=[0])
    return r.results[0]["out_0_dram"]
```

```python
from contextlib import ExitStack

import concourse.bass as bass
from concourse import mybir

F32 = mybir.dt.float32
F32R = mybir.dt.float32r
I32 = mybir.dt.int32
ALU = mybir.AluOpType
ACT = mybir.ActivationFunctionType
AX_X = mybir.AxisListType.X

P = 128
N = 6250
D = 256
E = 106250
DH = D // P
LN_EPS = 1e-5
BN_EPS = 1e-5

GT = 8
GROUPS = -(-E // (GT * P))
TILES = GROUPS * GT
RING = 4
WIN = P

CT = 4
CN = CT * P
FULL = N // CN
CHUNKS = FULL + 1
TAIL = N - FULL * CN
NT = FULL * CT + 1
ROWS = NT * P
QT = 4
QUADS = TILES // QT
COPIES = QT
ZR = -(-(N + P) // (QUADS // 4))
SPARE = ZR * (QUADS // 4)
FAR = 65536.0

H1, H2, H3 = 512, 1024, 512
K1, K2, K3, K4 = D // P, H1 // P, H2 // P, H3 // P

assert TAIL <= P and FULL % 2 == 0 and GROUPS % RING == 0 and GT == 2 * QT and SPARE >= ROWS
assert SPARE % (CHUNKS * ZR) == 0 and ZR <= P


def over_chunks(eng, step):
    for q in range(2):
        step(0, q, CT, True)
    with eng.Fori(1, FULL // 2) as i:
        for q in range(2):
            step(i, q, CT, False)
    step(FULL // 2, 0, 1, False)


def over_groups(eng, step):
    for q in range(RING):
        step(0, q, True, False)
    with eng.Fori(1, GROUPS // RING - 1) as i:
        for q in range(RING):
            step(i, q, False, False)
    for q in range(RING):
        step(GROUPS // RING - 1, q, False, True)


def over_quads(eng, step):
    for q in range(4):
        step(0, q, True, False)
    with eng.Fori(1, QUADS // 4 - 1) as i:
        for q in range(4):
            step(i, q, False, False)
    for q in range(4):
        step(QUADS // 4 - 1, q, False, True)


def rest_of_table(eng, extra, step=lambda i, q, first, last: None):
    def both(i, tiles, after, first):
        for q in range(4):
            step(i, q, first, False)
            extra(i, q, tiles, after, first)
    both(0, CT, CT, True)
    with eng.Fori(1, CHUNKS - 3) as i:
        both(i, CT, CT, False)
    both(CHUNKS - 3, CT, 1, False)
    both(CHUNKS - 2, 1, 0, False)


def over_quads_and_table(eng, step, extra, behind=lambda q: None):
    rest_of_table(eng, extra, step)
    with eng.Fori(CHUNKS - 1, QUADS // 4 - 1) as i:
        for q in range(4):
            behind(q)
            step(i, q, False, False)
    for q in range(4):
        step(QUADS // 4 - 1, q, False, True)


def gnn(nc, x, src_t, dst_t, dst_g, w_t, wg, logits, eps, W1, b1, g1, be1, W2, b2, g2, be2,
        W3, b3, g3, be3, W4, b4, out):
    with ExitStack() as ctx:
        def sb(name, shape, dt=F32):
            return ctx.enter_context(nc.sbuf_tensor(name, shape, dt))

        def both(name, n):
            with nc.sbuf_tensor(name, [P, n], F32) as a:
                pass
            return a, sb(name + "_r", [P, n], F32R)

        def sem(name):
            return ctx.enter_context(nc.semaphore(name))

        def dram(name, shape):
            return nc.dram_tensor(name, shape, F32, kind="Internal").ap()

        table = [dram("table_hop1", (ROWS, D)), dram("table_hop2", (ROWS, D)), dram("table_gin", (ROWS, D))]
        copies = [[dram(f"hop{h + 1}_copy{k}", (SPARE, D)) for k in range(COPIES)] for h in range(2)]
        x1_dram = dram("x1_dram", (ROWS, D))
        z2_dram = dram("z2_dram", (CHUNKS * P, K3 * CN))

        big = sb("big", [P, K2 * N])
        sum_b, sum_r = both("sum_b", DH * ROWS)
        edge_buf, edge_r = both("edge_buf", 5 * TILES)
        work, work_r = both("work", 8 * CT * D)
        w1_all, w1_r = both("w1", K1 * H1)
        w1_sb = w1_all[:, :].rearrange("p (k m) -> p k m", k=K1)
        w4_sb = sb("w4_sb", [P, K4, D])
        iota = sb("iota", [P, WIN])
        ident = sb("ident", [P, P])
        ones = sb("ones", [P, P])

        acc_b = sum_b[:, :].rearrange("p (h n) -> p h n", h=DH)
        z = big[:, :].rearrange("p (m n) -> p m n", m=K2)

        src_all = edge_buf[:, 0:TILES]
        dst_all = edge_buf[:, TILES:2 * TILES]
        dst_loc = edge_buf[:, 2 * TILES:3 * TILES]
        w_all = edge_buf[:, 3 * TILES:4 * TILES]
        to_all = edge_buf[:, 4 * TILES:5 * TILES].bitcast(I32)

        rows = work[:, 0:2 * GT * D].rearrange("p (s t d) -> p s t d", s=2, t=GT)
        onehot = work[:, 2 * GT * D:2 * GT * (D + WIN)].rearrange("p (s t w) -> p s t w", s=2, t=GT)
        dst_i = work[:, 0:TILES].bitcast(I32)
        dst_gi = work[:, TILES:TILES + GT * P].bitcast(I32)
        src_i = work[:, TILES + GT * P:2 * TILES + GT * P].bitcast(I32)
        diag = work[:, 3 * TILES:3 * TILES + 2 * P].rearrange("p (a b) -> p a b", a=2)
        made = work[:, 3 * TILES + 2 * P:3 * TILES + 2 * P + GROUPS]
        stage = work[:, 8 * CT * D - 2 * DH * CN:8 * CT * D].rearrange("p (s h n) -> p s h n", s=2, h=DH)
        parts = work[:, :].rearrange("p (s k t d) -> p s k t d", s=2, k=COPIES, t=CT)
        assert 3 * TILES + 2 * P + GROUPS <= 8 * CT * D - 2 * DH * CN

        at = [0]

        def place(n, **dims):
            at[0] += 2 * n
            return big[:, at[0] - 2 * n:at[0]]
        window = place(D).rearrange("p (s d) -> p s d", s=2)
        same = place(QT * P).rearrange("p (s t e) -> p s t e", s=2, t=QT)
        hot = place(QT * P).rearrange("p (s t e) -> p s t e", s=2, t=QT)
        mix = place(QT * P).rearrange("p (s t e) -> p s t e", s=2, t=QT)
        msgs = place(QT * D).rearrange("p (s t d) -> p s t d", s=2, t=QT)
        hr, nr = [place(CT * D).rearrange("p (s t d) -> p s t d", s=2, t=CT) for _ in range(2)]
        wg_sb = place(DH * D // 2).rearrange("p (k m) -> p k m", k=DH)
        zeros = place(D // 2)
        at[0] += NT * D
        x_res = big[:, at[0] - NT * D:at[0]]
        before = big[:, at[0]:at[0] + P]
        same_src = big[:, at[0] + P:at[0] + (1 + QT) * P].rearrange("p (t e) -> p t e", e=P)
        assert at[0] + (1 + QT) * P <= K2 * N

        base_bc = sb("base_bc", [P, GROUPS])
        reach = sb("reach", [P, 2])
        base_i = sb("base_i", [1, GROUPS], I32)
        reach_i = sb("reach_i", [1, 1], I32)
        ends = sb("ends", [P, 2])
        idx = sb("idx", [P, RING, GT], I32)
        to_ring = sb("to_ring", [P, 4, QT], I32)
        src_ring = sb("src_ring", [P, 4, QT])
        dup = sb("dup", [P, 4, QT])
        dup_to = sb("dup_to", [P, 4, QT])
        from_any = sb("from_any", [P, 1], I32)
        spare_row = sb("spare_row", [P, 1])
        lg = sb("lg", [P, 2])
        hw = sb("hw", [P, 8])
        eps_sb = sb("eps_sb", [P, 2])
        done = sb("done", [P, 1])
        lst = sb("lst", [P, 2, CT, 6])
        lmv = sb("lmv", [P, 2, CT, 2])
        lve = sb("lve", [P, 2, CT])
        lsd = sb("lsd", [P, 2, CT])
        lrs = sb("lrs", [P, 2, CT])
        lnm = sb("lnm", [P, 2, CT])

        M = [K2, K3, K4]
        bvec = [sb(f"bvec{n}", [P, M[n]]) for n in range(3)]
        gvec = [sb(f"gvec{n}", [P, M[n]]) for n in range(3)]
        tvec = [sb(f"tvec{n}", [P, M[n]]) for n in range(3)]
        b4_bc = sb("b4_bc", [P, D])
        stats = edge_buf[:, 4 * CN:4 * CN + K3 * CHUNKS * 6].rearrange("p (m c s) -> p m c s", m=K3, c=CHUNKS)
        at = [4 * CN + K3 * CHUNKS * 6]
        bn = edge_buf[:, at[0]:at[0] + 8 * K3].rearrange("p (a m) -> p a m", a=8)
        mv = edge_buf[:, at[0] + 8 * K3:at[0] + 10 * K3].rearrange("p (m a) -> p m a", a=2)
        w1_hi = edge_r[:, at[0] + 10 * K3:at[0] + 10 * K3 + K1 * H1]
        assert at[0] + 10 * K3 + K1 * H1 <= 5 * TILES and 3 * K3 * CN <= DH * ROWS
        ev = edge_buf[:, 0:2 * CN].rearrange("p (s n) -> p s n", s=2)
        yv = edge_buf[:, 2 * CN:4 * CN].rearrange("p (s n) -> p s n", s=2)

        def split(region, kk):
            return [a.rearrange("p (k m) -> p k m", k=kk) for a in region]
        w1_split = split([w1_hi, w1_r[:, :]], K1)
        w2_raw, w3_raw = [work[:, K2 * H2:2 * K2 * H2].rearrange("p (k m) -> p k m", k=kk) for kk in (K2, K3)]
        w2_split, w3_split = [split([work_r[:, 0:K2 * H2], work_r[:, K2 * H2:2 * K2 * H2]], kk) for kk in (K2, K3)]
        a0 = edge_r[:, 0:4 * CN].rearrange("p (k x n) -> p k x n", k=K1, x=2)
        a1 = sum_r[:, 0:4 * K2 * CN].rearrange("p (s k x n) -> p s k x n", s=2, k=K2, x=2)
        z2_out = sum_b[:, 4 * K2 * CN:4 * K2 * CN + K3 * CN].rearrange("p (h m n) -> p h m n", h=2, m=K3 // 2)
        z2_in = sum_b[:, 0:K3 * CN].rearrange("p (k n) -> p k n", k=K3)
        a2 = sum_r[:, K3 * CN:3 * K3 * CN].rearrange("p (k x n) -> p k x n", k=K3, x=2)
        a3 = sum_b[:, 0:2 * K4 * CN].rearrange("p (s k n) -> p s k n", s=2, k=K4)
        x1_in = sum_b[:, 2 * K4 * CN:2 * K4 * CN + 2 * CT * D].rearrange("p (s t d) -> p s t d", s=2, t=CT)
        o_out = sum_b[:, 2 * K4 * CN + 2 * CT * D:2 * K4 * CN + 4 * CT * D].rearrange("p (s t d) -> p s t d", s=2, t=CT)

        ps = ctx.enter_context(nc.psum_tensor("ps", [P, 8, 512], F32))
        ps_rows = [ps[:, 2 * s:2 * s + 2, :].rearrange("p b (t d) -> p (b t) d", d=D) for s in range(2)]
        ps_cols = [ps[:, 4 + 2 * s:6 + 2 * s, :] for s in range(2)]

        ps_src = [ps[:, s, :].rearrange("p (t e) -> p t e", e=P) for s in range(2)]
        ps_mix = [ps[:, 2 + s, :].rearrange("p (t e) -> p t e", e=P) for s in range(2)]
        ps_msg = [ps[:, 4 + 2 * s:6 + 2 * s, :].rearrange("p b (t d) -> p (b t) d", d=D) for s in range(2)]

        edges_in = sem("edges_in")
        vectors_in = sem("vectors_in")
        weights_in = sem("weights_in")
        consts_made = sem("consts_made")
        dst_cast = sem("dst_cast")
        dst_masked = sem("dst_masked")
        prep = sem("prep")
        prep_mm = sem("prep_mm")
        edges_ready = sem("edges_ready")
        act_small = sem("act_small")
        dve_small = sem("dve_small")
        zeroed = sem("zeroed")
        zeros_stored = sem("zeros_stored")
        zeros2_stored = sem("zeros2_stored")
        hop_done = sem("hop_done")
        window_in = [sem("window_in0"), sem("window_in1")]
        src_staged = sem("src_staged")
        src_turned = sem("src_turned")
        dup_found = sem("dup_found")
        to_step = sem("to_step")
        to_found = sem("to_found")
        same_done = sem("same_done")
        mix_mm = sem("mix_mm")
        mix_done = sem("mix_done")
        msg_mm = sem("msg_mm")
        msg_done = sem("msg_done")
        to_staged = sem("to_staged")
        scattered = [sem(f"scattered{k}") for k in range(COPIES)]
        scatter_opened = sem("scatter_opened")
        far_src = sem("far_src")
        far_turned = sem("far_turned")
        far_rows = sem("far_rows")
        far_step = sem("far_step")
        far_same = sem("far_same")
        far_mm = sem("far_mm")
        far_msg = sem("far_msg")
        far_done = sem("far_done")
        idx_ready = sem("idx_ready")
        gathered = [sem("gathered0"), sem("gathered1")]
        gather_opened = sem("gather_opened")
        ln_aggr_opened = sem("ln_aggr_opened")
        eq_done = sem("eq_done")
        onehot_ready = sem("onehot_ready")
        mm_done = sem("mm_done")
        evac_done = sem("evac_done")
        far_zeroed = sem("far_zeroed")
        far_back = sem("far_back")
        far_cols = sem("far_cols")
        far_added = sem("far_added")
        ln_in = [[sem(f"ln{n}_in{q}") for q in range(2)] for n in range(2)]
        ln_pad = sem("ln_pad")
        ln_bn = [sem(f"ln{n}_bn") for n in range(2)]
        ln_ag = [sem(f"ln{n}_ag") for n in range(2)]
        ln_var = [sem(f"ln{n}_var") for n in range(2)]
        ln_std = [sem(f"ln{n}_std") for n in range(2)]
        ln_rstd = [sem(f"ln{n}_rstd") for n in range(2)]
        ln_coef = [sem(f"ln{n}_coef") for n in range(2)]
        ln_h = [sem(f"ln{n}_h") for n in range(2)]
        ln_stored = [sem(f"ln1_stored{q}") for q in range(2)]
        h_turned = sem("h_turned")
        h_cols = sem("h_cols")
        sup_mm = sem("sup_mm")
        sup_rows = sem("sup_rows")
        sup_stored = [sem(f"sup_stored{q}") for q in range(2)]
        t2_in = [sem(f"t2_in{q}") for q in range(2)]
        t2_half = sem("t2_half")
        t2_other = sem("t2_other")
        t2_rows = sem("t2_rows")
        t2_stored = sem("t2_stored")
        w_scaled = sem("w_scaled")
        h_kept = sem("h_kept")
        t2_kept = sem("t2_kept")
        rest_in = [sem(f"rest_in{k}") for k in range(COPIES)]
        rest_opened = sem("rest_opened")
        rest_half = sem("rest_half")
        rest_other = sem("rest_other")
        rest_rows = sem("rest_rows")
        rest_kept = sem("rest_kept")
        rest_stored = sem("rest_stored")
        x1_stored = sem("x1_stored")
        c_quarter = sem("c_quarter")
        c_half = sem("c_half")
        c_other = sem("c_other")
        c_sum = sem("c_sum")
        c_x1 = sem("c_x1")
        c_turned = sem("c_turned")
        c_cols = sem("c_cols")
        z_mm = [sem(f"z{n}_mm") for n in range(3)]
        z_evac = [sem(f"z{n}_evac") for n in range(3)]
        z_stat = [sem(f"z{n}_stat") for n in range(3)]
        bn_step = [sem(f"bn{n}_step") for n in range(3)]
        bn_std = [sem(f"bn{n}_std") for n in range(3)]
        bn_ready = [sem(f"bn{n}_ready") for n in range(3)]
        e_done = [sem(f"e{n}_done") for n in range(3)]
        a_done = [sem(f"a{n}_done") for n in range(3)]
        z2_stored = [sem(f"z2_stored_half{h}") for h in range(2)]
        z2_loaded = sem("z2_loaded")
        w2_in = sem("w2_in")
        w3_in = sem("w3_in")
        w_hi = sem("w_hi")
        w_split = sem("w_split")
        sums_hi = sem("sums_hi")
        sums_split = sem("sums_split")
        sums_used = sem("sums_used")
        a2_used = sem("a2_used")
        elu_done = [sem(f"elu{n}_done") for n in range(2)]
        hi_done = [sem(f"hi{n}_done") for n in range(2)]
        colsum_mm = sem("colsum_mm")
        colsum_done = sem("colsum_done")
        x1_loaded = [sem(f"x1_loaded{q}") for q in range(2)]
        o_mm = sem("o_mm")
        o_b4 = sem("o_b4")
        o_ready = sem("o_ready")
        o_stored = [sem(f"o_stored{q}") for q in range(2)]

        block = ctx.enter_context(nc.Block())

        def rows_of(t, c, tiles):
            return t[bass.ds(c * CN, tiles * P), :].rearrange("(t p) d -> p t d", p=P)

        def x_rows(c, tiles):
            return x_res[:, bass.ds(c * CT * D, tiles * D)]

        def x_tile(c, t):
            return x_res[:, bass.ds(c * CT * D + t * D, D)]

        def base_of(c, tiles):
            return acc_b[:, :, bass.ds(c * CN, tiles * P)]

        def as_base(buf, tiles):
            return buf[:, 0:tiles, :].rearrange("p t d -> p (t d)").rearrange("p (h n) -> p h n", h=DH)

        def zero_rows(eng, h, i, s):
            for k in range(COPIES):
                eng.dma_start(copies[h][k][bass.ds(i * ZR, ZR), :], zeros[0:ZR, :]).then_inc(s, 16)

        def is_near(eng):
            eng.wait_ge(edges_ready, 1)
            return eng.value_load(reach_i[0:1, 0:1], min_val=0, max_val=N) < WIN

        @block.sync
        def _(sp):
            sp.dma_start(dst_i, dst_t).then_inc(edges_in, 16)
            sp.dma_start(dst_gi[0:GROUPS, :], dst_g).then_inc(edges_in, 16)
            sp.dma_start(src_i, src_t).then_inc(edges_in, 16)
            sp.dma_start(w_all, w_t).then_inc(edges_in, 16)
            for to, of in ((lg[:, :], logits), (eps_sb[:, 0:1], eps), (b4_bc[:, :], b4),
                           (bvec[0][:, :], b1), (gvec[0][:, :], g1), (tvec[0][:, :], be1),
                           (bvec[1][:, :], b2), (gvec[1][:, :], g2), (tvec[1][:, :], be2),
                           (bvec[2][:, :], b3), (gvec[2][:, :], g3), (tvec[2][:, :], be3)):
                sp.dma_start(to, of).then_inc(vectors_in, 16)
            sp.dma_start(wg_sb, wg.rearrange("(k p) m -> p k m", p=P)).then_inc(weights_in, 16)
            sp.dma_start(w1_sb[:, :, :], W1.rearrange("(k p) m -> p k m", p=P)).then_inc(weights_in, 16)
            sp.dma_start(w4_sb[:, :, :], W4.rearrange("(k p) m -> p k m", p=P)).then_inc(weights_in, 16)

            def ln0(i, q, tiles, first):
                c = 2 * i + q
                if not first:
                    sp.wait_ge(ln_in[0][q], 16 * i)
                if tiles == CT:
                    to = x_rows(c, tiles).rearrange("p (t d) -> p t d", d=D)
                    sp.dma_start(to, rows_of(x, c, tiles)).then_inc(ln_in[0][q], 16)
                else:
                    sp.wait_ge(ln_pad, 1)
                    sp.dma_start(x_rows(c, 1)[0:TAIL, :], x[FULL * CN:N, :]).then_inc(ln_in[0][q], 16)
            over_chunks(sp, ln0)
            near = is_near(sp)

            def rest_part(c, k, tiles):
                sp.dma_start(parts[:, 0, k, 0:tiles, :], rows_of(copies[0][k], c, tiles)).then_inc(rest_in[k], 16)

            def rest_load(i, q, tiles, after, first):
                if q == 0:
                    if first:
                        sp.wait_ge(t2_rows, 1)
                        rest_part(1, 1, CT)
                        rest_part(1, 3, CT)
                    else:
                        sp.wait_ge(rest_rows, i)
                        sp.sem_inc(rest_opened, 1)
                    rest_part(i + 1, 0, tiles)
                elif q == 1:
                    rest_part(i + 1, 2, tiles)
                elif after:
                    sp.wait_ge(rest_half if q == 2 else rest_other, i + 1)
                    sp.sem_inc(rest_opened, 1)
                    rest_part(i + 2, 2 * q - 3, after)

            def hop(h, table_ready):
                off = h * QUADS
                for s, n in table_ready:
                    sp.wait_ge(s, n)

                def load(i, q, first, last):
                    if q % 2 == 0:
                        g = 2 * i + q // 2
                        par = q // 2
                        base = sp.value_load(base_i[0:1, bass.ds(g, 1)], min_val=0, max_val=ROWS - WIN)
                        if not first:
                            sp.wait_ge(msg_mm, off + 4 * i + q - 2)
                        sp.dma_start(window[:, par, :], table[h][bass.ds(base, WIN), :]).then_inc(window_in[par], 16)
                    elif h == 0 and q == 1:
                        zero_rows(sp, 1, i, zeros2_stored)

                def table_of_step(i, q, tiles, after, first):
                    if q == 1 and not first:
                        sp.wait_ge(msg_mm, off + 4 * i)
                        sp.sem_inc(rest_opened, 1)
                    rest_load(i, q, tiles, after, first)
                    if q == 3 and not first:
                        sp.wait_ge(rest_stored, 16 * i)
                        sp.sem_inc(rest_opened, 1)

                def whole_table(q):
                    if q == 2:
                        sp.wait_ge(rest_stored, 16 * (CHUNKS - 1))

                with sp.If(near):
                    if h == 0:
                        over_quads(sp, load)
                    else:
                        over_quads_and_table(sp, load, table_of_step, whole_table)
                with sp.Else():
                    if h == 0:
                        with sp.Fori(0, QUADS // 4) as i:
                            zero_rows(sp, 1, i, zeros2_stored)
                    else:
                        rest_of_table(sp, rest_load)
                sp.wait_ge(hop_done, h + 1)

            def load_parts(h, i, q, tiles, s):
                for k in range(COPIES):
                    sp.dma_start(parts[:, q, k, 0:tiles, :], rows_of(copies[h][k], 2 * i + q, tiles)).then_inc(s[q], 16)
            hop(0, [(sup_stored[0], 16 * (FULL // 2 + 1)), (sup_stored[1], 16 * (FULL // 2))])

            def t2(i, q, tiles, first):
                load_parts(0, i, q, tiles, t2_in)
            t2(0, 0, CT, True)
            hop(1, [(t2_stored, 16)])

            def mid_in(i, q, tiles, first):
                if not first:
                    sp.wait_ge(c_x1, 2 * i + q - 1)
                load_parts(1, i, q, tiles, ln_in[1])
            over_chunks(sp, mid_in)
            sp.wait_ge(c_x1, CHUNKS)

            def x1_out(i, q, tiles, paced):
                if paced:
                    sp.wait_ge(mm_done, 2 * i + q + 1)
                    sp.sem_inc(rest_opened, 1)
                sp.dma_start(rows_of(x1_dram, 2 * i + q, tiles),
                             x_rows(2 * i + q, tiles).rearrange("p (t d) -> p t d", d=D)).then_inc(x1_stored, 16)
            with sp.If(near):
                over_chunks(sp, lambda i, q, tiles, first: x1_out(i, q, tiles, True))
            with sp.Else():
                over_chunks(sp, lambda i, q, tiles, first: x1_out(i, q, tiles, False))

            sp.wait_ge(hop_done, 3)
            sp.dma_start(w2_raw, W2.rearrange("(k p) m -> p k m", p=P)).then_inc(w2_in, 16)

            def z2_save(i, q, tiles, first):
                n = CN if tiles == CT else TAIL
                c = 2 * i + q
                to = z2_dram[bass.ds(c * P, P), :].rearrange("p (h m n) -> p h m n", h=2, m=K3 // 2)
                for h in range(2):
                    sp.wait_ge(z_evac[1], K3 * c + (h + 1) * (K3 // 2))
                    sp.dma_start(to[:, h, :, 0:n], z2_out[:, h, :, 0:n]).then_inc(z2_stored[h], 16)
            over_chunks(sp, z2_save)

            sp.wait_ge(z_mm[1], K3 * CHUNKS)
            sp.dma_start(w3_raw, W3.rearrange("(k p) m -> p k m", p=P)).then_inc(w3_in, 16)
            for h in range(2):
                sp.wait_ge(z2_stored[h], 16 * CHUNKS)

            def z2_load(i, q, tiles, first):
                n = CN if tiles == CT else TAIL
                if not (first and q == 0):
                    sp.wait_ge(e_done[1], K3 * (2 * i + q))
                of = z2_dram[bass.ds((2 * i + q) * P, P), :].rearrange("p (k n) -> p k n", k=K3)
                sp.dma_start(z2_in[:, :, 0:n], of[:, :, 0:n]).then_inc(z2_loaded, 16)
            over_chunks(sp, z2_load)

            sp.wait_ge(z_mm[2], K4 * CHUNKS)
            sp.wait_ge(x1_stored, 16 * CHUNKS)

            def last(i, q, tiles, first):
                if not first:
                    sp.wait_ge(o_ready, 2 * i + q - 1)
                sp.dma_start(x1_in[:, q, 0:tiles, :], rows_of(x1_dram, 2 * i + q, tiles)).then_inc(x1_loaded[q], 16)
            over_chunks(sp, last)
            sp.wait_ge(o_stored[0], 16 * (FULL // 2 + 1))
            sp.wait_ge(o_stored[1], 16 * (FULL // 2))

        @block.gpsimd
        def _(pool):
            pool.memset(ident[:, :], 0.0).then_inc(consts_made, 1)
            pool.wait_ge(consts_made, 1)
            pool.affine_select(out=ident[:, :], in_=ident[:, :], compare_op=ALU.not_equal, fill=1.0, base=0,
                               pattern=[[-1, P]], channel_multiplier=1).then_inc(consts_made, 1)
            pool.memset(ones[:, :], 1.0).then_inc(consts_made, 1)
            pool.iota(iota[:, :], pattern=[[1, WIN]], base=0, channel_multiplier=0,
                      allow_small_or_imprecise_dtypes=True).then_inc(consts_made, 1)
            pool.iota(made, pattern=[[CN, GROUPS // 2], [0, 2]], base=0, channel_multiplier=0,
                      allow_small_or_imprecise_dtypes=True).then_inc(consts_made, 1)
            pool.wait_ge(consts_made, 3)
            pool.affine_select(out=before, in_=ones[:, :], compare_op=ALU.is_gt, fill=0.0, base=0,
                               pattern=[[-1, P]], channel_multiplier=1).then_inc(consts_made, 1)
            pool.iota(spare_row[:, :], pattern=[[0, 1]], base=N, channel_multiplier=1,
                      allow_small_or_imprecise_dtypes=True).then_inc(consts_made, 1)
            pool.wait_ge(dst_cast, 1)
            t0 = TILES - GT
            pool.affine_select(out=dst_all[:, t0:TILES], in_=dst_all[:, t0:TILES], compare_op=ALU.is_ge, fill=FAR,
                               base=E - 1 - t0 * P, pattern=[[-P, GT]], channel_multiplier=-1).then_inc(dst_masked, 1)

            def support(i, q, tiles, first):
                c = 2 * i + q
                pool.wait_ge(ln_h[0], c + 1)
                pool.tensor_copy(base_of(c, tiles), as_base(hr[:, q], tiles)).then_inc(h_kept, 1)
                pool.wait_ge(sup_rows, c + 1)
                pool.sem_inc(scatter_opened, 1)
                pool.dma_start(rows_of(table[0], c, tiles), nr[:, q, 0:tiles, :]).then_inc(sup_stored[q], 16)
            over_chunks(pool, support)
            near = is_near(pool)

            def far_hop(h, sums):
                with pool.Fori(0, TILES) as t:
                    n = h * TILES + t
                    pool.wait_ge(far_src, n + 1)
                    pool.sem_inc(scatter_opened, 1)
                    pool.indirect_dma_start(rows[:, 0, 0, :], None, table[h],
                                            bass.IndirectOffsetOnAxis(from_any[:, 0:1], 0)).then_inc(far_rows, 16)
                    pool.wait_ge(far_msg, n + 1)
                    pool.sem_inc(scatter_opened, 1)
                    pool.indirect_dma_start(sums, bass.IndirectOffsetOnAxis(to_ring[:, 0, 0:1], 0),
                                            msgs[:, 0, 0, :], None, compute_op=ALU.add).then_inc(far_done, 16)

            def scatter_hop(h, sums_ready):
                off = h * QUADS
                for s, n in sums_ready:
                    pool.wait_ge(s, n)

                def scatter(i, q, first, last):
                    u = 4 * i + q
                    pool.wait_ge(msg_done, off + u + 1)
                    pool.wait_ge(to_staged, off + u + 1)
                    pool.sem_inc(scatter_opened, 1)
                    for t in range(QT):
                        if not (first and q == 0):
                            pool.wait_ge(scattered[t], 16 * (off + u))
                            pool.sem_inc(scatter_opened, 1)
                        pool.indirect_dma_start(copies[h][t], bass.IndirectOffsetOnAxis(to_ring[:, q, t:t + 1], 0),
                                                msgs[:, q % 2, t, :], None, compute_op=ALU.add).then_inc(scattered[t], 16)

                with pool.If(near):
                    over_quads(pool, scatter)
                with pool.Else():
                    if h == 1:
                        pool.wait_ge(t2_stored, 16)
                        pool.wait_ge(rest_stored, 16 * (CHUNKS - 1))
                    far_hop(h, copies[h][0])
                pool.wait_ge(hop_done, h + 1)

            def add_parts(i, q, tiles, loaded, done_):
                pool.wait_ge(loaded[q], 16 * COPIES * (i + 1))
                pool.tensor_tensor(parts[:, q, 2, 0:tiles, :], parts[:, q, 2, 0:tiles, :], parts[:, q, 3, 0:tiles, :],
                                   ALU.add).then_inc(done_, 1)

            def add_base(i, q, tiles, first):
                c = 2 * i + q
                add_parts(i, q, tiles, ln_in[1], c_quarter)
                pool.wait_ge(c_quarter, c + 1)
                to = as_base(parts[:, q, 2], tiles)
                pool.tensor_tensor(to, to, base_of(c, tiles), ALU.add).then_inc(c_other, 1)

            scatter_hop(0, [(zeros_stored, 16 * COPIES * CHUNKS), (sup_stored[0], 16 * (FULL // 2 + 1)),
                            (sup_stored[1], 16 * (FULL // 2))])
            add_parts(0, 0, CT, t2_in, t2_other)
            scatter_hop(1, [(zeros2_stored, 16 * COPIES * (QUADS // 4))])
            over_chunks(pool, add_base)

            def gather_hop(table_ready):
                off = 0
                for s, n in table_ready:
                    pool.wait_ge(s, n)

                def gather(i, q, first, last):
                    par = q % 2
                    pool.wait_ge(idx_ready, off + RING * i + q + 1)
                    if not (first and q < 2):
                        pool.wait_ge(mm_done, off + RING * i + q - 1)
                    pool.sem_inc(gather_opened, 1)
                    for t in range(GT):
                        pool.indirect_dma_start(rows[:, par, t, :], None, table[2],
                                                bass.IndirectOffsetOnAxis(idx[:, q, t:t + 1], 0)).then_inc(gathered[par], 16)

                with pool.If(near):
                    over_groups(pool, gather)
                with pool.Else():
                    with pool.Fori(0, QUADS // 4) as i:
                        pool.dma_start(copies[0][0][bass.ds(i * ZR, ZR), :], zeros[0:ZR, :]).then_inc(far_zeroed, 16)
                    pool.wait_ge(far_zeroed, 16 * (QUADS // 4))
                    far_hop(2, copies[0][0])
                    pool.wait_ge(far_done, 16 * 3 * TILES)
                    with pool.Fori(0, NT) as b:
                        pool.dma_start(rows[:, 0, 1, :], copies[0][0][bass.ds(b * P, P), :]).then_inc(far_back, 16)
                        pool.wait_ge(far_added, b + 1)
                pool.wait_ge(hop_done, 3)
            gather_hop([(ln_stored[0], 16 * (FULL // 2 + 1)), (ln_stored[1], 16 * (FULL // 2))])

            n = 0
            for loaded, raw, (hi, lo), kk in ((None, w1_sb, w1_split, K1), (w2_in, w2_raw, w2_split, K2),
                                              (w3_in, w3_raw, w3_split, K3)):
                if loaded is None:
                    pool.wait_ge(weights_in, 48)
                else:
                    pool.wait_ge(loaded, 16)
                for k in range(kk):
                    n += 1
                    pool.tensor_copy(hi[:, k, :], raw[:, k, :]).then_inc(w_hi, 1)
                    pool.wait_ge(w_hi, n)
                    pool.tensor_tensor(lo[:, k, :], raw[:, k, :], hi[:, k, :].bitcast(F32), ALU.subtract).then_inc(w_split, 1)

        @block.scalar
        def _(act):
            act.wait_ge(prep, 2)
            act.activation(hw[:, 0:2], lg[:, :], ACT.Exp, bias=hw[:, 3:4]).then_inc(act_small, 1)

            def ln_std_and_norm(n, i, q, tiles, to):
                c = 2 * i + q
                act.wait_ge(ln_var[n], c + 1)
                act.activation(lsd[:, q, 0:tiles], lve[:, q, 0:tiles], ACT.Sqrt).then_inc(ln_std[n], 1)
                act.wait_ge(ln_coef[n], c + 1)
                for t in range(tiles):
                    last = act.activation(to[:, q, t, :], x_tile(c, t), ACT.Relu,
                                          scale=lrs[:, q, t:t + 1], bias=lnm[:, q, t:t + 1])
                last.then_inc(ln_h[n], 1)

            def zero_sums(c):
                n = SPARE // CHUNKS
                for k in range(COPIES):
                    act.dma_start(copies[0][k][bass.ds(c * n, n), :].rearrange("(p a) d -> p a d", p=ZR),
                                  zeros[0:ZR, :].unsqueeze(1).to_broadcast([ZR, n // ZR, D])).then_inc(zeros_stored, 16)

            act.wait_ge(zeroed, 1)

            def ln0(i, q, tiles, first):
                c = 2 * i + q
                zero_sums(c)
                if not first:
                    act.wait_ge(h_kept, c - 1)
                    act.wait_ge(h_turned, c - 1)
                ln_std_and_norm(0, i, q, tiles, hr)
                if not first:
                    act.wait_ge(sup_mm, c - 1)
                act.wait_ge(h_turned, c + 1)
                act.copy(stage[:, q, :, 0:tiles * P], ps_cols[q][:, :, 0:tiles * P]).then_inc(h_cols, 1)
            over_chunks(act, ln0)
            near = is_near(act)

            def first_hop(h):
                off = h * QUADS

                def stage_src(i, q, first):
                    u = 4 * i + q
                    if not first:
                        act.wait_ge(src_turned, off + u - 3)
                    act.wait_ge(edges_ready, 1)
                    act.copy(src_ring[:, q, :], src_all[:, bass.ds(u * QT, QT)]).then_inc(src_staged, 1)

                def take_mix(i, q, first):
                    u = 4 * i + q
                    par = q % 2
                    act.wait_ge(mix_mm, off + u + 1)
                    if not (first and q < 2):
                        act.wait_ge(msg_mm, off + u - 1)
                    act.copy(mix[:, par], ps_mix[par]).then_inc(mix_done, 1)

                def take_msgs(i, q, first):
                    u = 4 * i + q
                    par = q % 2
                    act.wait_ge(msg_mm, off + u + 1)
                    if not (first and q < 2):
                        for t in range(QT):
                            act.wait_ge(scattered[t], 16 * (off + u - 1))
                    act.copy(msgs[:, par], ps_msg[par]).then_inc(msg_done, 1)

                def stage_to(i, q, first):
                    u = 4 * i + q
                    if h == 0:
                        act.wait_ge(to_found, u + 1)
                    if not first:
                        for t in range(QT):
                            act.wait_ge(scattered[t], 16 * (off + u - 3))
                    act.wait_ge(edges_ready, 1)
                    act.copy(to_ring[:, q, :], to_all[:, bass.ds(u * QT, QT)]).then_inc(to_staged, 1)

                def step(i, q, first, last):
                    take_mix(i, q, first)
                    if not (first and q == 0):
                        take_msgs(i if q > 0 else i - 1, (q - 1) % 4, first)
                    if not (last and q > 0):
                        stage_src(i if q == 0 else i + 1, (q + 3) % 4, first and q == 0)
                    stage_to(i, q, first)

                def rest_store(i, q, tiles, after, first):
                    if q == 3:
                        act.wait_ge(rest_rows, i + 1)
                        act.dma_start(rows_of(table[1], i + 1, tiles), hr[:, 0, 0:tiles, :]).then_inc(rest_stored, 16)

                with act.If(near):
                    for q in range(3):
                        stage_src(0, q, True)
                    if h == 0:
                        over_quads(act, step)
                    else:
                        over_quads_and_table(act, step, rest_store)
                    take_msgs(QUADS // 4 - 1, 3, False)
                with act.Else():
                    act.wait_ge(edges_ready, 1)
                    if h == 1:
                        rest_of_table(act, rest_store)
                act.wait_ge(hop_done, h + 1)

            first_hop(0)

            def t2(i, q, tiles, first):
                c = 2 * i + q
                act.wait_ge(t2_rows, c + 1)
                act.dma_start(rows_of(table[1], c, tiles), hr[:, q, 0:tiles, :]).then_inc(t2_stored, 16)
            t2(0, 0, CT, True)
            first_hop(1)

            def mid(i, q, tiles, first):
                c = 2 * i + q
                if not first:
                    act.wait_ge(ln_stored[q], 16 * i)
                    act.wait_ge(c_turned, c - 1)
                ln_std_and_norm(1, i, q, tiles, nr)
                act.wait_ge(ln_h[1], c + 1)
                act.dma_start(rows_of(table[2], c, tiles), nr[:, q, 0:tiles, :]).then_inc(ln_stored[q], 16)
                act.wait_ge(c_turned, c + 1)
                act.activation(acc_b[:, :, bass.ds(c * CN, tiles * P)], ps_cols[q][:, :, 0:tiles * P], ACT.Copy,
                               scale=eps_sb[:, 1:2]).then_inc(c_cols, 1)
            over_chunks(act, mid)

            def fill(i, q, first, last):
                g = RING * i + q
                if not first:
                    act.wait_ge(mm_done, g - RING + 1)
                act.wait_ge(edges_ready, 1)
                act.copy(idx[:, q, :], src_all[:, bass.ds(g * GT, GT)]).then_inc(idx_ready, 1)

            with act.If(near):
                over_groups(act, fill)
            with act.Else():
                act.wait_ge(edges_ready, 1)
            act.wait_ge(hop_done, 3)

            act.wait_ge(x1_stored, 16 * CHUNKS)

            def z1(i, q, tiles, first):
                n = CN if tiles == CT else TAIL
                c = 2 * i + q
                for m in range(K2):
                    act.wait_ge(z_mm[0], K2 * c + m + 1)
                    act.wait_ge(vectors_in, 16 * 12)
                    act.activation(z[:, m, bass.ds(c * CN, n)], ps[:, K2 * q + m, 0:n], ACT.Identity,
                                   bias=bvec[0][:, m:m + 1]).then_inc(z_evac[0], 1)
            over_chunks(act, z1)

            def bn_sqrt(n):
                act.wait_ge(bn_step[n], 2)
                act.activation(bn[:, 2, 0:M[n]], bn[:, 1, 0:M[n]], ACT.Sqrt).then_inc(bn_std[n], 1)
                act.wait_ge(bn_ready[n], 1)

            def elu_terms(n, zk, k, c, width, K):
                j = K * c + k
                if not (isinstance(j, int) and j < 2):
                    act.wait_ge(a_done[n], j - 1)
                act.wait_ge(bn_ready[n], 1)
                act.activation(ev[:, k % 2, 0:width], zk, ACT.Exp,
                               scale=bn[:, 4, k:k + 1], bias=bn[:, 5, k:k + 1])
                act.activation(yv[:, k % 2, 0:width], zk, ACT.Identity,
                               scale=bn[:, 4, k:k + 1], bias=bn[:, 6, k:k + 1]).then_inc(e_done[n], 1)

            bn_sqrt(0)

            def save_z2(i, q, tiles, first):
                n = CN if tiles == CT else TAIL
                c = 2 * i + q
                for m in range(K3):
                    h, r = divmod(m, K3 // 2)
                    if r == 0 and not (first and q == 0):
                        act.wait_ge(z2_stored[h], 16 * c)
                        act.wait_ge(z_stat[1], K3 * (c - 1) + (h + 1) * (K3 // 2))
                    act.wait_ge(z_mm[1], K3 * c + m + 1)
                    act.activation(z2_out[:, h, r, 0:n], ps[:, m, 0:n], ACT.Identity,
                                   bias=bvec[1][:, m:m + 1]).then_inc(z_evac[1], 1)

            def elu1(i, q, tiles, first):
                n = CN if tiles == CT else TAIL
                c = 2 * i + q
                for k in range(K2):
                    elu_terms(0, z[:, k, bass.ds(c * CN, n)], k, c, n, K2)

            elu1(0, 0, CT, True)

            def z2(i, q, tiles, first):
                if tiles == CT:
                    if q == 0:
                        elu1(i, 1, CT, False)
                    else:
                        elu1(i + 1, 0, CT, False)
                save_z2(i, q, tiles, first)
            z2(0, 0, CT, True)
            z2(0, 1, CT, True)
            with act.Fori(1, FULL // 2 - 1) as i:
                for q in range(2):
                    z2(i, q, CT, False)
            z2(FULL // 2 - 1, 0, CT, False)
            elu1(FULL // 2, 0, 1, False)
            save_z2(FULL // 2 - 1, 1, CT, False)
            save_z2(FULL // 2, 0, 1, False)
            bn_sqrt(1)

            def elu2(i, q, tiles):
                n = CN if tiles == CT else TAIL
                c = 2 * i + q
                act.wait_ge(z2_loaded, 16 * (c + 1))
                for k in range(K3):
                    elu_terms(1, z2_in[:, k, 0:n], k, c, n, K3)

            def save_z3(i, q, tiles):
                n = CN if tiles == CT else TAIL
                c = 2 * i + q
                for m in range(K4):
                    act.wait_ge(z_mm[2], K4 * c + m + 1)
                    act.activation(z[:, m, bass.ds(c * CN, n)], ps[:, K4 * q + m, 0:n], ACT.Identity,
                                   bias=bvec[2][:, m:m + 1]).then_inc(z_evac[2], 1)
            elu2(0, 0, CT)
            elu2(0, 1, CT)
            save_z3(0, 0, CT)
            with act.Fori(1, FULL // 2) as i:
                elu2(i, 0, CT)
                save_z3(i - 1, 1, CT)
                elu2(i, 1, CT)
                save_z3(i, 0, CT)
            elu2(FULL // 2, 0, 1)
            save_z3(FULL // 2 - 1, 1, CT)
            save_z3(FULL // 2, 0, 1)
            bn_sqrt(2)

            def elu3(i, q, tiles, first):
                n = CN if tiles == CT else TAIL
                c = 2 * i + q
                for k in range(K4):
                    elu_terms(2, z[:, k, bass.ds(c * CN, n)], k, c, n, K4)
            def store(i, q, tiles):
                c = 2 * i + q
                act.wait_ge(o_ready, c + 1)
                if tiles == CT:
                    act.dma_start(rows_of(out, c, tiles), o_out[:, q, :, :]).then_inc(o_stored[q], 16)
                else:
                    act.dma_start(out[FULL * CN:N, :], o_out[0:TAIL, q, 0, :]).then_inc(o_stored[q], 16)
            elu3(0, 0, CT, True)
            elu3(0, 1, CT, True)
            store(0, 0, CT)
            with act.Fori(1, FULL // 2) as i:
                elu3(i, 0, CT, False)
                store(i - 1, 1, CT)
                elu3(i, 1, CT, False)
                store(i, 0, CT)
            elu3(FULL // 2, 0, 1, False)
            store(FULL // 2 - 1, 1, CT)
            store(FULL // 2, 0, 1)

        @block.vector
        def _(dve):
            small = [0]

            def chain(ins):
                small[0] += 1
                ins.then_inc(dve_small, 1)
                dve.wait_ge(dve_small, small[0])

            dve.memset(zeros, 0.0).then_inc(zeroed, 1)
            dve.memset(x_tile(FULL, 0)[96:P, :], 0.0).then_inc(ln_pad, 1)
            dve.wait_ge(edges_in, 64)
            dve.tensor_copy(dst_all, dst_i).then_inc(dst_cast, 1)
            chain(dve.tensor_copy(src_all, src_i))
            dve.wait_ge(vectors_in, 16 * 12)
            dve.tensor_tensor(hw[:, 2:3], lg[:, 0:1], lg[:, 1:2], ALU.max).then_inc(prep, 1)
            dve.wait_ge(prep, 1)
            dve.tensor_scalar(hw[:, 3:4], hw[:, 2:3], -1.0, None, ALU.mult).then_inc(prep, 1)
            chain(dve.tensor_scalar(eps_sb[:, 1:2], eps_sb[:, 0:1], 1.0, None, ALU.add))
            chain(dve.tensor_reduce(ends[0:GROUPS, 0:1], dst_gi[0:GROUPS, :], AX_X, ALU.min))
            chain(dve.tensor_reduce(ends[0:GROUPS, 1:2], dst_gi[0:GROUPS, :], AX_X, ALU.max))
            dve.wait_ge(consts_made, 7)
            for a in range(2):
                chain(dve.tensor_scalar(diag[0:GROUPS, a, 0:GROUPS], ident[0:GROUPS, 0:GROUPS], ends[0:GROUPS, a:a + 1],
                                        None, ALU.mult))
            dve.wait_ge(prep_mm, 1)
            chain(dve.tensor_scalar(base_bc[:, :], ps[:, 0, 0:GROUPS], float(ROWS - WIN), None, ALU.min))
            chain(dve.tensor_copy(base_i[:, :], base_bc[0:1, :]))
            chain(dve.tensor_tensor(diag[:, 0, 0:GROUPS], ps[:, 1, 0:GROUPS], base_bc[:, :], ALU.subtract))
            chain(dve.tensor_scalar(made, made, float(CN), None, ALU.max))
            chain(dve.tensor_tensor(diag[:, 1, 0:GROUPS], base_bc[:, :], made, ALU.subtract))
            chain(dve.scalar_tensor_tensor(out=diag[:, 0, 0:GROUPS], in0=diag[:, 1, 0:GROUPS], scalar=float(2 * WIN - 1),
                                           in1=diag[:, 0, 0:GROUPS], op0=ALU.add, op1=ALU.max))
            chain(dve.tensor_reduce(reach[:, 0:1], diag[:, 0, 0:GROUPS], AX_X, ALU.max))
            chain(dve.tensor_copy(reach_i[:, :], reach[0:1, 0:1]))
            dve.wait_ge(dst_masked, 1)
            by_group = [a.rearrange("p (g t) -> p g t", t=GT) for a in (dst_loc, dst_all)]
            chain(dve.tensor_tensor(by_group[0], by_group[1], base_bc[:, :].unsqueeze(2).to_broadcast([P, GROUPS, GT]),
                                    ALU.subtract))
            dve.wait_ge(act_small, 1)
            chain(dve.tensor_tensor(hw[:, 4:5], hw[:, 0:1], hw[:, 1:2], ALU.add))
            chain(dve.reciprocal(hw[:, 5:6], hw[:, 4:5]))
            chain(dve.tensor_scalar(hw[:, 6:8], hw[:, 0:2], hw[:, 5:6], None, ALU.mult))
            dve.memset(done[:, :], 0.0).then_inc(edges_ready, 1)
            near = is_near(dve)

            def ln_coefficients(n, i, q, tiles):
                c = 2 * i + q
                dve.sem_inc(ln_aggr_opened, 1)
                for t in range(tiles):
                    last = dve.bn_stats(lst[:, q, t, :], x_tile(c, t))
                last.then_inc(ln_bn[n], 1)
                dve.wait_ge(ln_bn[n], c + 1)
                dve.sem_inc(ln_aggr_opened, 1)
                for t in range(tiles):
                    last = dve.bn_aggr(lmv[:, q, t, :], lst[:, q, t, :])
                last.then_inc(ln_ag[n], 1)
                dve.wait_ge(ln_ag[n], c + 1)
                dve.tensor_scalar(lve[:, q, 0:tiles], lmv[:, q, 0:tiles, 1], LN_EPS, None, ALU.add).then_inc(ln_var[n], 1)
                dve.wait_ge(ln_std[n], c + 1)
                dve.reciprocal(lrs[:, q, 0:tiles], lsd[:, q, 0:tiles]).then_inc(ln_rstd[n], 1)
                dve.wait_ge(ln_rstd[n], c + 1)
                dve.scalar_tensor_tensor(out=lnm[:, q, 0:tiles], in0=lmv[:, q, 0:tiles, 0], scalar=-1.0,
                                         in1=lrs[:, q, 0:tiles], op0=ALU.mult, op1=ALU.mult).then_inc(ln_coef[n], 1)

            def ln0(i, q, tiles, first):
                c = 2 * i + q
                if not first:
                    dve.wait_ge(ln_h[0], c - 1)
                dve.wait_ge(ln_in[0][q], 16 * (i + 1))
                ln_coefficients(0, i, q, tiles)

            def support(i, q, tiles):
                c = 2 * i + q
                if not (isinstance(i, int) and i == 0):
                    dve.wait_ge(sup_stored[q], 16 * i)
                dve.wait_ge(sup_mm, c + 1)
                dve.tensor_copy(nr[:, q, 0:tiles, :], ps_rows[q][:, 0:tiles, :]).then_inc(sup_rows, 1)

            def ln0_step(i, q, tiles, first):
                ln0(i, q, tiles, first)
                if not (first and q == 0):
                    support(i if q else i - 1, 1 - q, CT)
            over_chunks(dve, ln0_step)
            support(FULL // 2, 0, 1)

            def far_hop(h):
                with dve.Fori(0, TILES) as t:
                    n = h * TILES + t
                    col = bass.ds(t, 1)
                    if h > 0:
                        dve.wait_ge(far_done, 16 * n)
                    if h < 2:
                        added, read, weight = src_all, dst_all, w_all[:, col]
                        dve.tensor_copy(src_ring[:, 0, 0:1], added[:, col]).then_inc(far_step, 1)
                    else:
                        added, read, weight = dst_all, src_all, ones[:, 0:1]
                        dve.tensor_scalar(src_ring[:, 0, 0:1], added[:, col], float(N), None, ALU.min).then_inc(far_step, 1)
                    dve.tensor_scalar(from_any[:, :], read[:, col], float(N - 1), None, ALU.min).then_inc(far_src, 1)
                    dve.wait_ge(far_turned, n + 1)
                    dve.wait_ge(far_step, 4 * n + 1)
                    dve.tensor_scalar(same[:, 0, 0, :], ps_src[0][:, 0, :], src_ring[:, 0, 0:1], weight,
                                      ALU.is_equal, ALU.mult).then_inc(far_same, 1)
                    dve.scalar_tensor_tensor(out=same_src[:, 0, :], in0=ps_src[0][:, 0, :], scalar=src_ring[:, 0, 0:1],
                                             in1=before, op0=ALU.is_equal, op1=ALU.mult,
                                             accum_out=dup[:, 0, 0:1]).then_inc(far_step, 1)
                    dve.wait_ge(far_step, 4 * n + 2)
                    to = dup_to[:, 0, 0:1]
                    dve.tensor_scalar(to, src_ring[:, 0, 0:1], -1.0, spare_row[:, 0:1], ALU.mult, ALU.add).then_inc(far_step, 1)
                    dve.wait_ge(far_step, 4 * n + 3)
                    dve.scalar_tensor_tensor(out=to, in0=dup[:, 0, 0:1], scalar=1.0, in1=to,
                                             op0=ALU.min, op1=ALU.mult).then_inc(far_step, 1)
                    dve.wait_ge(far_step, 4 * n + 4)
                    dve.tensor_tensor(to_ring[:, 0, 0:1], src_ring[:, 0, 0:1], to, ALU.add)
                    dve.wait_ge(far_mm, n + 1)
                    dve.tensor_copy(msgs[:, 0, 0, :], ps_msg[0][:, 0, :]).then_inc(far_msg, 1)
                    dve.wait_ge(far_done, 16 * n + 16)

            def first_hop(h):
                off = h * QUADS

                def step(i, q, first, last):
                    u = 4 * i + q
                    par = q % 2
                    cols = bass.ds(u * QT, QT)
                    dve.wait_ge(src_turned, off + u + 1)
                    if not (first and q < 2):
                        dve.wait_ge(mix_mm, off + u - 1)
                    for t in range(QT):
                        dve.tensor_scalar(same[:, par, t, :], ps_src[par][:, t, :], src_all[:, bass.ds(u * QT + t, 1)],
                                          w_all[:, bass.ds(u * QT + t, 1)], ALU.is_equal, ALU.mult)
                    loc = dst_loc[:, cols].unsqueeze(2).to_broadcast([P, QT, WIN])
                    nodes = iota[:, :].unsqueeze(1).to_broadcast([P, QT, WIN])
                    dve.tensor_tensor(hot[:, par], nodes, loc, ALU.is_equal).then_inc(same_done, 1)
                    if h == 0:
                        for t in range(QT):
                            last_ = dve.scalar_tensor_tensor(out=same_src[:, t, :], in0=ps_src[par][:, t, :],
                                                             scalar=src_all[:, bass.ds(u * QT + t, 1)], in1=before,
                                                             op0=ALU.is_equal, op1=ALU.mult, accum_out=dup[:, q, t:t + 1])
                        last_.then_inc(dup_found, 1)
                        to = dup_to[:, q, :]
                        dve.tensor_scalar(to, src_all[:, cols], -1.0, spare_row[:, 0:1], ALU.mult, ALU.add).then_inc(to_step, 1)
                        dve.wait_ge(dup_found, u + 1)
                        dve.wait_ge(to_step, 2 * u + 1)
                        dve.scalar_tensor_tensor(out=to, in0=dup[:, q, :], scalar=1.0, in1=to,
                                                 op0=ALU.min, op1=ALU.mult).then_inc(to_step, 1)
                        dve.wait_ge(to_step, 2 * u + 2)
                        dve.tensor_tensor(to_all[:, cols], src_all[:, cols], to, ALU.add).then_inc(to_found, 1)

                def rest_rows_of(i, q, tiles, after, first):
                    part = [parts[:, 0, k, 0:tiles, :] for k in range(COPIES)]
                    rows_ = hr[:, 0, 0:tiles, :]
                    if q == 0:
                        dve.wait_ge(rest_in[0], 16 * (i + 1))
                        dve.wait_ge(rest_in[1], 16 * (i + 1))
                        dve.tensor_tensor(part[0], part[0], part[1], ALU.add).then_inc(rest_half, 1)
                    elif q == 1:
                        dve.wait_ge(rest_in[2], 16 * (i + 1))
                        dve.wait_ge(rest_in[3], 16 * (i + 1))
                        dve.tensor_tensor(part[2], part[2], part[3], ALU.add).then_inc(rest_other, 1)
                    elif q == 2:
                        dve.wait_ge(rest_half, i + 1)
                        dve.wait_ge(rest_other, i + 1)
                        if first:
                            dve.wait_ge(t2_stored, 16)
                        else:
                            dve.wait_ge(rest_stored, 16 * i)
                        dve.tensor_tensor(rows_, part[0], part[2], ALU.add).then_inc(rest_rows, 1)
                    else:
                        dve.wait_ge(rest_rows, i + 1)
                        to = base_of(i + 1, tiles)
                        dve.scalar_tensor_tensor(out=to, in0=as_base(hr[:, 0], tiles), scalar=hw[:, 6:7], in1=to,
                                                 op0=ALU.mult, op1=ALU.add).then_inc(rest_kept, 1)

                with dve.If(near):
                    if h == 0:
                        over_quads(dve, step)
                    else:
                        over_quads_and_table(dve, step, rest_rows_of)
                    for t in range(COPIES):
                        dve.wait_ge(scattered[t], 16 * (off + QUADS))
                with dve.Else():
                    if h == 1:
                        rest_of_table(dve, rest_rows_of)
                        dve.wait_ge(rest_kept, CHUNKS - 1)
                    far_hop(h)
                dve.memset(done[:, :], 0.0).then_inc(hop_done, 1)

            def sum_parts(i, q, tiles, loaded, half, other, to, done_):
                c = 2 * i + q
                dve.wait_ge(loaded[q], 16 * COPIES * (i + 1))
                dve.tensor_tensor(parts[:, q, 0, 0:tiles, :], parts[:, q, 0, 0:tiles, :], parts[:, q, 1, 0:tiles, :],
                                  ALU.add).then_inc(half, 1)
                dve.wait_ge(half, c + 1)
                dve.wait_ge(other, c + 1)
                dve.tensor_tensor(to, parts[:, q, 0, 0:tiles, :], parts[:, q, 2, 0:tiles, :], ALU.add).then_inc(done_, 1)

            first_hop(0)

            def t2(i, q, tiles, first):
                c = 2 * i + q
                sum_parts(i, q, tiles, t2_in, t2_half, t2_other, hr[:, q, 0:tiles, :], t2_rows)
                dve.wait_ge(t2_rows, c + 1)
                to = base_of(c, tiles)
                dve.scalar_tensor_tensor(out=to, in0=as_base(hr[:, q], tiles), scalar=hw[:, 6:7], in1=to,
                                         op0=ALU.mult, op1=ALU.add).then_inc(t2_kept, 1)
            dve.tensor_scalar(w_all, w_all, hw[:, 7:8], None, ALU.mult).then_inc(w_scaled, 1)
            dve.wait_ge(w_scaled, 1)
            dve.wait_ge(h_kept, CHUNKS)
            dve.wait_ge(h_turned, CHUNKS)
            t2(0, 0, CT, True)
            dve.wait_ge(t2_kept, 1)
            first_hop(1)

            def mid(i, q, tiles, first):
                c = 2 * i + q
                to = parts[:, q, 0, 0:tiles, :]
                sum_parts(i, q, tiles, ln_in[1], c_half, c_other, to, c_sum)
                dve.wait_ge(c_sum, c + 1)
                x1 = x_rows(c, tiles)
                dve.scalar_tensor_tensor(out=x1, in0=to.rearrange("p t d -> p (t d)"), scalar=0.0, in1=x1,
                                         op0=ALU.max, op1=ALU.add).then_inc(c_x1, 1)
                dve.wait_ge(c_x1, c + 1)
                if not first:
                    dve.wait_ge(ln_h[1], c - 1)
                ln_coefficients(1, i, q, tiles)
            over_chunks(dve, mid)
            dve.wait_ge(c_cols, CHUNKS)

            def build(i, q, first):
                g = RING * i + q
                if not (first and q < 2):
                    dve.wait_ge(mm_done, g - 1)
                loc = dst_loc[:, bass.ds(g * GT, GT)].unsqueeze(2).to_broadcast([P, GT, WIN])
                nodes = iota[:, :].unsqueeze(1).to_broadcast([P, GT, WIN])
                dve.tensor_tensor(onehot[:, q % 2], nodes, loc, ALU.is_equal).then_inc(onehot_ready, 1)

            def add(i, q, first):
                g = RING * i + q
                par = q % 2
                base = dve.value_load(base_i[0:1, bass.ds(g, 1)], min_val=0, max_val=ROWS - WIN)
                dve.wait_ge(mm_done, g + 1)
                if not (first and q == 0):
                    dve.wait_ge(evac_done, g)
                to = acc_b[:, :, bass.ds(base, WIN)]
                dve.tensor_tensor(to, to, ps[:, 2 * par:2 * par + 2, 0:WIN], ALU.add).then_inc(evac_done, 1)

            def gin(i, q, first, last):
                if not (last and q == RING - 1):
                    build(i if q < RING - 1 else i + 1, (q + 1) % RING, first and q < RING - 1)
                add(i, q, first)

            with dve.If(near):
                build(0, 0, True)
                over_groups(dve, gin)
                dve.wait_ge(evac_done, GROUPS)
            with dve.Else():
                far_hop(2)
                with dve.Fori(0, NT) as b:
                    dve.wait_ge(far_cols, b + 1)
                    to = acc_b[:, :, bass.ds(b * P, P)]
                    dve.tensor_tensor(to, to, ps[:, 0:2, 0:P], ALU.add).then_inc(far_added, 1)
                dve.wait_ge(far_added, NT)
            dve.memset(done[:, :], 0.0).then_inc(hop_done, 1)

            def column_stats(n, i, q, tiles, slices, of):
                width = CN if tiles == CT else TAIL
                c = 2 * i + q
                for m in range(slices):
                    dve.wait_ge(z_evac[n], slices * c + m + 1)
                    dve.bn_stats(stats[:, m, bass.ds(c, 1), :].rearrange("p c s -> p (c s)"), of(m, c, width)).then_inc(z_stat[n], 1)

            def bn_vectors(n):
                m = M[n]
                dve.wait_ge(z_stat[n], m * CHUNKS)
                for k in range(m):
                    last = dve.bn_aggr(mv[:, k, :], stats[:, k, :, :].rearrange("p c s -> p (c s)"))
                last.then_inc(bn_step[n], 1)
                dve.wait_ge(bn_step[n], 1)
                dve.tensor_scalar(bn[:, 1, 0:m], mv[:, 0:m, 1], BN_EPS, None, ALU.add).then_inc(bn_step[n], 1)
                dve.wait_ge(bn_std[n], 1)
                chain(dve.reciprocal(bn[:, 3, 0:m], bn[:, 2, 0:m]))
                chain(dve.tensor_tensor(bn[:, 4, 0:m], bn[:, 3, 0:m], gvec[n][:, :], ALU.mult))
                chain(dve.tensor_tensor(bn[:, 7, 0:m], mv[:, 0:m, 0], bn[:, 4, 0:m], ALU.mult))
                chain(dve.tensor_tensor(bn[:, 5, 0:m], tvec[n][:, :], bn[:, 7, 0:m], ALU.subtract))
                chain(dve.tensor_scalar(bn[:, 6, 0:m], bn[:, 5, 0:m], 1.0, None, ALU.add))
                dve.memset(done[:, :], 0.0).then_inc(bn_ready[n], 1)

            def split_sums(i, q, tiles):
                w = CN if tiles == CT else TAIL
                c = 2 * i + q
                for k in range(K1):
                    if not (isinstance(c, int) and c == 0):
                        if k < K1 - 1:
                            dve.wait_ge(sums_used, (K1 - 1) * (c - 1) + k + 1)
                        else:
                            dve.wait_ge(z_mm[0], K2 * c)
                    of = acc_b[:, k, bass.ds(c * CN, w)]
                    dve.tensor_copy(a0[:, k, 0, 0:w], of).then_inc(sums_hi, 1)
                    dve.wait_ge(sums_hi, K1 * c + k + 1)
                    dve.tensor_tensor(a0[:, k, 1, 0:w], of, a0[:, k, 0, 0:w].bitcast(F32), ALU.subtract).then_inc(sums_split, 1)

            def stats1(i, q, tiles):
                column_stats(0, i, q, tiles, K2, lambda m, c, w: z[:, m, bass.ds(c * CN, w)])
            split_sums(0, 0, CT)
            split_sums(0, 1, CT)
            stats1(0, 0, CT)
            with dve.Fori(1, FULL // 2) as i:
                split_sums(i, 0, CT)
                stats1(i - 1, 1, CT)
                split_sums(i, 1, CT)
                stats1(i, 0, CT)
            split_sums(FULL // 2, 0, 1)
            stats1(FULL // 2 - 1, 1, CT)
            stats1(FULL // 2, 0, 1)
            dve.wait_ge(colsum_mm, 1)
            chain(dve.tensor_tensor(b4_bc[:, :], b4_bc[:, :], ps[:, 2, 0:D], ALU.subtract))
            dve.memset(done[:, :], 0.0).then_inc(colsum_done, 1)
            bn_vectors(0)

            def elu(n, k, c, width, to, K):
                dve.wait_ge(e_done[n], K * c + k + 1)
                dve.scalar_tensor_tensor(out=to, in0=ev[:, k % 2, 0:width], scalar=1.0, in1=yv[:, k % 2, 0:width],
                                         op0=ALU.min, op1=ALU.max).then_inc(a_done[n], 1)

            def elu_split(n, k, c, w, to, K):
                dve.wait_ge(e_done[n], K * c + k + 1)
                y = yv[:, k % 2, 0:w]
                dve.scalar_tensor_tensor(out=y, in0=ev[:, k % 2, 0:w], scalar=1.0, in1=y,
                                         op0=ALU.min, op1=ALU.max).then_inc(elu_done[n], 1)
                dve.wait_ge(elu_done[n], K * c + k + 1)
                dve.tensor_copy(to[:, 0, 0:w], y).then_inc(hi_done[n], 1)
                dve.wait_ge(hi_done[n], K * c + k + 1)
                dve.tensor_tensor(to[:, 1, 0:w], y, to[:, 0, 0:w].bitcast(F32), ALU.subtract).then_inc(a_done[n], 1)

            def elu1(i, q, tiles, first):
                w = CN if tiles == CT else TAIL
                if not first:
                    dve.wait_ge(z_mm[1], K3 * (2 * i + q - 1))
                for k in range(K2):
                    elu_split(0, k, 2 * i + q, w, a1[:, q, k], K2)

            def stats2(i, q, tiles):
                column_stats(1, i, q, tiles, K3, lambda m, c, w: z2_out[:, m // (K3 // 2), m % (K3 // 2), 0:w])
            elu1(0, 0, CT, True)
            elu1(0, 1, CT, True)
            stats2(0, 0, CT)
            with dve.Fori(1, FULL // 2) as i:
                elu1(i, 0, CT, False)
                stats2(i - 1, 1, CT)
                elu1(i, 1, CT, False)
                stats2(i, 0, CT)
            elu1(FULL // 2, 0, 1, False)
            stats2(FULL // 2 - 1, 1, CT)
            stats2(FULL // 2, 0, 1)
            bn_vectors(1)

            def elu2(i, q, tiles, first):
                w = CN if tiles == CT else TAIL
                c = 2 * i + q
                for k in range(K3):
                    if not (first and q == 0):
                        if k < K3 - 1:
                            dve.wait_ge(a2_used, (K3 - 1) * (c - 1) + k + 1)
                        else:
                            dve.wait_ge(z_mm[2], K4 * c)
                    elu_split(1, k, c, w, a2[:, k], K3)

            def stats3(i, q, tiles):
                column_stats(2, i, q, tiles, K4, lambda m, c, w: z[:, m, bass.ds(c * CN, w)])
            dve.wait_ge(z_mm[1], K3 * CHUNKS)
            for h in range(2):
                dve.wait_ge(z2_stored[h], 16 * CHUNKS)
            elu2(0, 0, CT, True)
            elu2(0, 1, CT, True)
            stats3(0, 0, CT)
            with dve.Fori(1, FULL // 2) as i:
                elu2(i, 0, CT, False)
                stats3(i - 1, 1, CT)
                elu2(i, 1, CT, False)
                stats3(i, 0, CT)
            elu2(FULL // 2, 0, 1, False)
            stats3(FULL // 2 - 1, 1, CT)
            stats3(FULL // 2, 0, 1)
            bn_vectors(2)
            dve.wait_ge(z_mm[2], K4 * CHUNKS)

            def elu3(i, q, tiles, first):
                w = CN if tiles == CT else TAIL
                if not first:
                    dve.wait_ge(o_mm, 2 * i + q - 1)
                for k in range(K4):
                    elu(2, k, 2 * i + q, w, a3[:, q, k, 0:w], K4)

            def result(i, q, tiles, first):
                c = 2 * i + q
                dve.wait_ge(o_mm, c + 1)
                dve.wait_ge(x1_loaded[q], 16 * (i + 1))
                to = x1_in[:, q, 0:tiles, :]
                bias = b4_bc[:, :].unsqueeze(1).to_broadcast([P, tiles, D])
                dve.tensor_tensor(to, to, bias, ALU.add).then_inc(o_b4, 1)
                dve.wait_ge(o_b4, c + 1)
                if not first:
                    dve.wait_ge(o_stored[q], 16 * i)
                dve.tensor_tensor(o_out[:, q, 0:tiles, :], ps_rows[q][:, 0:tiles, :], to, ALU.add).then_inc(o_ready, 1)
            elu3(0, 0, CT, True)
            elu3(0, 1, CT, True)
            result(0, 0, CT, True)
            elu3(1, 0, CT, False)
            result(0, 1, CT, True)
            elu3(1, 1, CT, False)
            result(1, 0, CT, False)
            with dve.Fori(2, FULL // 2) as i:
                elu3(i, 0, CT, False)
                result(i - 1, 1, CT, False)
                elu3(i, 1, CT, False)
                result(i, 0, CT, False)
            elu3(FULL // 2, 0, 1, False)
            result(FULL // 2 - 1, 1, CT, False)
            result(FULL // 2, 0, 1, False)

        @block.tensor
        def _(pe):
            pe.wait_ge(dve_small, 6)
            for a in range(2):
                mm = pe.matmul(ps[:, a, 0:GROUPS], ones[0:GROUPS, :], diag[0:GROUPS, a, 0:GROUPS], start=True, stop=True)
            mm.then_inc(prep_mm, 1)
            near = is_near(pe)
            pe.wait_ge(weights_in, 48)

            def turn(i, q, tiles, of, ready, free, done_, first):
                c = 2 * i + q
                pe.wait_ge(ready, c + 1)
                if not first:
                    pe.wait_ge(free, c - 1)
                for t in range(tiles):
                    for a in range(DH):
                        mm = pe.transpose(ps_cols[q][:, a, t * P:(t + 1) * P], of[:, q, t, a * P:(a + 1) * P], ident[:, :])
                mm.then_inc(done_, 1)

            def support(i, q, tiles, first):
                c = 2 * i + q
                turn(i, q, tiles, hr, ln_h[0], h_cols, h_turned, first)
                pe.wait_ge(h_cols, c + 1)
                if not first:
                    pe.wait_ge(sup_rows, c - 1)
                for t in range(tiles):
                    for a in range(DH):
                        mm = pe.matmul(ps_rows[q][:, t, :], stage[:, q, a, t * P:(t + 1) * P], wg_sb[:, a, :],
                                       start=(a == 0), stop=(a == DH - 1))
                mm.then_inc(sup_mm, 1)
            over_chunks(pe, support)
            pe.wait_ge(sup_rows, CHUNKS)

            def far_hop(h):
                with pe.Fori(0, TILES) as t:
                    n = h * TILES + t
                    pe.wait_ge(far_step, 4 * n + 1)
                    pe.transpose(ps_src[0][:, 0, :], src_ring[:, 0, 0:1].to_broadcast([P, P]), ident[:, :]).then_inc(far_turned, 1)
                    pe.wait_ge(far_same, n + 1)
                    pe.wait_ge(far_rows, 16 * n + 16)
                    pe.matmul(ps_msg[0][:, 0, :], same[:, 0, 0, :], rows[:, 0, 0, :], start=True, stop=True).then_inc(far_mm, 1)

            def first_hop(h):
                off = h * QUADS

                def turn_src(i, q, first):
                    u = 4 * i + q
                    par = q % 2
                    pe.wait_ge(src_staged, off + u + 1)
                    if not (first and q < 2):
                        pe.wait_ge(same_done, off + u - 1)
                        if h == 0:
                            pe.wait_ge(to_found, u - 1)
                    for t in range(QT):
                        mm = pe.transpose(ps_src[par][:, t, :], src_ring[:, q, t:t + 1].to_broadcast([P, P]), ident[:, :])
                    mm.then_inc(src_turned, 1)

                def mix_edges(i, q, first):
                    u = 4 * i + q
                    par = q % 2
                    pe.wait_ge(same_done, off + u + 1)
                    if not (first and q < 2):
                        pe.wait_ge(mix_done, off + u - 1)
                    for t in range(QT):
                        mm = pe.matmul(ps_mix[par][:, t, :], hot[:, par, t, :], same[:, par, t, :], start=True, stop=True)
                    mm.then_inc(mix_mm, 1)

                def messages(i, q, first):
                    u = 4 * i + q
                    par = q % 2
                    pe.wait_ge(mix_done, off + u + 1)
                    pe.wait_ge(window_in[q // 2], 16 * (off // 4 + i + 1))
                    if not (first and q < 2):
                        pe.wait_ge(msg_done, off + u - 1)
                    for t in range(QT):
                        mm = pe.matmul(ps_msg[par][:, t, :], mix[:, par, t, :], window[:, q // 2, :], start=True, stop=True)
                    mm.then_inc(msg_mm, 1)

                def step(i, q, first, last):
                    mix_edges(i, q, first)
                    if not (first and q == 0):
                        messages(i if q > 0 else i - 1, (q - 1) % 4, first)
                    if not (last and q > 1):
                        turn_src(i if q < 2 else i + 1, (q + 2) % 4, False)

                with pe.If(near):
                    for q in range(2):
                        turn_src(0, q, True)
                    over_quads(pe, step)
                    messages(QUADS // 4 - 1, 3, False)
                with pe.Else():
                    far_hop(h)
                pe.wait_ge(hop_done, h + 1)
            first_hop(0)
            first_hop(1)

            over_chunks(pe, lambda i, q, tiles, first: turn(i, q, tiles, nr, ln_h[1], c_cols, c_turned, first))

            def group(i, q, first, last):
                g = RING * i + q
                par = q % 2
                pe.wait_ge(onehot_ready, g + 1)
                pe.wait_ge(gathered[par], 16 * GT * (2 * i + q // 2 + 1))
                if not (first and q < 2):
                    pe.wait_ge(evac_done, g - 1)
                for t in range(GT):
                    for a in range(DH):
                        mm = pe.matmul(ps[:, 2 * par + a, 0:WIN], rows[:, par, t, a * P:(a + 1) * P],
                                       onehot[:, par, t, :], start=(t == 0), stop=(t == GT - 1))
                mm.then_inc(mm_done, 1)

            with pe.If(near):
                over_groups(pe, group)
            with pe.Else():
                far_hop(2)
                with pe.Fori(0, NT) as b:
                    pe.wait_ge(far_back, 16 * b + 16)
                    for a in range(DH):
                        mm = pe.transpose(ps[:, a, 0:P], rows[:, 0, 1, a * P:(a + 1) * P], ident[:, :])
                    mm.then_inc(far_cols, 1)
            pe.wait_ge(hop_done, 3)

            def product(to, n, w, k, m, a, start, stop):
                hi, lo = [half[:, k, m * P:(m + 1) * P] for half in w]
                pe.matmul(to[:, 0:n], hi, a[:, 0, 0:n], start=start, stop=False)
                pe.matmul(to[:, 0:n], hi, a[:, 1, 0:n], start=False, stop=False)
                return pe.matmul(to[:, 0:n], lo, a[:, 0, 0:n], start=False, stop=stop)

            wide = max(TAIL, 256)

            def z1(i, q, tiles, first):
                n = CN if tiles == CT else wide
                c = 2 * i + q
                for k in range(K1):
                    pe.wait_ge(sums_split, K1 * c + k + 1)
                    for m in range(K2):
                        if k == 0 and not first:
                            pe.wait_ge(z_evac[0], K2 * (c - 2) + m + 1)
                        mm = product(ps[:, K2 * q + m, :], n, w1_split, k, m, a0[:, k], k == 0, k == K1 - 1)
                        if k == K1 - 1:
                            mm.then_inc(z_mm[0], 1)
                    if k < K1 - 1:
                        mm.then_inc(sums_used, 1)
            pe.wait_ge(w_split, K1)
            over_chunks(pe, z1)

            pe.wait_ge(z_evac[0], K2 * CHUNKS)
            for k in range(K4):
                mm = pe.matmul(ps[:, 2, 0:D], ones[:, :], w4_sb[:, k, :], start=(k == 0), stop=(k == K4 - 1))
            mm.then_inc(colsum_mm, 1)
            pe.wait_ge(colsum_done, 1)

            def z2(i, q, tiles, first):
                n = CN if tiles == CT else wide
                c = 2 * i + q
                pe.wait_ge(a_done[0], K2 * (c + 1))
                for m in range(K3):
                    if not (first and q == 0):
                        pe.wait_ge(z_evac[1], K3 * (c - 1) + m + 1)
                    for k in range(K2):
                        mm = product(ps[:, m, :], n, w2_split, k, m, a1[:, q, k], k == 0, k == K2 - 1)
                    mm.then_inc(z_mm[1], 1)
            pe.wait_ge(w_split, K1 + K2)
            over_chunks(pe, z2)
            pe.wait_ge(z_evac[1], K3 * CHUNKS)

            def z3(i, q, tiles, first):
                n = CN if tiles == CT else wide
                c = 2 * i + q
                for k in range(K3):
                    if first and q == 0:
                        pe.wait_ge(w_split, K1 + K2 + k + 1)
                    pe.wait_ge(a_done[1], K3 * c + k + 1)
                    for m in range(K4):
                        if k == 0 and not first:
                            pe.wait_ge(z_evac[2], K4 * (c - 2) + m + 1)
                        mm = product(ps[:, K4 * q + m, :], n, w3_split, k, m, a2[:, k], k == 0, k == K3 - 1)
                        if k == K3 - 1:
                            mm.then_inc(z_mm[2], 1)
                    if k < K3 - 1:
                        mm.then_inc(a2_used, 1)
            over_chunks(pe, z3)
            pe.wait_ge(z_evac[2], K4 * CHUNKS)

            def last(i, q, tiles, first):
                rest = P if tiles == CT else TAIL
                c = 2 * i + q
                pe.wait_ge(a_done[2], K4 * (c + 1))
                if not first:
                    pe.wait_ge(o_ready, c - 1)
                for t in range(tiles):
                    for k in range(K4):
                        mm = pe.matmul(ps_rows[q][0:rest, t, :], a3[:, q, k, t * P:t * P + rest], w4_sb[:, k, :],
                                       start=(k == 0), stop=(k == K4 - 1))
                mm.then_inc(o_mm, 1)
            over_chunks(pe, last)


def kernel(**inputs):
    import numpy as np
    import concourse.bacc as bacc
    from concourse.bass_utils import run_bass_kernel_spmd

    nc = bacc.Bacc("TRN2", target_bir_lowering=False, num_devices=1)
    arrays, args = {}, []

    def give(name, a):
        a = np.ascontiguousarray(a)
        arrays[name] = a
        args.append(nc.dram_tensor(name, a.shape, mybir.dt.from_np(a.dtype), kind="ExternalInput").ap())

    def by_tile(a, mode):
        return np.pad(np.asarray(a), (0, TILES * P - E), mode=mode).reshape(TILES, P).T

    def by_feature(name):
        return np.asarray(inputs[name]).reshape(-1, P).T

    give("x", inputs["x"])
    give("src_t", by_tile(inputs["src"], "edge"))
    give("dst_t", by_tile(inputs["dst"], "edge"))
    give("dst_g", np.pad(np.asarray(inputs["dst"]), (0, TILES * P - E), mode="edge").reshape(GROUPS, GT * P))
    give("w_t", by_tile(inputs["edge_weight"], "constant"))
    give("wg", inputs["L0_gnn_weight"])
    give("logits", np.broadcast_to(np.asarray(inputs["L0_gnn_hop_logits"]), (P, 2)))
    give("eps", np.broadcast_to(np.asarray(inputs["L1_gnn_eps"]), (P, 1)))
    for n in (1, 2, 3):
        give(f"W{n}", inputs[f"L1_gnn_W{n}"])
        give(f"b{n}", by_feature(f"L1_gnn_b{n}"))
        give(f"g{n}", by_feature(f"L1_gnn_g{n}"))
        give(f"be{n}", by_feature(f"L1_gnn_beta{n}"))
    give("W4", inputs["L1_gnn_W4"])
    give("b4", np.broadcast_to(np.asarray(inputs["L1_gnn_b4"]), (P, D)))
    args.append(nc.dram_tensor("out_0_dram", (N, D), F32, kind="ExternalOutput").ap())
    gnn(nc, *args)
    r = run_bass_kernel_spmd(nc, [arrays], core_ids=[0])
    return r.results[0]["out_0_dram"]
```

```python
from contextlib import ExitStack

import concourse.bass as bass
from concourse import mybir

F32 = mybir.dt.float32
F32R = mybir.dt.float32r
I32 = mybir.dt.int32
ALU = mybir.AluOpType
ACT = mybir.ActivationFunctionType
AX_X = mybir.AxisListType.X

P = 128
N = 6250
D = 256
E = 106250
DH = D // P
LN_EPS = 1e-5
BN_EPS = 1e-5

GT = 8
GROUPS = -(-E // (GT * P))
TILES = GROUPS * GT
RING = 4
WIN = P

CT = 4
CN = CT * P
FULL = N // CN
CHUNKS = FULL + 1
TAIL = N - FULL * CN
NT = FULL * CT + 1
ROWS = NT * P
QT = 4
QUADS = TILES // QT
COPIES = QT
ZR = -(-(N + P) // (QUADS // 4))
SPARE = ZR * (QUADS // 4)
FAR = 65536.0

H1, H2, H3 = 512, 1024, 512
K1, K2, K3, K4 = D // P, H1 // P, H2 // P, H3 // P

assert TAIL <= P and FULL % 2 == 0 and GROUPS % RING == 0 and GT == 2 * QT and SPARE >= ROWS
assert GROUPS == 2 * RING * CHUNKS
assert SPARE % (CHUNKS * ZR) == 0 and ZR <= P


def over_chunks(eng, step):
    for q in range(2):
        step(0, q, CT, True)
    with eng.Fori(1, FULL // 2) as i:
        for q in range(2):
            step(i, q, CT, False)
    step(FULL // 2, 0, 1, False)


def over_groups_and_z1(eng, step, extra):
    def eight(j, first, last):
        for h in range(2):
            for q in range(RING):
                step(2 * j + h, q, first and h == 0, last and h == 1)
                extra(j, RING * h + q)
    for j in range(3):
        eight(j, j == 0, False)
    with eng.Fori(3, CHUNKS - 1) as j:
        eight(j, False, False)
    eight(CHUNKS - 1, False, True)


def z1_chunks(eng, chunk):
    chunk(0, CT, True)
    with eng.Fori(1, FULL) as c:
        chunk(c, CT, False)
    chunk(FULL, 1, False)


def over_quads(eng, step):
    for q in range(4):
        step(0, q, True, False)
    with eng.Fori(1, QUADS // 4 - 1) as i:
        for q in range(4):
            step(i, q, False, False)
    for q in range(4):
        step(QUADS // 4 - 1, q, False, True)


def rest_of_table(eng, extra, step=lambda i, q, first, last: None):
    def chunk(i, tiles, after, first):
        if first:
            step(i, 0, first, False)
        for q in range(4):
            if not first:
                step(i, q, first, False)
            elif q < 3:
                step(i, q + 1, first, False)
            extra(i, q, tiles, after, first)
    chunk(0, CT, CT, True)
    with eng.Fori(1, CHUNKS - 3) as i:
        chunk(i, CT, CT, False)
    chunk(CHUNKS - 3, CT, 1, False)
    chunk(CHUNKS - 2, 1, 0, False)


def over_quads_and_table(eng, step, extra, behind=lambda q: None):
    rest_of_table(eng, extra, step)
    with eng.Fori(CHUNKS - 1, QUADS // 4 - 1) as i:
        for q in range(4):
            behind(q)
            step(i, q, False, False)
    for q in range(4):
        step(QUADS // 4 - 1, q, False, True)


def gnn(nc, x, src_t, dst_t, dst_g, w_t, wg, logits, eps, W1, b1, g1, be1, W2, b2, g2, be2,
        W3, b3, g3, be3, W4, b4, out):
    with ExitStack() as ctx:
        def sb(name, shape, dt=F32):
            return ctx.enter_context(nc.sbuf_tensor(name, shape, dt))

        def both(name, n):
            with nc.sbuf_tensor(name, [P, n], F32) as a:
                pass
            return a, sb(name + "_r", [P, n], F32R)

        def sem(name):
            return ctx.enter_context(nc.semaphore(name))

        def dram(name, shape):
            return nc.dram_tensor(name, shape, F32, kind="Internal").ap()

        table = [dram("table_hop1", (ROWS, D)), dram("table_hop2", (ROWS, D)), dram("table_gin", (ROWS, D))]
        copies = [[dram(f"hop{h + 1}_copy{k}", (SPARE, D)) for k in range(COPIES)] for h in range(2)]
        x1_dram = dram("x1_dram", (ROWS, D))
        z2_dram = dram("z2_dram", (CHUNKS * P, K3 * CN))

        big = sb("big", [P, K2 * N])
        sum_b, sum_r = both("sum_b", DH * ROWS)
        edge_buf = sb("edge_buf", [P, 5 * TILES])
        work, work_r = both("work", 8 * CT * D)
        w1_all, w1_r = both("w1", K1 * H1)
        w1_sb = w1_all[:, :].rearrange("p (k m) -> p k m", k=K1)
        w4_sb = w1_all[:, :].rearrange("p (k m) -> p k m", k=K4)
        w1_hi_sb = sb("w1_hi", [P, K1 * H1], F32R)
        iota = sb("iota", [P, WIN])
        ident = sb("ident", [P, P])
        ones = sb("ones", [P, P])

        acc_b = sum_b[:, :].rearrange("p (h n) -> p h n", h=DH)
        z = big[:, :].rearrange("p (m n) -> p m n", m=K2)

        src_all = edge_buf[:, 0:TILES]
        dst_all = edge_buf[:, TILES:2 * TILES]
        dst_loc = edge_buf[:, 2 * TILES:3 * TILES]
        w_all = edge_buf[:, 3 * TILES:4 * TILES]
        to_all = edge_buf[:, 4 * TILES:5 * TILES].bitcast(I32)

        at = [4 * CN]
        rows = work[:, at[0]:at[0] + 2 * GT * D].rearrange("p (s t d) -> p s t d", s=2, t=GT)
        at[0] += 2 * GT * D
        onehot = work[:, at[0]:at[0] + 2 * GT * WIN].rearrange("p (s t w) -> p s t w", s=2, t=GT)
        dst_i = work[:, 0:TILES].bitcast(I32)
        dst_gi = work[:, TILES:TILES + GT * P].bitcast(I32)
        src_i = work[:, TILES + GT * P:2 * TILES + GT * P].bitcast(I32)
        diag = work[:, 3 * TILES:3 * TILES + 2 * P].rearrange("p (a b) -> p a b", a=2)
        made = work[:, 3 * TILES + 2 * P:3 * TILES + 2 * P + GROUPS]
        at = 3 * TILES + 2 * P + GROUPS
        left = work[:, at:at + GROUPS]
        zeros_wide = work[:, 4 * CT * D - SPARE // CHUNKS // ZR * D:4 * CT * D]
        stage = work[:, 8 * CT * D - 2 * DH * CN:8 * CT * D].rearrange("p (s h n) -> p s h n", s=2, h=DH)
        parts = work[:, :].rearrange("p (s k t d) -> p s k t d", s=2, k=COPIES, t=CT)
        assert 3 * TILES + 2 * P + 2 * GROUPS <= 4 * CT * D - SPARE // CHUNKS // ZR * D
        assert 4 * CT * D <= 8 * CT * D - 2 * DH * CN

        at = [0]

        def place(n):
            at[0] += 2 * n
            return big[:, at[0] - 2 * n:at[0]]
        window = place(D).rearrange("p (s d) -> p s d", s=2)
        same = place(QT * P).rearrange("p (s t e) -> p s t e", s=2, t=QT)
        hot = place(QT * P).rearrange("p (s t e) -> p s t e", s=2, t=QT)
        mix = place(QT * P).rearrange("p (s t e) -> p s t e", s=2, t=QT)
        msgs = place(QT * D).rearrange("p (s t d) -> p s t d", s=2, t=QT)
        hr, nr = [place(CT * D).rearrange("p (s t d) -> p s t d", s=2, t=CT) for _ in range(2)]
        wg_sb = place(DH * D // 2).rearrange("p (k m) -> p k m", k=DH)
        zeros = place(D // 2)
        at[0] += NT * D
        x_res = big[:, at[0] - NT * D:at[0]]
        before = big[:, at[0]:at[0] + P]
        same_src = big[:, at[0] + P:at[0] + (1 + QT) * P].rearrange("p (t e) -> p t e", e=P)
        assert at[0] + (1 + QT) * P <= K2 * N

        base_bc = sb("base_bc", [P, GROUPS])
        reach = sb("reach", [P, 2])
        base_i = sb("base_i", [1, GROUPS], I32)
        reach_i = sb("reach_i", [1, 1], I32)
        ends = sb("ends", [P, 2])
        idx = sb("idx", [P, RING, GT], I32)
        to_ring = sb("to_ring", [P, 4, QT], I32)
        src_ring = sb("src_ring", [P, 4, QT])
        dup = sb("dup", [P, 4, QT])
        dup_to = sb("dup_to", [P, 4, QT])
        from_any = sb("from_any", [P, 1], I32)
        spare_row = sb("spare_row", [P, 1])
        lg = sb("lg", [P, 2])
        hw = sb("hw", [P, 8])
        eps_sb = sb("eps_sb", [P, 2])
        done = sb("done", [P, 1])
        lst = sb("lst", [P, 2, CT, 6])
        lmv = sb("lmv", [P, 2, CT, 2])
        lve = sb("lve", [P, 2, CT])
        lsd = sb("lsd", [P, 2, CT])
        lrs = sb("lrs", [P, 2, CT])
        lnm = sb("lnm", [P, 2, CT])

        M = [K2, K3, K4]
        bvec = [sb(f"bvec{n}", [P, M[n]]) for n in range(3)]
        gvec = [sb(f"gvec{n}", [P, M[n]]) for n in range(3)]
        tvec = [sb(f"tvec{n}", [P, M[n]]) for n in range(3)]
        b4_bc = sb("b4_bc", [P, D])
        at = [3 * TILES]
        stats = edge_buf[:, at[0]:at[0] + K3 * CHUNKS * 6].rearrange("p (m c s) -> p m c s", m=K3, c=CHUNKS)
        at[0] += K3 * CHUNKS * 6
        bn = edge_buf[:, at[0]:at[0] + 8 * K3].rearrange("p (a m) -> p a m", a=8)
        mv = edge_buf[:, at[0] + 8 * K3:at[0] + 10 * K3].rearrange("p (m a) -> p m a", a=2)
        w1_hi = w1_hi_sb[:, :]
        assert at[0] + 10 * K3 <= 5 * TILES and 3 * K3 * CN <= DH * ROWS and 4 * CN <= 3 * TILES
        ev = edge_buf[:, 0:2 * CN].rearrange("p (s n) -> p s n", s=2)
        yv = edge_buf[:, 2 * CN:4 * CN].rearrange("p (s n) -> p s n", s=2)

        def split(region, kk):
            return [a.rearrange("p (k m) -> p k m", k=kk) for a in region]
        w1_split = split([w1_hi, w1_r[:, :]], K1)
        w2_raw, w3_raw = [work[:, K2 * H2:2 * K2 * H2].rearrange("p (k m) -> p k m", k=kk) for kk in (K2, K3)]
        w2_split, w3_split = [split([work_r[:, 0:K2 * H2], work_r[:, K2 * H2:2 * K2 * H2]], kk) for kk in (K2, K3)]
        a0 = work_r[:, 0:4 * CN].rearrange("p (k x n) -> p k x n", k=K1, x=2)
        a1 = sum_r[:, 0:4 * K2 * CN].rearrange("p (s k x n) -> p s k x n", s=2, k=K2, x=2)
        z2_out = sum_b[:, 4 * K2 * CN:4 * K2 * CN + K3 * CN].rearrange("p (h m n) -> p h m n", h=2, m=K3 // 2)
        z2_in = sum_b[:, 0:K3 * CN].rearrange("p (k n) -> p k n", k=K3)
        a2 = sum_r[:, K3 * CN:3 * K3 * CN].rearrange("p (k x n) -> p k x n", k=K3, x=2)
        a3 = sum_b[:, 0:2 * K4 * CN].rearrange("p (s k n) -> p s k n", s=2, k=K4)
        x1_in = sum_b[:, 2 * K4 * CN:2 * K4 * CN + 2 * CT * D].rearrange("p (s t d) -> p s t d", s=2, t=CT)
        o_out = sum_b[:, 2 * K4 * CN + 2 * CT * D:2 * K4 * CN + 4 * CT * D].rearrange("p (s t d) -> p s t d", s=2, t=CT)

        ps = ctx.enter_context(nc.psum_tensor("ps", [P, 8, 512], F32))
        ps_rows = [ps[:, 2 * s:2 * s + 2, :].rearrange("p b (t d) -> p (b t) d", d=D) for s in range(2)]
        ps_cols = [ps[:, 4 + 2 * s:6 + 2 * s, :] for s in range(2)]

        ps_src = [ps[:, s, :].rearrange("p (t e) -> p t e", e=P) for s in range(2)]
        ps_mix = [ps[:, 2 + s, :].rearrange("p (t e) -> p t e", e=P) for s in range(2)]
        ps_msg = [ps[:, 4 + 2 * s:6 + 2 * s, :].rearrange("p b (t d) -> p (b t) d", d=D) for s in range(2)]

        edges_in = sem("edges_in")
        vectors_in = sem("vectors_in")
        logits_in = sem("logits_in")
        weights_in = sem("weights_in")
        consts_made = sem("consts_made")
        dst_cast = sem("dst_cast")
        dst_masked = sem("dst_masked")
        prep = sem("prep")
        prep_mm = sem("prep_mm")
        edges_ready = sem("edges_ready")
        act_small = sem("act_small")
        dve_small = sem("dve_small")
        zeroed = sem("zeroed")
        zeros_stored = sem("zeros_stored")
        zeros2_stored = sem("zeros2_stored")
        hop_done = sem("hop_done")
        window_in = [sem("window_in0"), sem("window_in1")]
        src_staged = sem("src_staged")
        src_turned = sem("src_turned")
        dup_found = sem("dup_found")
        to_step = sem("to_step")
        to_found = sem("to_found")
        same_done = sem("same_done")
        mix_mm = sem("mix_mm")
        mix_done = sem("mix_done")
        msg_mm = sem("msg_mm")
        msg_done = sem("msg_done")
        to_staged = sem("to_staged")
        scattered = [sem(f"scattered{k}") for k in range(COPIES)]
        pool_opened = sem("pool_opened")
        far_src = sem("far_src")
        far_turned = sem("far_turned")
        far_rows = sem("far_rows")
        far_step = sem("far_step")
        far_same = sem("far_same")
        far_mm = sem("far_mm")
        far_msg = sem("far_msg")
        far_done = sem("far_done")
        idx_ready = sem("idx_ready")
        gathered = [sem("gathered0"), sem("gathered1")]
        ln_aggr_opened = sem("ln_aggr_opened")
        onehot_ready = sem("onehot_ready")
        mm_done = sem("mm_done")
        evac_done = sem("evac_done")
        far_zeroed = sem("far_zeroed")
        far_back = sem("far_back")
        far_cols = sem("far_cols")
        far_added = sem("far_added")
        ln_in = [[sem(f"ln{n}_in{q}") for q in range(2)] for n in range(2)]
        ln_pad = sem("ln_pad")
        ln_bn = [sem(f"ln{n}_bn") for n in range(2)]
        ln_ag = [sem(f"ln{n}_ag") for n in range(2)]
        ln_var = [sem(f"ln{n}_var") for n in range(2)]
        ln_std = [sem(f"ln{n}_std") for n in range(2)]
        ln_rstd = [sem(f"ln{n}_rstd") for n in range(2)]
        ln_coef = [sem(f"ln{n}_coef") for n in range(2)]
        ln_h = [sem(f"ln{n}_h") for n in range(2)]
        ln_stored = [sem(f"ln1_stored{q}") for q in range(2)]
        h_turned = sem("h_turned")
        h_cols = sem("h_cols")
        sup_mm = sem("sup_mm")
        sup_rows = sem("sup_rows")
        sup_stored = [sem(f"sup_stored{q}") for q in range(2)]
        t2_in = [sem(f"t2_in{q}") for q in range(2)]
        t2_half = sem("t2_half")
        t2_other = sem("t2_other")
        t2_rows = sem("t2_rows")
        t2_stored = sem("t2_stored")
        w_scaled = sem("w_scaled")
        h_kept = sem("h_kept")
        t2_kept = sem("t2_kept")
        rest_in = [sem(f"rest_in{k}") for k in range(COPIES)]
        rest_opened = sem("rest_opened")
        rest_half = sem("rest_half")
        rest_other = sem("rest_other")
        rest_rows = sem("rest_rows")
        rest_kept = sem("rest_kept")
        rest_stored = sem("rest_stored")
        x1_stored = sem("x1_stored")
        c_quarter = sem("c_quarter")
        c_half = sem("c_half")
        c_other = sem("c_other")
        c_sum = sem("c_sum")
        c_x1 = sem("c_x1")
        c_turned = sem("c_turned")
        c_cols = sem("c_cols")
        z_mm = [sem(f"z{n}_mm") for n in range(3)]
        z_evac = [sem(f"z{n}_evac") for n in range(3)]
        z_stat = [sem(f"z{n}_stat") for n in range(3)]
        bn_step = [sem(f"bn{n}_step") for n in range(3)]
        bn_std = [sem(f"bn{n}_std") for n in range(3)]
        bn_ready = [sem(f"bn{n}_ready") for n in range(3)]
        e_done = [sem(f"e{n}_done") for n in range(3)]
        a_done = [sem(f"a{n}_done") for n in range(3)]
        z2_stored = [sem(f"z2_stored_half{h}") for h in range(2)]
        z2_loaded = [sem(f"z2_loaded{h}") for h in range(2)]
        w2_in = sem("w2_in")
        w4_in = sem("w4_in")
        w3_in = [sem(f"w3_in{h}") for h in range(2)]
        w_hi = sem("w_hi")
        w_split = sem("w_split")
        sums_hi = sem("sums_hi")
        sums_split = sem("sums_split")
        sums_used = sem("sums_used")
        a2_used = sem("a2_used")
        elu_done = [sem(f"elu{n}_done") for n in range(2)]
        hi_done = [sem(f"hi{n}_done") for n in range(2)]
        colsum_mm = sem("colsum_mm")
        x1_loaded = [sem(f"x1_loaded{q}") for q in range(2)]
        o_mm = sem("o_mm")
        o_b4 = sem("o_b4")
        o_ready = sem("o_ready")
        o_stored = [sem(f"o_stored{q}") for q in range(2)]

        block = ctx.enter_context(nc.Block())

        def rows_of(t, c, tiles):
            return t[bass.ds(c * CN, tiles * P), :].rearrange("(t p) d -> p t d", p=P)

        def x_rows(c, tiles):
            return x_res[:, bass.ds(c * CT * D, tiles * D)]

        def x_tile(c, t):
            return x_res[:, bass.ds(c * CT * D + t * D, D)]

        def base_of(c, tiles):
            return acc_b[:, :, bass.ds(c * CN, tiles * P)]

        def as_base(buf, tiles):
            return buf[:, 0:tiles, :].rearrange("p t d -> p (t d)").rearrange("p (h n) -> p h n", h=DH)

        def zero_rows(eng, h, i, s):
            for k in range(COPIES):
                eng.dma_start(copies[h][k][bass.ds(i * ZR, ZR), :], zeros[0:ZR, :]).then_inc(s, 16)

        def is_near(eng):
            eng.wait_ge(edges_ready, 1)
            return eng.value_load(reach_i[0:1, 0:1], min_val=0, max_val=N) < WIN

        @block.sync
        def _(sp):
            sp.dma_start(dst_i, dst_t).then_inc(edges_in, 16)
            sp.dma_start(dst_gi[0:GROUPS, :], dst_g).then_inc(edges_in, 16)
            sp.dma_start(src_i, src_t).then_inc(edges_in, 16)
            sp.dma_start(w_all, w_t).then_inc(edges_in, 16)
            sp.dma_start(lg[:, :], logits).then_inc(logits_in, 16)
            sp.dma_start(eps_sb[:, 0:1], eps).then_inc(logits_in, 16)

            def ln0(i, q, tiles, first):
                c = 2 * i + q
                if not first:
                    sp.wait_ge(ln_in[0][q], 16 * i)
                if tiles == CT:
                    to = x_rows(c, tiles).rearrange("p (t d) -> p t d", d=D)
                    sp.dma_start(to, rows_of(x, c, tiles)).then_inc(ln_in[0][q], 16)
                else:
                    sp.wait_ge(ln_pad, 1)
                    sp.dma_start(x_rows(c, 1)[0:TAIL, :], x[FULL * CN:N, :]).then_inc(ln_in[0][q], 16)
                if first and q == 0:
                    sp.dma_start(wg_sb, wg.rearrange("(k p) m -> p k m", p=P)).then_inc(weights_in, 16)
                if first and q == 1:
                    sp.dma_start(w1_sb, W1.rearrange("(k p) m -> p k m", p=P)).then_inc(weights_in, 16)
                    for to, of in ((b4_bc[:, :], b4),
                                   (bvec[0][:, :], b1), (gvec[0][:, :], g1), (tvec[0][:, :], be1),
                                   (bvec[1][:, :], b2), (gvec[1][:, :], g2), (tvec[1][:, :], be2),
                                   (bvec[2][:, :], b3), (gvec[2][:, :], g3), (tvec[2][:, :], be3)):
                        sp.dma_start(to, of).then_inc(vectors_in, 16)
            over_chunks(sp, ln0)
            near = is_near(sp)

            def rest_part(c, k, tiles):
                sp.dma_start(parts[:, 0, k, 0:tiles, :], rows_of(copies[0][k], c, tiles)).then_inc(rest_in[k], 16)

            def rest_load(i, q, tiles, after, first):
                if q == 0:
                    if first:
                        sp.wait_ge(t2_rows, 1)
                        rest_part(1, 1, CT)
                        rest_part(1, 3, CT)
                    else:
                        sp.wait_ge(rest_rows, i)
                        sp.sem_inc(rest_opened, 1)
                    rest_part(i + 1, 0, tiles)
                elif q == 1:
                    rest_part(i + 1, 2, tiles)
                elif after:
                    sp.wait_ge(rest_half if q == 2 else rest_other, i + 1)
                    sp.sem_inc(rest_opened, 1)
                    rest_part(i + 2, 2 * q - 3, after)

            def hop(h, table_ready):
                off = h * QUADS
                for s, n in table_ready:
                    sp.wait_ge(s, n)

                def load(i, q, first, last):
                    if q % 2 == 0:
                        g = 2 * i + q // 2
                        par = q // 2
                        base = sp.value_load(base_i[0:1, bass.ds(g, 1)], min_val=0, max_val=ROWS - WIN)
                        if not first:
                            sp.wait_ge(msg_mm, off + 4 * i + q - 2)
                        sp.dma_start(window[:, par, :], table[h][bass.ds(base, WIN), :]).then_inc(window_in[par], 16)
                    elif h == 0 and q == 1:
                        zero_rows(sp, 1, i, zeros2_stored)

                def table_of_step(i, q, tiles, after, first):
                    if q == 1 and not first:
                        sp.wait_ge(msg_mm, off + 4 * i)
                        sp.sem_inc(rest_opened, 1)
                    rest_load(i, q, tiles, after, first)
                    if q == 3 and not first:
                        sp.wait_ge(rest_stored, 16 * i)
                        sp.sem_inc(rest_opened, 1)

                def whole_table(q):
                    if q == 2:
                        sp.wait_ge(rest_stored, 16 * (CHUNKS - 1))

                with sp.If(near):
                    if h == 0:
                        over_quads(sp, load)
                    else:
                        over_quads_and_table(sp, load, table_of_step, whole_table)
                with sp.Else():
                    if h == 0:
                        with sp.Fori(0, QUADS // 4) as i:
                            zero_rows(sp, 1, i, zeros2_stored)
                    else:
                        rest_of_table(sp, rest_load)
                sp.wait_ge(hop_done, h + 1)

            def load_parts(h, i, q, tiles, s):
                for k in range(COPIES):
                    sp.dma_start(parts[:, q, k, 0:tiles, :], rows_of(copies[h][k], 2 * i + q, tiles)).then_inc(s[q], 16)
            hop(0, [(sup_stored[0], 16 * (FULL // 2 + 1)), (sup_stored[1], 16 * (FULL // 2))])

            def t2(i, q, tiles, first):
                load_parts(0, i, q, tiles, t2_in)
            t2(0, 0, CT, True)
            hop(1, [(t2_stored, 16)])

            def mid_in(i, q, tiles, first):
                if not first:
                    sp.wait_ge(c_x1, 2 * i + q - 1)
                load_parts(1, i, q, tiles, ln_in[1])
            over_chunks(sp, mid_in)
            sp.wait_ge(c_x1, CHUNKS)

            def x1_out(i, q, tiles, paced):
                if paced:
                    sp.wait_ge(mm_done, 2 * i + q + 1)
                    sp.sem_inc(rest_opened, 1)
                sp.dma_start(rows_of(x1_dram, 2 * i + q, tiles),
                             x_rows(2 * i + q, tiles).rearrange("p (t d) -> p t d", d=D)).then_inc(x1_stored, 16)
            with sp.If(near):
                over_chunks(sp, lambda i, q, tiles, first: x1_out(i, q, tiles, True))
            with sp.Else():
                over_chunks(sp, lambda i, q, tiles, first: x1_out(i, q, tiles, False))

            sp.wait_ge(hop_done, 3)
            sp.dma_start(w2_raw, W2.rearrange("(k p) m -> p k m", p=P)).then_inc(w2_in, 16)
            sp.wait_ge(z_mm[0], K2 * CHUNKS)
            sp.dma_start(w4_sb, W4.rearrange("(k p) m -> p k m", p=P)).then_inc(w4_in, 16)

            def z2_save(i, q, tiles, first):
                n = CN if tiles == CT else TAIL
                c = 2 * i + q
                to = z2_dram[bass.ds(c * P, P), :].rearrange("p (h m n) -> p h m n", h=2, m=K3 // 2)
                for h in range(2):
                    sp.wait_ge(z_evac[1], K3 * c + (h + 1) * (K3 // 2))
                    sp.dma_start(to[:, h, :, 0:n], z2_out[:, h, :, 0:n]).then_inc(z2_stored[h], 16)
            over_chunks(sp, z2_save)

            sp.wait_ge(z_mm[1], K3 * CHUNKS)
            for h in range(2):
                sp.wait_ge(z2_stored[h], 16 * CHUNKS)

            def z2_load(i, q, tiles, first):
                n = CN if tiles == CT else TAIL
                of = z2_dram[bass.ds((2 * i + q) * P, P), :].rearrange("p (k n) -> p k n", k=K3)
                for h in range(2):
                    ks = slice(h * (K3 // 2), (h + 1) * (K3 // 2))
                    if not (first and q == 0):
                        sp.wait_ge(e_done[1], K3 * (2 * i + q - 1) + (h + 1) * (K3 // 2))
                    sp.dma_start(z2_in[:, ks, 0:n], of[:, ks, 0:n]).then_inc(z2_loaded[h], 16)
                    if first and q == 0:
                        w3 = W3.rearrange("(k p) m -> p k m", p=P)
                        sp.dma_start(w3_raw[:, ks, :], w3[:, ks, :]).then_inc(w3_in[h], 16)
            over_chunks(sp, z2_load)

            sp.wait_ge(z_mm[2], K4 * CHUNKS)
            sp.wait_ge(x1_stored, 16 * CHUNKS)

            def x1_back(i, q, tiles):
                sp.dma_start(x1_in[:, q, 0:tiles, :], rows_of(x1_dram, 2 * i + q, tiles)).then_inc(x1_loaded[q], 16)

            def result_out(i, q, tiles):
                c = 2 * i + q
                sp.wait_ge(o_ready, c + 1)
                if tiles == CT:
                    sp.dma_start(rows_of(out, c, tiles), o_out[:, q, :, :]).then_inc(o_stored[q], 16)
                else:
                    sp.dma_start(out[FULL * CN:N, :], o_out[0:TAIL, q, 0, :]).then_inc(o_stored[q], 16)
            x1_back(0, 0, CT)
            x1_back(0, 1, CT)
            with sp.Fori(1, FULL // 2) as i:
                for q in range(2):
                    result_out(i - 1, q, CT)
                    x1_back(i, q, CT)
            result_out(FULL // 2 - 1, 0, CT)
            x1_back(FULL // 2, 0, 1)
            result_out(FULL // 2 - 1, 1, CT)
            result_out(FULL // 2, 0, 1)
            sp.wait_ge(o_stored[0], 16 * (FULL // 2 + 1))
            sp.wait_ge(o_stored[1], 16 * (FULL // 2))

        @block.gpsimd
        def _(pool):
            pool.memset(ident[:, :], 0.0).then_inc(consts_made, 1)
            pool.wait_ge(consts_made, 1)
            pool.affine_select(out=ident[:, :], in_=ident[:, :], compare_op=ALU.not_equal, fill=1.0, base=0,
                               pattern=[[-1, P]], channel_multiplier=1).then_inc(consts_made, 1)
            pool.memset(ones[:, :], 1.0).then_inc(consts_made, 1)
            pool.iota(iota[:, :], pattern=[[1, WIN]], base=0, channel_multiplier=0,
                      allow_small_or_imprecise_dtypes=True).then_inc(consts_made, 1)
            pool.iota(made, pattern=[[CN, GROUPS // 2], [0, 2]], base=0, channel_multiplier=0,
                      allow_small_or_imprecise_dtypes=True).then_inc(consts_made, 1)
            pool.iota(left, pattern=[[CN, CHUNKS], [0, 2 * RING]], base=-CN, channel_multiplier=0,
                      allow_small_or_imprecise_dtypes=True).then_inc(consts_made, 1)
            pool.wait_ge(consts_made, 3)
            pool.affine_select(out=before, in_=ones[:, :], compare_op=ALU.is_gt, fill=0.0, base=0,
                               pattern=[[-1, P]], channel_multiplier=1).then_inc(consts_made, 1)
            pool.iota(spare_row[:, :], pattern=[[0, 1]], base=N, channel_multiplier=1,
                      allow_small_or_imprecise_dtypes=True).then_inc(consts_made, 1)
            pool.wait_ge(dst_cast, 1)
            t0 = TILES - GT
            pool.affine_select(out=dst_all[:, t0:TILES], in_=dst_all[:, t0:TILES], compare_op=ALU.is_ge, fill=FAR,
                               base=E - 1 - t0 * P, pattern=[[-P, GT]], channel_multiplier=-1).then_inc(dst_masked, 1)

            def support(i, q, tiles, first):
                c = 2 * i + q
                pool.wait_ge(ln_h[0], c + 1)
                pool.tensor_copy(base_of(c, tiles), as_base(hr[:, q], tiles)).then_inc(h_kept, 1)
                pool.wait_ge(sup_rows, c + 1)
                pool.sem_inc(pool_opened, 1)
                pool.dma_start(rows_of(table[0], c, tiles), nr[:, q, 0:tiles, :]).then_inc(sup_stored[q], 16)
            over_chunks(pool, support)
            near = is_near(pool)

            def far_hop(h, sums):
                with pool.Fori(0, TILES) as t:
                    n = h * TILES + t
                    pool.wait_ge(far_src, n + 1)
                    pool.sem_inc(pool_opened, 1)
                    pool.indirect_dma_start(rows[:, 0, 0, :], None, table[h],
                                            bass.IndirectOffsetOnAxis(from_any[:, 0:1], 0)).then_inc(far_rows, 16)
                    pool.wait_ge(far_msg, n + 1)
                    pool.sem_inc(pool_opened, 1)
                    pool.indirect_dma_start(sums, bass.IndirectOffsetOnAxis(to_ring[:, 0, 0:1], 0),
                                            msgs[:, 0, 0, :], None, compute_op=ALU.add).then_inc(far_done, 16)

            def scatter_hop(h, sums_ready):
                off = h * QUADS
                for s, n in sums_ready:
                    pool.wait_ge(s, n)

                def scatter(i, q, first, last):
                    u = 4 * i + q
                    pool.wait_ge(msg_done, off + u + 1)
                    pool.wait_ge(to_staged, off + u + 1)
                    pool.sem_inc(pool_opened, 1)
                    for t in range(QT):
                        if not (first and q == 0):
                            pool.wait_ge(scattered[t], 16 * (off + u))
                            pool.sem_inc(pool_opened, 1)
                        pool.indirect_dma_start(copies[h][t], bass.IndirectOffsetOnAxis(to_ring[:, q, t:t + 1], 0),
                                                msgs[:, q % 2, t, :], None, compute_op=ALU.add).then_inc(scattered[t], 16)

                with pool.If(near):
                    over_quads(pool, scatter)
                with pool.Else():
                    if h == 1:
                        pool.wait_ge(t2_stored, 16)
                        pool.wait_ge(rest_stored, 16 * (CHUNKS - 1))
                    far_hop(h, copies[h][0])
                pool.wait_ge(hop_done, h + 1)

            def add_parts(i, q, tiles, loaded, done_):
                pool.wait_ge(loaded[q], 16 * COPIES * (i + 1))
                pool.tensor_tensor(parts[:, q, 2, 0:tiles, :], parts[:, q, 2, 0:tiles, :], parts[:, q, 3, 0:tiles, :],
                                   ALU.add).then_inc(done_, 1)

            def add_base(i, q, tiles, first):
                c = 2 * i + q
                add_parts(i, q, tiles, ln_in[1], c_quarter)
                pool.wait_ge(c_quarter, c + 1)
                to = as_base(parts[:, q, 2], tiles)
                pool.tensor_tensor(to, to, base_of(c, tiles), ALU.add).then_inc(c_other, 1)

            scatter_hop(0, [(zeros_stored, 16 * COPIES * CHUNKS), (sup_stored[0], 16 * (FULL // 2 + 1)),
                            (sup_stored[1], 16 * (FULL // 2))])
            add_parts(0, 0, CT, t2_in, t2_other)
            scatter_hop(1, [(zeros2_stored, 16 * COPIES * (QUADS // 4))])
            def split_low(raw, halves, k, n):
                hi, lo = [half[:, k, :] for half in halves]
                pool.wait_ge(w_hi, n + 1)
                pool.tensor_tensor(lo, raw[:, k, :], hi.bitcast(F32), ALU.subtract).then_inc(w_split, 1)

            for k in range(K1):
                split_low(w1_sb, w1_split, k, k)
            over_chunks(pool, add_base)

            def gather_hop(table_ready):
                off = 0
                for s, n in table_ready:
                    pool.wait_ge(s, n)

                def gather(i, q, first, last):
                    par = q % 2
                    pool.wait_ge(idx_ready, off + RING * i + q + 1)
                    if not (first and q < 2):
                        pool.wait_ge(mm_done, off + RING * i + q - 1)
                    pool.sem_inc(pool_opened, 1)
                    for t in range(GT):
                        pool.indirect_dma_start(rows[:, par, t, :], None, table[2],
                                                bass.IndirectOffsetOnAxis(idx[:, q, t:t + 1], 0)).then_inc(gathered[par], 16)

                with pool.If(near):
                    over_groups_and_z1(pool, gather, lambda j, u: None)
                with pool.Else():
                    with pool.Fori(0, QUADS // 4) as i:
                        pool.dma_start(copies[0][0][bass.ds(i * ZR, ZR), :], zeros[0:ZR, :]).then_inc(far_zeroed, 16)
                    pool.wait_ge(far_zeroed, 16 * (QUADS // 4))
                    far_hop(2, copies[0][0])
                    pool.wait_ge(far_done, 16 * 3 * TILES)
                    with pool.Fori(0, NT) as b:
                        pool.dma_start(rows[:, 0, 1, :], copies[0][0][bass.ds(b * P, P), :]).then_inc(far_back, 16)
                        pool.wait_ge(far_added, b + 1)
                pool.wait_ge(hop_done, 3)
            gather_hop([(ln_stored[0], 16 * (FULL // 2 + 1)), (ln_stored[1], 16 * (FULL // 2))])

            for k in range(K2):
                split_low(w2_raw, w2_split, k, K1 + k)
            for k in range(K3):
                split_low(w3_raw, w3_split, k, K1 + K2 + k)

        @block.scalar
        def _(act):
            def zero_sums(c):
                n = SPARE // CHUNKS
                for k in range(COPIES):
                    act.dma_start(copies[0][k][bass.ds(c * n, n), :].rearrange("(p a) d -> p (a d)", p=ZR),
                                  zeros_wide[0:ZR, :]).then_inc(zeros_stored, 16)

            act.wait_ge(zeroed, 2)
            zero_sums(0)
            zero_sums(FULL)

            act.wait_ge(prep, 2)
            act.activation(hw[:, 0:2], lg[:, :], ACT.Exp, bias=hw[:, 3:4]).then_inc(act_small, 1)

            def ln_std_and_norm(n, i, q, tiles, to):
                c = 2 * i + q
                act.wait_ge(ln_var[n], c + 1)
                act.activation(lsd[:, q, 0:tiles], lve[:, q, 0:tiles], ACT.Sqrt).then_inc(ln_std[n], 1)
                act.wait_ge(ln_coef[n], c + 1)
                for t in range(tiles):
                    last = act.activation(to[:, q, t, :], x_tile(c, t), ACT.Relu,
                                          scale=lrs[:, q, t:t + 1], bias=lnm[:, q, t:t + 1])
                last.then_inc(ln_h[n], 1)

            def ln0(i, q, tiles, first):
                c = 2 * i + q
                if tiles == CT and not (first and q == 0):
                    zero_sums(c)
                if not first:
                    act.wait_ge(h_kept, c - 1)
                    act.wait_ge(h_turned, c - 1)
                ln_std_and_norm(0, i, q, tiles, hr)
                if not first:
                    act.wait_ge(sup_mm, c - 1)
                act.wait_ge(h_turned, c + 1)
                act.copy(stage[:, q, :, 0:tiles * P], ps_cols[q][:, :, 0:tiles * P]).then_inc(h_cols, 1)
            over_chunks(act, ln0)
            near = is_near(act)

            def first_hop(h):
                off = h * QUADS

                def stage_src(i, q, first):
                    u = 4 * i + q
                    if not first:
                        act.wait_ge(src_turned, off + u - 3)
                    act.wait_ge(edges_ready, 1)
                    act.copy(src_ring[:, q, :], src_all[:, bass.ds(u * QT, QT)]).then_inc(src_staged, 1)

                def take_mix(i, q, first):
                    u = 4 * i + q
                    par = q % 2
                    act.wait_ge(mix_mm, off + u + 1)
                    if not (first and q < 2):
                        act.wait_ge(msg_mm, off + u - 1)
                    act.copy(mix[:, par], ps_mix[par]).then_inc(mix_done, 1)

                def take_msgs(i, q, first):
                    u = 4 * i + q
                    par = q % 2
                    act.wait_ge(msg_mm, off + u + 1)
                    if not (first and q < 2):
                        for t in range(QT):
                            act.wait_ge(scattered[t], 16 * (off + u - 1))
                    act.copy(msgs[:, par], ps_msg[par]).then_inc(msg_done, 1)

                def stage_to(i, q, first):
                    u = 4 * i + q
                    if h == 0:
                        act.wait_ge(to_found, u + 1)
                    if not first:
                        for t in range(QT):
                            act.wait_ge(scattered[t], 16 * (off + u - 3))
                    act.wait_ge(edges_ready, 1)
                    act.copy(to_ring[:, q, :], to_all[:, bass.ds(u * QT, QT)]).then_inc(to_staged, 1)

                def step(i, q, first, last):
                    take_mix(i, q, first)
                    if not (first and q == 0):
                        take_msgs(i if q > 0 else i - 1, (q - 1) % 4, first)
                    if not (last and q > 0):
                        stage_src(i if q == 0 else i + 1, (q + 3) % 4, first and q == 0)
                    stage_to(i, q, first)

                def rest_store(i, q, tiles, after, first):
                    if q == 3:
                        act.wait_ge(rest_rows, i + 1)
                        act.dma_start(rows_of(table[1], i + 1, tiles), hr[:, 0, 0:tiles, :]).then_inc(rest_stored, 16)

                with act.If(near):
                    for q in range(3):
                        stage_src(0, q, True)
                    if h == 0:
                        over_quads(act, step)
                    else:
                        over_quads_and_table(act, step, rest_store)
                    take_msgs(QUADS // 4 - 1, 3, False)
                with act.Else():
                    act.wait_ge(edges_ready, 1)
                    if h == 1:
                        rest_of_table(act, rest_store)
                act.wait_ge(hop_done, h + 1)

            first_hop(0)

            def t2(i, q, tiles, first):
                c = 2 * i + q
                act.wait_ge(t2_rows, c + 1)
                act.dma_start(rows_of(table[1], c, tiles), hr[:, q, 0:tiles, :]).then_inc(t2_stored, 16)
            t2(0, 0, CT, True)
            first_hop(1)

            def mid(i, q, tiles, first):
                c = 2 * i + q
                if not first:
                    act.wait_ge(ln_stored[q], 16 * i)
                    act.wait_ge(c_turned, c - 1)
                ln_std_and_norm(1, i, q, tiles, nr)
                act.wait_ge(ln_h[1], c + 1)
                act.dma_start(rows_of(table[2], c, tiles), nr[:, q, 0:tiles, :]).then_inc(ln_stored[q], 16)
                act.wait_ge(c_turned, c + 1)
                act.activation(acc_b[:, :, bass.ds(c * CN, tiles * P)], ps_cols[q][:, :, 0:tiles * P], ACT.Copy,
                               scale=eps_sb[:, 1:2]).then_inc(c_cols, 1)
            over_chunks(act, mid)

            def fill(i, q, first, last):
                g = RING * i + q
                if not first:
                    act.wait_ge(mm_done, g - RING + 1)
                act.wait_ge(edges_ready, 1)
                act.copy(idx[:, q, :], src_all[:, bass.ds(g * GT, GT)]).then_inc(idx_ready, 1)

            def take_z1(c, m, tiles):
                n = CN if tiles == CT else TAIL
                act.wait_ge(z_mm[0], K2 * c + m + 1)
                act.activation(z[:, m, bass.ds(c * CN, n)], ps[:, 4 + m, 0:n], ACT.Identity,
                               bias=bvec[0][:, m:m + 1]).then_inc(z_evac[0], 1)

            def z1_space():
                act.wait_ge(vectors_in, 16 * 10)
                act.wait_ge(x1_stored, 16 * CHUNKS)
                for s, n in zip(ln_stored, (FULL // 2 + 1, FULL // 2)):
                    act.wait_ge(s, 16 * n)

            def z1_beside(j, u):
                early = isinstance(j, int) and j < 3
                if early and (j, u) == (2, 2 * RING - 1):
                    z1_space()
                if not early and u < K2:
                    take_z1(j - 3, u, CT)

            def z1_chunk(c, tiles, first):
                for m in range(K2):
                    take_z1(c, m, tiles)

            with act.If(near):
                over_groups_and_z1(act, fill, z1_beside)
                for c, tiles in ((FULL - 2, CT), (FULL - 1, CT), (FULL, 1)):
                    z1_chunk(c, tiles, False)
            with act.Else():
                act.wait_ge(edges_ready, 1)
                z1_space()
                act.wait_ge(hop_done, 3)
                z1_chunks(act, z1_chunk)
            act.wait_ge(hop_done, 3)

            def bn_sqrt(n):
                act.wait_ge(bn_step[n], 2)
                act.activation(bn[:, 2, 0:M[n]], bn[:, 1, 0:M[n]], ACT.Sqrt).then_inc(bn_std[n], 1)
                act.wait_ge(bn_ready[n], 1)

            def elu_terms(n, zk, k, c, width, K):
                j = K * c + k
                if not (isinstance(j, int) and j < 2):
                    act.wait_ge(a_done[n], j - 1)
                act.wait_ge(bn_ready[n], 1)
                act.activation(ev[:, k % 2, 0:width], zk, ACT.Exp,
                               scale=bn[:, 4, k:k + 1], bias=bn[:, 5, k:k + 1])
                act.activation(yv[:, k % 2, 0:width], zk, ACT.Identity,
                               scale=bn[:, 4, k:k + 1], bias=bn[:, 6, k:k + 1]).then_inc(e_done[n], 1)

            bn_sqrt(0)

            def save_z2(i, q, tiles, first):
                n = CN if tiles == CT else TAIL
                c = 2 * i + q
                for m in range(K3):
                    h, r = divmod(m, K3 // 2)
                    if r == 0 and not (first and q == 0):
                        act.wait_ge(z2_stored[h], 16 * c)
                        act.wait_ge(z_stat[1], K3 * (c - 1) + (h + 1) * (K3 // 2))
                    act.wait_ge(z_mm[1], K3 * c + m + 1)
                    act.activation(z2_out[:, h, r, 0:n], ps[:, m, 0:n], ACT.Identity,
                                   bias=bvec[1][:, m:m + 1]).then_inc(z_evac[1], 1)

            def elu1(i, q, tiles, first):
                n = CN if tiles == CT else TAIL
                c = 2 * i + q
                for k in range(K2):
                    elu_terms(0, z[:, k, bass.ds(c * CN, n)], k, c, n, K2)

            elu1(0, 0, CT, True)

            def z2(i, q, tiles, first):
                if tiles == CT:
                    if q == 0:
                        elu1(i, 1, CT, False)
                    else:
                        elu1(i + 1, 0, CT, False)
                save_z2(i, q, tiles, first)
            z2(0, 0, CT, True)
            z2(0, 1, CT, True)
            with act.Fori(1, FULL // 2 - 1) as i:
                for q in range(2):
                    z2(i, q, CT, False)
            z2(FULL // 2 - 1, 0, CT, False)
            elu1(FULL // 2, 0, 1, False)
            save_z2(FULL // 2 - 1, 1, CT, False)
            save_z2(FULL // 2, 0, 1, False)
            bn_sqrt(1)

            def elu2(i, q, tiles):
                n = CN if tiles == CT else TAIL
                c = 2 * i + q
                for k in range(K3):
                    if k % (K3 // 2) == 0:
                        act.wait_ge(z2_loaded[k // (K3 // 2)], 16 * (c + 1))
                    elu_terms(1, z2_in[:, k, 0:n], k, c, n, K3)

            def save_z3(i, q, tiles):
                n = CN if tiles == CT else TAIL
                c = 2 * i + q
                for m in range(K4):
                    act.wait_ge(z_mm[2], K4 * c + m + 1)
                    act.activation(z[:, m, bass.ds(c * CN, n)], ps[:, K4 * q + m, 0:n], ACT.Identity,
                                   bias=bvec[2][:, m:m + 1]).then_inc(z_evac[2], 1)
            elu2(0, 0, CT)
            elu2(0, 1, CT)
            save_z3(0, 0, CT)
            with act.Fori(1, FULL // 2) as i:
                elu2(i, 0, CT)
                save_z3(i - 1, 1, CT)
                elu2(i, 1, CT)
                save_z3(i, 0, CT)
            elu2(FULL // 2, 0, 1)
            save_z3(FULL // 2 - 1, 1, CT)
            save_z3(FULL // 2, 0, 1)
            bn_sqrt(2)

            def elu3(i, q, tiles, first):
                n = CN if tiles == CT else TAIL
                c = 2 * i + q
                for k in range(K4):
                    elu_terms(2, z[:, k, bass.ds(c * CN, n)], k, c, n, K4)
            over_chunks(act, elu3)

        @block.vector
        def _(dve):
            small = [0]

            def chain(ins):
                small[0] += 1
                ins.then_inc(dve_small, 1)
                dve.wait_ge(dve_small, small[0])

            dve.memset(zeros_wide, 0.0).then_inc(zeroed, 1)
            dve.memset(zeros, 0.0).then_inc(zeroed, 1)
            dve.memset(x_tile(FULL, 0)[96:P, :], 0.0).then_inc(ln_pad, 1)
            dve.wait_ge(edges_in, 64)
            dve.tensor_copy(dst_all, dst_i).then_inc(dst_cast, 1)
            chain(dve.tensor_copy(src_all, src_i))
            dve.wait_ge(logits_in, 32)
            dve.tensor_tensor(hw[:, 2:3], lg[:, 0:1], lg[:, 1:2], ALU.max).then_inc(prep, 1)
            dve.wait_ge(prep, 1)
            dve.tensor_scalar(hw[:, 3:4], hw[:, 2:3], -1.0, None, ALU.mult).then_inc(prep, 1)
            chain(dve.tensor_scalar(eps_sb[:, 1:2], eps_sb[:, 0:1], 1.0, None, ALU.add))
            chain(dve.tensor_reduce(ends[0:GROUPS, 0:1], dst_gi[0:GROUPS, :], AX_X, ALU.min))
            chain(dve.tensor_reduce(ends[0:GROUPS, 1:2], dst_gi[0:GROUPS, :], AX_X, ALU.max))
            dve.wait_ge(consts_made, 8)
            for a in range(2):
                chain(dve.tensor_scalar(diag[0:GROUPS, a, 0:GROUPS], ident[0:GROUPS, 0:GROUPS], ends[0:GROUPS, a:a + 1],
                                        None, ALU.mult))
            dve.wait_ge(prep_mm, 1)
            chain(dve.tensor_scalar(base_bc[:, :], ps[:, 0, 0:GROUPS], float(ROWS - WIN), None, ALU.min))
            chain(dve.tensor_copy(base_i[:, :], base_bc[0:1, :]))
            chain(dve.tensor_tensor(diag[:, 0, 0:GROUPS], ps[:, 1, 0:GROUPS], base_bc[:, :], ALU.subtract))
            chain(dve.tensor_scalar(made, made, float(CN), None, ALU.max))
            chain(dve.tensor_tensor(diag[:, 1, 0:GROUPS], base_bc[:, :], made, ALU.subtract))
            chain(dve.scalar_tensor_tensor(out=diag[:, 0, 0:GROUPS], in0=diag[:, 1, 0:GROUPS], scalar=float(2 * WIN - 1),
                                           in1=diag[:, 0, 0:GROUPS], op0=ALU.add, op1=ALU.max))
            chain(dve.tensor_tensor(diag[:, 1, 0:GROUPS], left, base_bc[:, :], ALU.subtract))
            chain(dve.scalar_tensor_tensor(out=diag[:, 0, 0:GROUPS], in0=diag[:, 1, 0:GROUPS], scalar=float(WIN - 1),
                                           in1=diag[:, 0, 0:GROUPS], op0=ALU.add, op1=ALU.max))
            chain(dve.tensor_reduce(reach[:, 0:1], diag[:, 0, 0:GROUPS], AX_X, ALU.max))
            chain(dve.tensor_copy(reach_i[:, :], reach[0:1, 0:1]))
            dve.wait_ge(dst_masked, 1)
            by_group = [a.rearrange("p (g t) -> p g t", t=GT) for a in (dst_loc, dst_all)]
            chain(dve.tensor_tensor(by_group[0], by_group[1], base_bc[:, :].unsqueeze(2).to_broadcast([P, GROUPS, GT]),
                                    ALU.subtract))
            dve.wait_ge(act_small, 1)
            chain(dve.tensor_tensor(hw[:, 4:5], hw[:, 0:1], hw[:, 1:2], ALU.add))
            chain(dve.reciprocal(hw[:, 5:6], hw[:, 4:5]))
            chain(dve.tensor_scalar(hw[:, 6:8], hw[:, 0:2], hw[:, 5:6], None, ALU.mult))
            dve.memset(done[:, :], 0.0).then_inc(edges_ready, 1)
            near = is_near(dve)

            def split_high(raw, halves, k):
                dve.tensor_copy(halves[0][:, k, :], raw[:, k, :]).then_inc(w_hi, 1)

            def ln_coefficients(n, i, q, tiles):
                c = 2 * i + q
                dve.sem_inc(ln_aggr_opened, 1)
                for t in range(tiles):
                    last = dve.bn_stats(lst[:, q, t, :], x_tile(c, t))
                last.then_inc(ln_bn[n], 1)
                dve.wait_ge(ln_bn[n], c + 1)
                dve.sem_inc(ln_aggr_opened, 1)
                for t in range(tiles):
                    last = dve.bn_aggr(lmv[:, q, t, :], lst[:, q, t, :])
                last.then_inc(ln_ag[n], 1)
                dve.wait_ge(ln_ag[n], c + 1)
                dve.tensor_scalar(lve[:, q, 0:tiles], lmv[:, q, 0:tiles, 1], LN_EPS, None, ALU.add).then_inc(ln_var[n], 1)
                dve.wait_ge(ln_std[n], c + 1)
                dve.reciprocal(lrs[:, q, 0:tiles], lsd[:, q, 0:tiles]).then_inc(ln_rstd[n], 1)
                dve.wait_ge(ln_rstd[n], c + 1)
                dve.scalar_tensor_tensor(out=lnm[:, q, 0:tiles], in0=lmv[:, q, 0:tiles, 0], scalar=-1.0,
                                         in1=lrs[:, q, 0:tiles], op0=ALU.mult, op1=ALU.mult).then_inc(ln_coef[n], 1)

            def ln0(i, q, tiles, first):
                c = 2 * i + q
                if not first:
                    dve.wait_ge(ln_h[0], c - 1)
                dve.wait_ge(ln_in[0][q], 16 * (i + 1))
                ln_coefficients(0, i, q, tiles)

            def support(i, q, tiles):
                c = 2 * i + q
                if not (isinstance(i, int) and i == 0):
                    dve.wait_ge(sup_stored[q], 16 * i)
                dve.wait_ge(sup_mm, c + 1)
                dve.tensor_copy(nr[:, q, 0:tiles, :], ps_rows[q][:, 0:tiles, :]).then_inc(sup_rows, 1)

            def ln0_step(i, q, tiles, first):
                ln0(i, q, tiles, first)
                if not (first and q == 0):
                    support(i if q else i - 1, 1 - q, CT)
            over_chunks(dve, ln0_step)
            support(FULL // 2, 0, 1)

            def far_hop(h):
                with dve.Fori(0, TILES) as t:
                    n = h * TILES + t
                    col = bass.ds(t, 1)
                    if h > 0:
                        dve.wait_ge(far_done, 16 * n)
                    if h < 2:
                        added, read, weight = src_all, dst_all, w_all[:, col]
                        dve.tensor_copy(src_ring[:, 0, 0:1], added[:, col]).then_inc(far_step, 1)
                    else:
                        added, read, weight = dst_all, src_all, ones[:, 0:1]
                        dve.tensor_scalar(src_ring[:, 0, 0:1], added[:, col], float(N), None, ALU.min).then_inc(far_step, 1)
                    dve.tensor_scalar(from_any[:, :], read[:, col], float(N - 1), None, ALU.min).then_inc(far_src, 1)
                    dve.wait_ge(far_turned, n + 1)
                    dve.wait_ge(far_step, 4 * n + 1)
                    dve.tensor_scalar(same[:, 0, 0, :], ps_src[0][:, 0, :], src_ring[:, 0, 0:1], weight,
                                      ALU.is_equal, ALU.mult).then_inc(far_same, 1)
                    dve.scalar_tensor_tensor(out=same_src[:, 0, :], in0=ps_src[0][:, 0, :], scalar=src_ring[:, 0, 0:1],
                                             in1=before, op0=ALU.is_equal, op1=ALU.mult,
                                             accum_out=dup[:, 0, 0:1]).then_inc(far_step, 1)
                    dve.wait_ge(far_step, 4 * n + 2)
                    to = dup_to[:, 0, 0:1]
                    dve.tensor_scalar(to, src_ring[:, 0, 0:1], -1.0, spare_row[:, 0:1], ALU.mult, ALU.add).then_inc(far_step, 1)
                    dve.wait_ge(far_step, 4 * n + 3)
                    dve.scalar_tensor_tensor(out=to, in0=dup[:, 0, 0:1], scalar=1.0, in1=to,
                                             op0=ALU.min, op1=ALU.mult).then_inc(far_step, 1)
                    dve.wait_ge(far_step, 4 * n + 4)
                    dve.tensor_tensor(to_ring[:, 0, 0:1], src_ring[:, 0, 0:1], to, ALU.add)
                    dve.wait_ge(far_mm, n + 1)
                    dve.tensor_copy(msgs[:, 0, 0, :], ps_msg[0][:, 0, :]).then_inc(far_msg, 1)
                    dve.wait_ge(far_done, 16 * n + 16)

            def first_hop(h):
                off = h * QUADS

                def step(i, q, first, last):
                    u = 4 * i + q
                    par = q % 2
                    cols = bass.ds(u * QT, QT)
                    dve.wait_ge(src_turned, off + u + 1)
                    if not (first and q < 2):
                        dve.wait_ge(mix_mm, off + u - 1)
                    for t in range(QT):
                        dve.tensor_scalar(same[:, par, t, :], ps_src[par][:, t, :], src_all[:, bass.ds(u * QT + t, 1)],
                                          w_all[:, bass.ds(u * QT + t, 1)], ALU.is_equal, ALU.mult)
                    loc = dst_loc[:, cols].unsqueeze(2).to_broadcast([P, QT, WIN])
                    nodes = iota[:, :].unsqueeze(1).to_broadcast([P, QT, WIN])
                    dve.tensor_tensor(hot[:, par], nodes, loc, ALU.is_equal).then_inc(same_done, 1)
                    if h == 0:
                        for t in range(QT):
                            last_ = dve.scalar_tensor_tensor(out=same_src[:, t, :], in0=ps_src[par][:, t, :],
                                                             scalar=src_all[:, bass.ds(u * QT + t, 1)], in1=before,
                                                             op0=ALU.is_equal, op1=ALU.mult, accum_out=dup[:, q, t:t + 1])
                        last_.then_inc(dup_found, 1)
                        to = dup_to[:, q, :]
                        dve.tensor_scalar(to, src_all[:, cols], -1.0, spare_row[:, 0:1], ALU.mult, ALU.add).then_inc(to_step, 1)
                        dve.wait_ge(dup_found, u + 1)
                        dve.wait_ge(to_step, 2 * u + 1)
                        dve.scalar_tensor_tensor(out=to, in0=dup[:, q, :], scalar=1.0, in1=to,
                                                 op0=ALU.min, op1=ALU.mult).then_inc(to_step, 1)
                        dve.wait_ge(to_step, 2 * u + 2)
                        dve.tensor_tensor(to_all[:, cols], src_all[:, cols], to, ALU.add).then_inc(to_found, 1)

                def rest_rows_of(i, q, tiles, after, first):
                    part = [parts[:, 0, k, 0:tiles, :] for k in range(COPIES)]
                    rows_ = hr[:, 0, 0:tiles, :]
                    if q == 0:
                        dve.wait_ge(rest_in[0], 16 * (i + 1))
                        dve.wait_ge(rest_in[1], 16 * (i + 1))
                        dve.tensor_tensor(part[0], part[0], part[1], ALU.add).then_inc(rest_half, 1)
                    elif q == 1:
                        dve.wait_ge(rest_in[2], 16 * (i + 1))
                        dve.wait_ge(rest_in[3], 16 * (i + 1))
                        dve.tensor_tensor(part[2], part[2], part[3], ALU.add).then_inc(rest_other, 1)
                    elif q == 2:
                        dve.wait_ge(rest_half, i + 1)
                        dve.wait_ge(rest_other, i + 1)
                        if first:
                            dve.wait_ge(t2_stored, 16)
                        else:
                            dve.wait_ge(rest_stored, 16 * i)
                        dve.tensor_tensor(rows_, part[0], part[2], ALU.add).then_inc(rest_rows, 1)
                    else:
                        dve.wait_ge(rest_rows, i + 1)
                        to = base_of(i + 1, tiles)
                        dve.scalar_tensor_tensor(out=to, in0=as_base(hr[:, 0], tiles), scalar=hw[:, 6:7], in1=to,
                                                 op0=ALU.mult, op1=ALU.add).then_inc(rest_kept, 1)

                with dve.If(near):
                    if h == 0:
                        over_quads(dve, step)
                    else:
                        over_quads_and_table(dve, step, rest_rows_of)
                    for t in range(COPIES):
                        dve.wait_ge(scattered[t], 16 * (off + QUADS))
                with dve.Else():
                    if h == 1:
                        rest_of_table(dve, rest_rows_of)
                        dve.wait_ge(rest_kept, CHUNKS - 1)
                    far_hop(h)
                dve.memset(done[:, :], 0.0).then_inc(hop_done, 1)

            def sum_parts(i, q, tiles, loaded, half, other, to, done_):
                c = 2 * i + q
                dve.wait_ge(loaded[q], 16 * COPIES * (i + 1))
                dve.tensor_tensor(parts[:, q, 0, 0:tiles, :], parts[:, q, 0, 0:tiles, :], parts[:, q, 1, 0:tiles, :],
                                  ALU.add).then_inc(half, 1)
                dve.wait_ge(half, c + 1)
                dve.wait_ge(other, c + 1)
                dve.tensor_tensor(to, parts[:, q, 0, 0:tiles, :], parts[:, q, 2, 0:tiles, :], ALU.add).then_inc(done_, 1)

            first_hop(0)

            def t2(i, q, tiles, first):
                c = 2 * i + q
                sum_parts(i, q, tiles, t2_in, t2_half, t2_other, hr[:, q, 0:tiles, :], t2_rows)
                dve.wait_ge(t2_rows, c + 1)
                to = base_of(c, tiles)
                dve.scalar_tensor_tensor(out=to, in0=as_base(hr[:, q], tiles), scalar=hw[:, 6:7], in1=to,
                                         op0=ALU.mult, op1=ALU.add).then_inc(t2_kept, 1)
            dve.tensor_scalar(w_all, w_all, hw[:, 7:8], None, ALU.mult).then_inc(w_scaled, 1)
            dve.wait_ge(w_scaled, 1)
            dve.wait_ge(h_kept, CHUNKS)
            dve.wait_ge(h_turned, CHUNKS)
            t2(0, 0, CT, True)
            dve.wait_ge(t2_kept, 1)
            first_hop(1)
            dve.wait_ge(weights_in, 32)
            for k in range(K1):
                split_high(w1_sb, w1_split, k)

            def mid(i, q, tiles, first):
                c = 2 * i + q
                to = parts[:, q, 0, 0:tiles, :]
                sum_parts(i, q, tiles, ln_in[1], c_half, c_other, to, c_sum)
                dve.wait_ge(c_sum, c + 1)
                x1 = x_rows(c, tiles)
                dve.scalar_tensor_tensor(out=x1, in0=to.rearrange("p t d -> p (t d)"), scalar=0.0, in1=x1,
                                         op0=ALU.max, op1=ALU.add).then_inc(c_x1, 1)
                dve.wait_ge(c_x1, c + 1)
                if not first:
                    dve.wait_ge(ln_h[1], c - 1)
                ln_coefficients(1, i, q, tiles)
            over_chunks(dve, mid)
            dve.wait_ge(c_cols, CHUNKS)

            def build(i, q, first):
                g = RING * i + q
                if not (first and q < 2):
                    dve.wait_ge(mm_done, g - 1)
                loc = dst_loc[:, bass.ds(g * GT, GT)].unsqueeze(2).to_broadcast([P, GT, WIN])
                nodes = iota[:, :].unsqueeze(1).to_broadcast([P, GT, WIN])
                dve.tensor_tensor(onehot[:, q % 2], nodes, loc, ALU.is_equal).then_inc(onehot_ready, 1)

            def add(i, q, first):
                g = RING * i + q
                par = q % 2
                base = dve.value_load(base_i[0:1, bass.ds(g, 1)], min_val=0, max_val=ROWS - WIN)
                dve.wait_ge(mm_done, g + 1)
                if not (first and q == 0):
                    dve.wait_ge(evac_done, g)
                to = acc_b[:, :, bass.ds(base, WIN)]
                dve.tensor_tensor(to, to, ps[:, 2 * par:2 * par + 2, 0:WIN], ALU.add).then_inc(evac_done, 1)

            def gin(i, q, first, last):
                if not (last and q == RING - 1):
                    build(i if q < RING - 1 else i + 1, (q + 1) % RING, first and q < RING - 1)
                add(i, q, first)

            def split_sums(c, k, tiles, first):
                w = CN if tiles == CT else TAIL
                if not first:
                    if k < K1 - 1:
                        dve.wait_ge(sums_used, (K1 - 1) * (c - 1) + k + 1)
                    else:
                        dve.wait_ge(z_mm[0], K2 * c)
                of = acc_b[:, k, bass.ds(c * CN, w)]
                dve.tensor_copy(a0[:, k, 0, 0:w], of).then_inc(sums_hi, 1)
                dve.wait_ge(sums_hi, K1 * c + k + 1)
                dve.tensor_tensor(a0[:, k, 1, 0:w], of, a0[:, k, 0, 0:w].bitcast(F32), ALU.subtract).then_inc(sums_split, 1)

            def z1_stats(c, m, tiles):
                width = CN if tiles == CT else TAIL
                dve.wait_ge(z_evac[0], K2 * c + m + 1)
                to = stats[:, m, bass.ds(c, 1), :].rearrange("p c s -> p (c s)")
                dve.bn_stats(to, z[:, m, bass.ds(c * CN, width)]).then_inc(z_stat[0], 1)

            def z1_beside(j, u):
                early = isinstance(j, int) and j < 2
                first = isinstance(j, int) and j == 2
                if early:
                    if (j, u) == (1, 2 * RING - 1):
                        dve.wait_ge(evac_done, 2 * RING * 2)
                        split_sums(0, 0, CT, True)
                    return
                if u == 2 and K1 > 1:
                    split_sums(j - 2, 1, CT, first)
                if u >= K2 and not first:
                    z1_stats(j - 3, u - K2, CT)
                if u == 2 * RING - 1 and not (isinstance(j, int) and j == CHUNKS - 1):
                    dve.wait_ge(evac_done, 2 * RING * (j + 1))
                    split_sums(j - 1, 0, CT, False)

            with dve.If(near):
                build(0, 0, True)
                over_groups_and_z1(dve, gin, z1_beside)
                dve.wait_ge(evac_done, GROUPS)
                dve.memset(done[:, :], 0.0).then_inc(hop_done, 1)
                for k in range(K1):
                    split_sums(FULL - 1, k, CT, False)
                for m in range(K2):
                    z1_stats(FULL - 2, m, CT)
                for k in range(K1):
                    split_sums(FULL, k, 1, False)
                for c, tiles in ((FULL - 1, CT), (FULL, 1)):
                    for m in range(K2):
                        z1_stats(c, m, tiles)
            with dve.Else():
                far_hop(2)
                with dve.Fori(0, NT) as b:
                    dve.wait_ge(far_cols, b + 1)
                    to = acc_b[:, :, bass.ds(b * P, P)]
                    dve.tensor_tensor(to, to, ps[:, 0:2, 0:P], ALU.add).then_inc(far_added, 1)
                dve.wait_ge(far_added, NT)
                dve.memset(done[:, :], 0.0).then_inc(hop_done, 1)

                def z1_chunk(c, tiles, first):
                    for k in range(K1):
                        split_sums(c, k, tiles, first)
                    for m in range(K2):
                        z1_stats(c, m, tiles)
                z1_chunks(dve, z1_chunk)

            def column_stats(n, i, q, tiles, slices, of):
                width = CN if tiles == CT else TAIL
                c = 2 * i + q
                for m in range(slices):
                    dve.wait_ge(z_evac[n], slices * c + m + 1)
                    to = stats[:, m, bass.ds(c, 1), :].rearrange("p c s -> p (c s)")
                    dve.bn_stats(to, of(m, c, width)).then_inc(z_stat[n], 1)

            dve.wait_ge(vectors_in, 16 * 10)

            def bn_vectors(n):
                m = M[n]
                dve.wait_ge(z_stat[n], m * CHUNKS)
                for k in range(m):
                    last = dve.bn_aggr(mv[:, k, :], stats[:, k, :, :].rearrange("p c s -> p (c s)"))
                last.then_inc(bn_step[n], 1)
                dve.wait_ge(bn_step[n], 1)
                dve.tensor_scalar(bn[:, 1, 0:m], mv[:, 0:m, 1], BN_EPS, None, ALU.add).then_inc(bn_step[n], 1)
                dve.wait_ge(bn_std[n], 1)
                chain(dve.reciprocal(bn[:, 3, 0:m], bn[:, 2, 0:m]))
                chain(dve.tensor_tensor(bn[:, 4, 0:m], bn[:, 3, 0:m], gvec[n][:, :], ALU.mult))
                chain(dve.tensor_tensor(bn[:, 7, 0:m], mv[:, 0:m, 0], bn[:, 4, 0:m], ALU.mult))
                chain(dve.tensor_tensor(bn[:, 5, 0:m], tvec[n][:, :], bn[:, 7, 0:m], ALU.subtract))
                chain(dve.tensor_scalar(bn[:, 6, 0:m], bn[:, 5, 0:m], 1.0, None, ALU.add))
                dve.memset(done[:, :], 0.0).then_inc(bn_ready[n], 1)

            dve.wait_ge(w2_in, 16)
            dve.wait_ge(z_mm[0], K2 * CHUNKS)
            for k in range(K2):
                split_high(w2_raw, w2_split, k)
            bn_vectors(0)

            def elu(n, k, c, width, to, K):
                dve.wait_ge(e_done[n], K * c + k + 1)
                dve.scalar_tensor_tensor(out=to, in0=ev[:, k % 2, 0:width], scalar=1.0, in1=yv[:, k % 2, 0:width],
                                         op0=ALU.min, op1=ALU.max).then_inc(a_done[n], 1)

            def elu_split(n, k, c, w, to, K):
                dve.wait_ge(e_done[n], K * c + k + 1)
                y = yv[:, k % 2, 0:w]
                dve.scalar_tensor_tensor(out=y, in0=ev[:, k % 2, 0:w], scalar=1.0, in1=y,
                                         op0=ALU.min, op1=ALU.max).then_inc(elu_done[n], 1)
                dve.wait_ge(elu_done[n], K * c + k + 1)
                dve.tensor_copy(to[:, 0, 0:w], y).then_inc(hi_done[n], 1)
                dve.wait_ge(hi_done[n], K * c + k + 1)
                dve.tensor_tensor(to[:, 1, 0:w], y, to[:, 0, 0:w].bitcast(F32), ALU.subtract).then_inc(a_done[n], 1)

            def elu1(i, q, tiles, first):
                w = CN if tiles == CT else TAIL
                if not first:
                    dve.wait_ge(z_mm[1], K3 * (2 * i + q - 1))
                for k in range(K2):
                    elu_split(0, k, 2 * i + q, w, a1[:, q, k], K2)

            def stats2(i, q, tiles):
                column_stats(1, i, q, tiles, K3, lambda m, c, w: z2_out[:, m // (K3 // 2), m % (K3 // 2), 0:w])
            elu1(0, 0, CT, True)
            elu1(0, 1, CT, True)
            stats2(0, 0, CT)
            with dve.Fori(1, FULL // 2) as i:
                elu1(i, 0, CT, False)
                stats2(i - 1, 1, CT)
                elu1(i, 1, CT, False)
                stats2(i, 0, CT)
            elu1(FULL // 2, 0, 1, False)
            stats2(FULL // 2 - 1, 1, CT)
            stats2(FULL // 2, 0, 1)
            bn_vectors(1)

            def elu2(i, q, tiles, first):
                w = CN if tiles == CT else TAIL
                c = 2 * i + q
                for k in range(K3):
                    if not (first and q == 0):
                        if k < K3 - 1:
                            dve.wait_ge(a2_used, (K3 - 1) * (c - 1) + k + 1)
                        else:
                            dve.wait_ge(z_mm[2], K4 * c)
                    elu_split(1, k, c, w, a2[:, k], K3)
                    if first and q == 0:
                        dve.wait_ge(w3_in[k // (K3 // 2)], 16)
                        split_high(w3_raw, w3_split, k)

            def stats3(i, q, tiles):
                column_stats(2, i, q, tiles, K4, lambda m, c, w: z[:, m, bass.ds(c * CN, w)])
            dve.wait_ge(z_mm[1], K3 * CHUNKS)
            for h in range(2):
                dve.wait_ge(z2_stored[h], 16 * CHUNKS)
            elu2(0, 0, CT, True)
            elu2(0, 1, CT, True)
            stats3(0, 0, CT)
            with dve.Fori(1, FULL // 2) as i:
                elu2(i, 0, CT, False)
                stats3(i - 1, 1, CT)
                elu2(i, 1, CT, False)
                stats3(i, 0, CT)
            elu2(FULL // 2, 0, 1, False)
            stats3(FULL // 2 - 1, 1, CT)
            stats3(FULL // 2, 0, 1)
            bn_vectors(2)
            dve.wait_ge(z_mm[2], K4 * CHUNKS)

            def elu3(i, q, tiles, first):
                w = CN if tiles == CT else TAIL
                if not first:
                    dve.wait_ge(o_mm, 2 * i + q - 1)
                for k in range(K4):
                    elu(2, k, 2 * i + q, w, a3[:, q, k, 0:w], K4)

            def result(i, q, tiles, first):
                c = 2 * i + q
                dve.wait_ge(o_mm, c + 1)
                dve.wait_ge(x1_loaded[q], 16 * (i + 1))
                to = x1_in[:, q, 0:tiles, :]
                bias = b4_bc[:, :].unsqueeze(1).to_broadcast([P, tiles, D])
                dve.tensor_tensor(to, to, bias, ALU.add).then_inc(o_b4, 1)
                dve.wait_ge(o_b4, c + 1)
                if not first:
                    dve.wait_ge(o_stored[q], 16 * i)
                dve.tensor_tensor(o_out[:, q, 0:tiles, :], ps_rows[q][:, 0:tiles, :], to, ALU.add).then_inc(o_ready, 1)
            elu3(0, 0, CT, True)
            dve.wait_ge(colsum_mm, 1)
            chain(dve.tensor_tensor(b4_bc[:, :], b4_bc[:, :], ps[:, 4, 0:D], ALU.subtract))
            elu3(0, 1, CT, True)
            result(0, 0, CT, True)
            elu3(1, 0, CT, False)
            result(0, 1, CT, True)
            elu3(1, 1, CT, False)
            result(1, 0, CT, False)
            with dve.Fori(2, FULL // 2) as i:
                elu3(i, 0, CT, False)
                result(i - 1, 1, CT, False)
                elu3(i, 1, CT, False)
                result(i, 0, CT, False)
            elu3(FULL // 2, 0, 1, False)
            result(FULL // 2 - 1, 1, CT, False)
            result(FULL // 2, 0, 1, False)

        @block.tensor
        def _(pe):
            pe.wait_ge(dve_small, 6)
            for a in range(2):
                mm = pe.matmul(ps[:, a, 0:GROUPS], ones[0:GROUPS, :], diag[0:GROUPS, a, 0:GROUPS], start=True, stop=True)
            mm.then_inc(prep_mm, 1)
            near = is_near(pe)
            pe.wait_ge(weights_in, 32)

            def turn(i, q, tiles, of, ready, free, done_, first):
                c = 2 * i + q
                pe.wait_ge(ready, c + 1)
                if not first:
                    pe.wait_ge(free, c - 1)
                for t in range(tiles):
                    for a in range(DH):
                        mm = pe.transpose(ps_cols[q][:, a, t * P:(t + 1) * P], of[:, q, t, a * P:(a + 1) * P], ident[:, :])
                mm.then_inc(done_, 1)

            def support(i, q, tiles, first):
                c = 2 * i + q
                turn(i, q, tiles, hr, ln_h[0], h_cols, h_turned, first)
                pe.wait_ge(h_cols, c + 1)
                if not first:
                    pe.wait_ge(sup_rows, c - 1)
                for t in range(tiles):
                    for a in range(DH):
                        mm = pe.matmul(ps_rows[q][:, t, :], stage[:, q, a, t * P:(t + 1) * P], wg_sb[:, a, :],
                                       start=(a == 0), stop=(a == DH - 1))
                mm.then_inc(sup_mm, 1)
            over_chunks(pe, support)
            pe.wait_ge(sup_rows, CHUNKS)

            def far_hop(h):
                with pe.Fori(0, TILES) as t:
                    n = h * TILES + t
                    pe.wait_ge(far_step, 4 * n + 1)
                    pe.transpose(ps_src[0][:, 0, :], src_ring[:, 0, 0:1].to_broadcast([P, P]), ident[:, :]).then_inc(far_turned, 1)
                    pe.wait_ge(far_same, n + 1)
                    pe.wait_ge(far_rows, 16 * n + 16)
                    pe.matmul(ps_msg[0][:, 0, :], same[:, 0, 0, :], rows[:, 0, 0, :], start=True, stop=True).then_inc(far_mm, 1)

            def first_hop(h):
                off = h * QUADS

                def turn_src(i, q, first):
                    u = 4 * i + q
                    par = q % 2
                    pe.wait_ge(src_staged, off + u + 1)
                    if not (first and q < 2):
                        pe.wait_ge(same_done, off + u - 1)
                        if h == 0:
                            pe.wait_ge(to_found, u - 1)
                    for t in range(QT):
                        mm = pe.transpose(ps_src[par][:, t, :], src_ring[:, q, t:t + 1].to_broadcast([P, P]), ident[:, :])
                    mm.then_inc(src_turned, 1)

                def mix_edges(i, q, first):
                    u = 4 * i + q
                    par = q % 2
                    pe.wait_ge(same_done, off + u + 1)
                    if not (first and q < 2):
                        pe.wait_ge(mix_done, off + u - 1)
                    for t in range(QT):
                        mm = pe.matmul(ps_mix[par][:, t, :], hot[:, par, t, :], same[:, par, t, :], start=True, stop=True)
                    mm.then_inc(mix_mm, 1)

                def messages(i, q, first):
                    u = 4 * i + q
                    par = q % 2
                    pe.wait_ge(mix_done, off + u + 1)
                    pe.wait_ge(window_in[q // 2], 16 * (off // 4 + i + 1))
                    if not (first and q < 2):
                        pe.wait_ge(msg_done, off + u - 1)
                    for t in range(QT):
                        mm = pe.matmul(ps_msg[par][:, t, :], mix[:, par, t, :], window[:, q // 2, :], start=True, stop=True)
                    mm.then_inc(msg_mm, 1)

                def step(i, q, first, last):
                    mix_edges(i, q, first)
                    if not (first and q == 0):
                        messages(i if q > 0 else i - 1, (q - 1) % 4, first)
                    if not (last and q > 1):
                        turn_src(i if q < 2 else i + 1, (q + 2) % 4, False)

                with pe.If(near):
                    for q in range(2):
                        turn_src(0, q, True)
                    over_quads(pe, step)
                    messages(QUADS // 4 - 1, 3, False)
                with pe.Else():
                    far_hop(h)
                pe.wait_ge(hop_done, h + 1)
            first_hop(0)
            first_hop(1)

            over_chunks(pe, lambda i, q, tiles, first: turn(i, q, tiles, nr, ln_h[1], c_cols, c_turned, first))

            def product(to, n, w, k, m, a, start, stop):
                hi, lo = [half[:, k, m * P:(m + 1) * P] for half in w]
                pe.matmul(to[:, 0:n], hi, a[:, 0, 0:n], start=start, stop=False)
                pe.matmul(to[:, 0:n], hi, a[:, 1, 0:n], start=False, stop=False)
                return pe.matmul(to[:, 0:n], lo, a[:, 0, 0:n], start=False, stop=stop)

            wide = max(TAIL, 256)

            def z1_part(c, u, tiles, first):
                n = CN if tiles == CT else wide
                k, m = divmod(u, K2)
                if m == 0:
                    pe.wait_ge(sums_split, K1 * c + k + 1)
                if k == 0 and not first:
                    pe.wait_ge(z_evac[0], K2 * (c - 1) + m + 1)
                mm = product(ps[:, 4 + m, :], n, w1_split, k, m, a0[:, k], k == 0, k == K1 - 1)
                if k == K1 - 1:
                    mm.then_inc(z_mm[0], 1)
                elif m == K2 - 1:
                    mm.then_inc(sums_used, 1)

            def z1_chunk(c, tiles, first):
                for u in range(K1 * K2):
                    z1_part(c, u, tiles, first)

            def z1_beside(j, u):
                if not (isinstance(j, int) and j < 2):
                    z1_part(j - 2, u, CT, isinstance(j, int) and j == 2)
            pe.wait_ge(w_split, K1)
            assert K1 * K2 == 2 * RING

            def group(i, q, first, last):
                g = RING * i + q
                par = q % 2
                pe.wait_ge(onehot_ready, g + 1)
                pe.wait_ge(gathered[par], 16 * GT * (2 * i + q // 2 + 1))
                if not (first and q < 2):
                    pe.wait_ge(evac_done, g - 1)
                for t in range(GT):
                    for a in range(DH):
                        mm = pe.matmul(ps[:, 2 * par + a, 0:WIN], rows[:, par, t, a * P:(a + 1) * P],
                                       onehot[:, par, t, :], start=(t == 0), stop=(t == GT - 1))
                mm.then_inc(mm_done, 1)

            with pe.If(near):
                over_groups_and_z1(pe, group, z1_beside)
                z1_chunk(FULL - 1, CT, False)
                z1_chunk(FULL, 1, False)
            with pe.Else():
                far_hop(2)
                with pe.Fori(0, NT) as b:
                    pe.wait_ge(far_back, 16 * b + 16)
                    for a in range(DH):
                        mm = pe.transpose(ps[:, a, 0:P], rows[:, 0, 1, a * P:(a + 1) * P], ident[:, :])
                    mm.then_inc(far_cols, 1)
                pe.wait_ge(hop_done, 3)
                z1_chunks(pe, z1_chunk)
            pe.wait_ge(hop_done, 3)

            pe.wait_ge(z_evac[0], K2 * CHUNKS)

            def z2(i, q, tiles, first):
                n = CN if tiles == CT else wide
                c = 2 * i + q
                if first and q == 0:
                    for k in range(K2):
                        pe.wait_ge(w_split, K1 + k + 1)
                        pe.wait_ge(a_done[0], k + 1)
                        for m in range(K3):
                            mm = product(ps[:, m, :], n, w2_split, k, m, a1[:, q, k], k == 0, k == K2 - 1)
                            if k == K2 - 1:
                                mm.then_inc(z_mm[1], 1)
                    return
                pe.wait_ge(a_done[0], K2 * (c + 1))
                for m in range(K3):
                    if not (first and q == 0):
                        pe.wait_ge(z_evac[1], K3 * (c - 1) + m + 1)
                    for k in range(K2):
                        mm = product(ps[:, m, :], n, w2_split, k, m, a1[:, q, k], k == 0, k == K2 - 1)
                    mm.then_inc(z_mm[1], 1)
            over_chunks(pe, z2)
            pe.wait_ge(z_evac[1], K3 * CHUNKS)

            def z3(i, q, tiles, first):
                n = CN if tiles == CT else wide
                c = 2 * i + q
                for k in range(K3):
                    if first and q == 0:
                        pe.wait_ge(w_split, K1 + K2 + k + 1)
                    pe.wait_ge(a_done[1], K3 * c + k + 1)
                    for m in range(K4):
                        if k == 0 and not first:
                            pe.wait_ge(z_evac[2], K4 * (c - 2) + m + 1)
                        mm = product(ps[:, K4 * q + m, :], n, w3_split, k, m, a2[:, k], k == 0, k == K3 - 1)
                        if k == K3 - 1:
                            mm.then_inc(z_mm[2], 1)
                    if k < K3 - 1:
                        mm.then_inc(a2_used, 1)
            over_chunks(pe, z3)
            pe.wait_ge(z_evac[2], K4 * CHUNKS)

            pe.wait_ge(w4_in, 16)
            for k in range(K4):
                mm = pe.matmul(ps[:, 4, 0:D], ones[:, :], w4_sb[:, k, :], start=(k == 0), stop=(k == K4 - 1))
            mm.then_inc(colsum_mm, 1)

            def last(i, q, tiles, first):
                rest = P if tiles == CT else TAIL
                c = 2 * i + q
                pe.wait_ge(a_done[2], K4 * (c + 1))
                if not first:
                    pe.wait_ge(o_ready, c - 1)
                for t in range(tiles):
                    for k in range(K4):
                        mm = pe.matmul(ps_rows[q][0:rest, t, :], a3[:, q, k, t * P:t * P + rest], w4_sb[:, k, :],
                                       start=(k == 0), stop=(k == K4 - 1))
                mm.then_inc(o_mm, 1)
            over_chunks(pe, last)


def kernel(**inputs):
    import numpy as np
    import concourse.bacc as bacc
    from concourse.bass_utils import run_bass_kernel_spmd

    nc = bacc.Bacc("TRN2", target_bir_lowering=False, num_devices=1)
    arrays, args = {}, []

    def give(name, a):
        a = np.ascontiguousarray(a)
        arrays[name] = a
        args.append(nc.dram_tensor(name, a.shape, mybir.dt.from_np(a.dtype), kind="ExternalInput").ap())

    def by_tile(a, mode):
        return np.pad(np.asarray(a), (0, TILES * P - E), mode=mode).reshape(TILES, P).T

    def by_feature(name):
        return np.asarray(inputs[name]).reshape(-1, P).T

    give("x", inputs["x"])
    give("src_t", by_tile(inputs["src"], "edge"))
    give("dst_t", by_tile(inputs["dst"], "edge"))
    give("dst_g", np.pad(np.asarray(inputs["dst"]), (0, TILES * P - E), mode="edge").reshape(GROUPS, GT * P))
    give("w_t", by_tile(inputs["edge_weight"], "constant"))
    give("wg", inputs["L0_gnn_weight"])
    give("logits", np.broadcast_to(np.asarray(inputs["L0_gnn_hop_logits"]), (P, 2)))
    give("eps", np.broadcast_to(np.asarray(inputs["L1_gnn_eps"]), (P, 1)))
    for n in (1, 2, 3):
        give(f"W{n}", inputs[f"L1_gnn_W{n}"])
        give(f"b{n}", by_feature(f"L1_gnn_b{n}"))
        give(f"g{n}", by_feature(f"L1_gnn_g{n}"))
        give(f"be{n}", by_feature(f"L1_gnn_beta{n}"))
    give("W4", inputs["L1_gnn_W4"])
    give("b4", np.broadcast_to(np.asarray(inputs["L1_gnn_b4"]), (P, D)))
    args.append(nc.dram_tensor("out_0_dram", (N, D), F32, kind="ExternalOutput").ap())
    gnn(nc, *args)
    r = run_bass_kernel_spmd(nc, [arrays], core_ids=[0])
    return r.results[0]["out_0_dram"]
```
